# Optimizing a Trainium2 kernel written in Bass

```python
import numpy as np
import jax
import jax.numpy as jnp

def _softmax(x, axis=-1):
    return jax.nn.softmax(x, axis=axis)

def _gelu(x):
    return jax.nn.gelu(x, approximate=True)

def _silu(x):
    return jax.nn.silu(x)

def _sigmoid(x):
    return jax.nn.sigmoid(x)

def _layernorm(x, axis=-1, eps=1e-05):
    m = jnp.mean(x, axis=axis, keepdims=True)
    v = jnp.var(x, axis=axis, keepdims=True)
    return (x - m) / jnp.sqrt(v + eps)

def _scatter_add(tgt, idx, src, axis=0):
    return tgt.at[idx].add(src)

def _segment_sum(src, seg, n):
    return jax.ops.segment_sum(src, seg, n)
kernel_name = 'mk_gnn_preln_d4_gnn_r8_650626'

def setup_inputs(seed: int=0):
    np.random.seed(seed)
    _w = jnp.asarray

    def _rec_inputs():
        import jax
        import jax.numpy as jnp
        _gk = jax.random.key(seed)
        x = -0.0003713 + 1 * jax.random.normal(jax.random.fold_in(_gk, 1), (12500, 128), jnp.float32)
        _s = jax.random.randint(jax.random.fold_in(_gk, 2), (100000,), 0, 12500, jnp.int32)
        _d = jax.random.randint(jax.random.fold_in(_gk, 3), (100000,), 0, 12500, jnp.int32)
        _loop = jnp.arange(12500, dtype=jnp.int32)
        src = jnp.concatenate([_s, _d, _loop])
        dst = jnp.concatenate([_d, _s, _loop])
        _o = jnp.argsort(dst, stable=True)
        src = src[_o]
        dst = dst[_o]
        edge_attr_4 = -0.000107899 + 1.00008 * jax.random.normal(jax.random.fold_in(_gk, 12), (212500, 4), jnp.float32)
        edge_attr_8 = 0.000398945 + 1.00003 * jax.random.normal(jax.random.fold_in(_gk, 13), (212500, 8), jnp.float32)
        edge_type_3 = jax.random.randint(jax.random.fold_in(_gk, 15), (212500,), 0, 3, jnp.int32)
        edge_weight = jax.random.uniform(jax.random.fold_in(_gk, 16), (212500,), jnp.float32, 0.0, 0.999998)
        node_type_5 = jax.random.randint(jax.random.fold_in(_gk, 17), (12500,), 0, 5, jnp.int32)
        return (x, src, dst, edge_attr_4, edge_attr_8, edge_type_3, edge_weight, node_type_5)
    x, src, dst, edge_attr_4, edge_attr_8, edge_type_3, edge_weight, node_type_5 = _rec_inputs()

    def _L0_gnn_setup():
        import jax, jax.numpy as jnp
        import numpy as np
        N_NODES = 12500
        key = jax.random.key(seed)
        k1, k2, k3, k4, k5 = jax.random.split(key, 5)
        in_dim, out_dim = (128, 128)
        x = jax.random.normal(k1, (N_NODES, in_dim), dtype=jnp.float32)
        edge_index = jax.random.randint(k2, (2, 75000), 0, N_NODES, dtype=jnp.int64)
        s = 1.0 / np.sqrt(in_dim)
        W_rel = jax.random.uniform(k3, (out_dim, in_dim), jnp.float32, -s, s)
        W_root = jax.random.uniform(k4, (out_dim, in_dim), jnp.float32, -s, s)
        b_rel = jax.random.uniform(k5, (out_dim,), jnp.float32, -s, s)
        return {'x': x, 'edge_index': edge_index, 'W_rel': W_rel, 'W_root': W_root, 'b_rel': b_rel}
    _L0_gnn_all = _L0_gnn_setup()
    _L0_gnn_in = {k: v for k, v in _L0_gnn_all.items() if k in ('W_rel', 'W_root', 'b_rel')}
    del _L0_gnn_all

    def _L1_gnn_setup():
        import jax, jax.numpy as jnp
        import numpy as np
        C = 32
        N_NODES = 6250
        N_EDGES = 100000
        R_DIM = 8
        R_HID = 8
        N_SPECIES = 5
        AVG_NEIGH = 16.0
        N_PATHS = 4
        key = jax.random.key(seed)
        ks = jax.random.split(key, 16)
        inp = {'node_features': jax.random.normal(ks[0], (N_NODES, 4 * C), jnp.float32), 'edge_features': jax.random.normal(ks[1], (N_EDGES, 4), jnp.float32), 'radial_embedding': jax.random.normal(ks[2], (N_EDGES, R_DIM), jnp.float32), 'senders': jax.random.randint(ks[3], (N_EDGES,), 0, N_NODES), 'receivers': jax.random.randint(ks[4], (N_EDGES,), 0, N_NODES), 'node_species': jax.random.randint(ks[5], (N_NODES,), 0, N_SPECIES), 'W_up_s': jax.random.normal(ks[6], (C, C), jnp.float32), 'W_up_v': jax.random.normal(ks[7], (C, C), jnp.float32), 'W_r1': jax.random.normal(ks[8], (R_DIM, R_HID), jnp.float32), 'W_r2': jax.random.normal(ks[9], (R_HID, N_PATHS * C), jnp.float32), 'W_down_s': jax.random.normal(ks[10], (2 * C, 2 * C), jnp.float32), 'W_down_v': jax.random.normal(ks[11], (2 * C, C), jnp.float32), 'W_skip_s': jax.random.normal(ks[12], (N_SPECIES, C, 2 * C), jnp.float32), 'W_skip_v': jax.random.normal(ks[13], (N_SPECIES, C, C), jnp.float32)}
        return inp
    _L1_gnn_all = _L1_gnn_setup()
    _L1_gnn_in = {k: v for k, v in _L1_gnn_all.items() if k in ('W_up_s', 'W_up_v', 'W_r1', 'W_r2', 'W_down_s', 'W_down_v', 'W_skip_s', 'W_skip_v')}
    del _L1_gnn_all

    def _L2_gnn_setup():
        import jax, jax.numpy as jnp
        import numpy as np
        N, E, H = (6250, 100000, 128)
        LN_EPS = 1e-05

        def layer_norm(x, gamma, beta):
            mu = jnp.mean(x, axis=-1, keepdims=True)
            var = jnp.mean((x - mu) ** 2, axis=-1, keepdims=True)
            return (x - mu) * jax.lax.rsqrt(var + LN_EPS) * gamma + beta
        key = jax.random.key(seed)
        ks = jax.random.split(key, 8)
        sc = 1.0 / np.sqrt(2 * H)
        return {'x': jax.random.normal(ks[0], (N, H), dtype=jnp.float32), 'edge_index': jax.random.randint(ks[1], (2, E), 0, N, dtype=jnp.int64), 'edge_weights': jax.random.uniform(ks[2], (E,), dtype=jnp.float32), 'msg_w': jax.random.normal(ks[3], (2 * H, H), dtype=jnp.float32) * sc, 'msg_b': jnp.zeros((H,), jnp.float32), 'msg_g': jnp.ones((H,), jnp.float32), 'msg_beta': jnp.zeros((H,), jnp.float32), 'upd_w': jax.random.normal(ks[4], (2 * H, H), dtype=jnp.float32) * sc, 'upd_b': jnp.zeros((H,), jnp.float32), 'upd_g': jnp.ones((H,), jnp.float32), 'upd_beta': jnp.zeros((H,), jnp.float32), 'gate_w': jax.random.normal(ks[5], (H, 1), dtype=jnp.float32) / np.sqrt(H), 'gate_b': jnp.zeros((1,), jnp.float32)}
    _L2_gnn_all = _L2_gnn_setup()
    _L2_gnn_in = {k: v for k, v in _L2_gnn_all.items() if k in ('msg_w', 'msg_b', 'msg_g', 'msg_beta', 'upd_w', 'upd_b', 'upd_g', 'upd_beta', 'gate_w', 'gate_b')}
    del _L2_gnn_all

    def _L3_gnn_setup():
        import jax, jax.numpy as jnp
        import numpy as np
        N_NODES = 6250
        N_EDGES = 75000
        D_IN = 128
        DIM = 128
        N_REL = 3
        N_LAYERS = 2
        key = jax.random.key(seed)
        ks = jax.random.split(key, 10)
        s = 1.0 / np.sqrt(DIM)
        x = jax.random.normal(ks[0], (N_NODES, D_IN), dtype=jnp.float32)
        edge_index = jax.random.randint(ks[1], (2, N_EDGES), 0, N_NODES)
        edge_type = jax.random.randint(ks[2], (N_EDGES,), 0, N_REL)
        edge_weight = jax.random.uniform(ks[3], (N_EDGES,), dtype=jnp.float32)
        w_rel = jax.random.normal(ks[4], (N_LAYERS, N_REL, DIM, DIM), dtype=jnp.float32) * s
        w_root = jax.random.normal(ks[5], (N_LAYERS, DIM, DIM), dtype=jnp.float32) * s
        b_conv = jnp.zeros((N_LAYERS, DIM), dtype=jnp.float32)
        w_skip = jax.random.normal(ks[6], (N_LAYERS, D_IN, DIM), dtype=jnp.float32) * s
        b_skip = jnp.zeros((N_LAYERS, DIM), dtype=jnp.float32)
        return {'x': x, 'edge_index': edge_index, 'edge_type': edge_type, 'edge_weight': edge_weight, 'w_rel': w_rel, 'w_root': w_root, 'b_conv': b_conv, 'w_skip': w_skip, 'b_skip': b_skip}
    _L3_gnn_all = _L3_gnn_setup()
    _L3_gnn_in = {k: v for k, v in _L3_gnn_all.items() if k in ('w_rel', 'w_root', 'b_conv', 'w_skip', 'b_skip')}
    del _L3_gnn_all
    return {'x': x, 'src': src, 'dst': dst, 'edge_attr_4': edge_attr_4, 'edge_attr_8': edge_attr_8, 'edge_type_3': edge_type_3, 'edge_weight': edge_weight, 'node_type_5': node_type_5, 'L0_gnn_W_rel': _L0_gnn_in['W_rel'], 'L0_gnn_W_root': _L0_gnn_in['W_root'], 'L0_gnn_b_rel': _L0_gnn_in['b_rel'], 'L1_gnn_W_up_s': _L1_gnn_in['W_up_s'], 'L1_gnn_W_up_v': _L1_gnn_in['W_up_v'], 'L1_gnn_W_r1': _L1_gnn_in['W_r1'], 'L1_gnn_W_r2': _L1_gnn_in['W_r2'], 'L1_gnn_W_down_s': _L1_gnn_in['W_down_s'], 'L1_gnn_W_down_v': _L1_gnn_in['W_down_v'], 'L1_gnn_W_skip_s': _L1_gnn_in['W_skip_s'], 'L1_gnn_W_skip_v': _L1_gnn_in['W_skip_v'], 'L2_gnn_msg_w': _L2_gnn_in['msg_w'], 'L2_gnn_msg_b': _L2_gnn_in['msg_b'], 'L2_gnn_msg_g': _L2_gnn_in['msg_g'], 'L2_gnn_msg_beta': _L2_gnn_in['msg_beta'], 'L2_gnn_upd_w': _L2_gnn_in['upd_w'], 'L2_gnn_upd_b': _L2_gnn_in['upd_b'], 'L2_gnn_upd_g': _L2_gnn_in['upd_g'], 'L2_gnn_upd_beta': _L2_gnn_in['upd_beta'], 'L2_gnn_gate_w': _L2_gnn_in['gate_w'], 'L2_gnn_gate_b': _L2_gnn_in['gate_b'], 'L3_gnn_w_rel': _L3_gnn_in['w_rel'], 'L3_gnn_w_root': _L3_gnn_in['w_root'], 'L3_gnn_b_conv': _L3_gnn_in['b_conv'], 'L3_gnn_w_skip': _L3_gnn_in['w_skip'], 'L3_gnn_b_skip': _L3_gnn_in['b_skip']}

def reference(x, src, dst, edge_attr_4, edge_attr_8, edge_type_3, edge_weight, node_type_5, L0_gnn_W_rel, L0_gnn_W_root, L0_gnn_b_rel, L1_gnn_W_up_s, L1_gnn_W_up_v, L1_gnn_W_r1, L1_gnn_W_r2, L1_gnn_W_down_s, L1_gnn_W_down_v, L1_gnn_W_skip_s, L1_gnn_W_skip_v, L2_gnn_msg_w, L2_gnn_msg_b, L2_gnn_msg_g, L2_gnn_msg_beta, L2_gnn_upd_w, L2_gnn_upd_b, L2_gnn_upd_g, L2_gnn_upd_beta, L2_gnn_gate_w, L2_gnn_gate_b, L3_gnn_w_rel, L3_gnn_w_root, L3_gnn_b_conv, L3_gnn_w_skip, L3_gnn_b_skip):
    import jax
    import jax.numpy as jnp

    def _L0_gnn_ref(x, edge_index, W_rel, W_root, b_rel):
        import jax, jax.numpy as jnp
        import numpy as np
        N_NODES = 12500
        src, dst = (edge_index[0], edge_index[1])
        agg = jax.ops.segment_sum(x[src], dst, num_segments=N_NODES)
        out = agg @ W_rel.T + b_rel + x @ W_root.T
        return out

    def _L1_gnn_ref(node_features, edge_features, radial_embedding, senders, receivers, node_species, W_up_s, W_up_v, W_r1, W_r2, W_down_s, W_down_v, W_skip_s, W_skip_v):
        import jax, jax.numpy as jnp
        import numpy as np
        C = 32
        N_NODES = 6250
        N_EDGES = 100000
        R_DIM = 8
        R_HID = 8
        N_SPECIES = 5
        AVG_NEIGH = 16.0
        N_PATHS = 4
        N = node_features.shape[0]
        inv_sqrt_C = 1.0 / np.sqrt(C)
        s = node_features[:, :C]
        v = node_features[:, C:].reshape(N, C, 3)
        s_up = s @ W_up_s * inv_sqrt_C
        v_up = jnp.einsum('ncx,cd->ndx', v, W_up_v) * inv_sqrt_C
        h = jax.nn.silu(radial_embedding @ W_r1 * (1.0 / np.sqrt(R_DIM)))
        w = (h @ W_r2 * (1.0 / np.sqrt(R_HID))).reshape(-1, N_PATHS, C)
        sh0 = edge_features[:, 0]
        sh1 = edge_features[:, 1:4]
        se = s_up[senders]
        ve = v_up[senders]
        m0 = jnp.concatenate([w[:, 0] * se * sh0[:, None], w[:, 3] * jnp.einsum('ecx,ex->ec', ve, sh1) * (1.0 / np.sqrt(3.0))], axis=1)
        m1 = jnp.concatenate([w[:, 1, :, None] * se[:, :, None] * sh1[:, None, :], w[:, 2, :, None] * ve * sh0[:, None, None]], axis=1)
        inv_sqrt_deg = 1.0 / np.sqrt(AVG_NEIGH)
        agg0 = jax.ops.segment_sum(m0, receivers, num_segments=N) * inv_sqrt_deg
        agg1 = jax.ops.segment_sum(m1, receivers, num_segments=N) * inv_sqrt_deg
        inv_sqrt_2C = 1.0 / np.sqrt(2 * C)
        sc = agg0 @ W_down_s * inv_sqrt_2C
        vc = jnp.einsum('ncx,cd->ndx', agg1, W_down_v) * inv_sqrt_2C
        skip_s = jnp.einsum('nc,ncd->nd', s, W_skip_s[node_species]) * inv_sqrt_C
        skip_v = jnp.einsum('ncx,ncd->ndx', v, W_skip_v[node_species]) * inv_sqrt_C
        sc = 0.5 * (sc + skip_s)
        vc = 0.5 * (vc + skip_v)
        feats = jax.nn.silu(sc[:, :C])
        gates = jax.nn.silu(sc[:, C:])
        vg = vc * gates[:, :, None]
        return jnp.concatenate([feats, vg.reshape(N, 3 * C)], axis=1)

    def _L2_gnn_ref(x, edge_index, edge_weights, msg_w, msg_b, msg_g, msg_beta, upd_w, upd_b, upd_g, upd_beta, gate_w, gate_b):
        import jax, jax.numpy as jnp
        import numpy as np
        N, E, H = (6250, 100000, 128)
        LN_EPS = 1e-05

        def layer_norm(x, gamma, beta):
            mu = jnp.mean(x, axis=-1, keepdims=True)
            var = jnp.mean((x - mu) ** 2, axis=-1, keepdims=True)
            return (x - mu) * jax.lax.rsqrt(var + LN_EPS) * gamma + beta
        num_nodes = x.shape[0]
        src, dst = (edge_index[0], edge_index[1])
        em = jnp.concatenate([x[src], x[dst]], axis=-1)
        em = jax.nn.relu(layer_norm(em @ msg_w + msg_b, msg_g, msg_beta))
        em = em * edge_weights[:, None]
        msgs = jax.ops.segment_sum(em, dst, num_segments=num_nodes)
        counts = jax.ops.segment_sum(jnp.ones((src.shape[0], 1), x.dtype), dst, num_segments=num_nodes)
        valid = (counts > 0).astype(x.dtype)
        messages = msgs / (counts + 1e-08) * valid
        gate = jax.nn.sigmoid(x @ gate_w + gate_b)
        combined = jnp.concatenate([x, messages], axis=-1)
        h_new = jax.nn.relu(layer_norm(combined @ upd_w + upd_b, upd_g, upd_beta))
        return gate * h_new + (1.0 - gate) * x

    def _L3_gnn_ref(x, edge_index, edge_type, edge_weight, w_rel, w_root, b_conv, w_skip, b_skip):
        import jax, jax.numpy as jnp
        import numpy as np
        N_NODES = 6250
        N_EDGES = 75000
        D_IN = 128
        DIM = 128
        N_REL = 3
        N_LAYERS = 2
        n = x.shape[0]
        src, dst = (edge_index[0], edge_index[1])
        h = x
        for l in range(w_rel.shape[0]):
            skip = x @ w_skip[l] + b_skip[l]
            hr = jnp.einsum('nd,rde->rne', h, w_rel[l])
            msgs = hr[edge_type, src] * edge_weight[:, None]
            agg = jax.ops.segment_sum(msgs, dst, num_segments=n)
            h = agg + h @ w_root[l] + b_conv[l] + skip
        return h
    edge_index = jnp.stack([src, dst])
    h = jnp.maximum(_layernorm(x, axis=-1), 0.0)
    x = x + _L0_gnn_ref(h, edge_index, L0_gnn_W_rel, L0_gnn_W_root, L0_gnn_b_rel)
    h = jnp.maximum(_layernorm(x, axis=-1), 0.0)
    x = x + _L1_gnn_ref(h, edge_attr_4, edge_attr_8, src, dst, node_type_5, L1_gnn_W_up_s, L1_gnn_W_up_v, L1_gnn_W_r1, L1_gnn_W_r2, L1_gnn_W_down_s, L1_gnn_W_down_v, L1_gnn_W_skip_s, L1_gnn_W_skip_v)
    h = jnp.maximum(_layernorm(x, axis=-1), 0.0)
    x = x + _L2_gnn_ref(h, edge_index, edge_weight, L2_gnn_msg_w, L2_gnn_msg_b, L2_gnn_msg_g, L2_gnn_msg_beta, L2_gnn_upd_w, L2_gnn_upd_b, L2_gnn_upd_g, L2_gnn_upd_beta, L2_gnn_gate_w, L2_gnn_gate_b)
    h = jnp.maximum(_layernorm(x, axis=-1), 0.0)
    x = x + _L3_gnn_ref(h, edge_index, edge_type_3, edge_weight, L3_gnn_w_rel, L3_gnn_w_root, L3_gnn_b_conv, L3_gnn_w_skip, L3_gnn_b_skip)
    return x

_drawn_inputs = setup_inputs


def setup_inputs(seed=0):
    import zlib

    import numpy as np

    out = dict(_drawn_inputs(seed))
    spreads = {'L2_gnn_msg_b': (0.0, 0.1),
     'L2_gnn_msg_g': (1.0, 0.2),
     'L2_gnn_msg_beta': (0.0, 0.1),
     'L2_gnn_upd_b': (0.0, 0.1),
     'L2_gnn_upd_g': (1.0, 0.2),
     'L2_gnn_upd_beta': (0.0, 0.1),
     'L3_gnn_b_conv': (0.0, 0.1),
     'L3_gnn_b_skip': (0.0, 0.1)}
    factors = {}
    for name, (base, spread) in spreads.items():
        noise = np.random.default_rng([zlib.crc32(name.encode()), seed]).standard_normal(out[name].shape)
        drawn = base * np.exp(spread * noise) if base else spread * noise
        out[name] = jnp.asarray(drawn.astype(out[name].dtype))
    for name, factor in factors.items():
        out[name] = (out[name] * factor).astype(out[name].dtype)
    return out
```

```python
from contextlib import ExitStack

import numpy as np

import concourse.bass as bass
from concourse import mybir

P = 128
GROUP = 4
BATCH_GROUPS = 4
SLOTS = 8
TURN_BATCHES = 4
TURN_GROUPS = TURN_BATCHES * BATCH_GROUPS
BATCH_TILES = BATCH_GROUPS * GROUP
TURN_TILES = TURN_GROUPS * GROUP
WINDOW = 48
GROUP_EDGES = GROUP * P
BATCH_EDGES = BATCH_TILES * P
TURN_EDGES = TURN_TILES * P
FAR = float(1 << 21)
EPS = 1e-5

C = 32
R = 8
SPECIES = 5
SKIP = 2 * C + 3 * C
DEG = 16.0
REL = 3

F32 = mybir.dt.float32
I32 = mybir.dt.int32
ALU = mybir.AluOpType
ACT = mybir.ActivationFunctionType
AX = mybir.AxisListType.X


class Counter:

    def __init__(self, sem, credit=False):
        self.sem = sem
        self.value = 0
        self.credit = credit


class Prev:

    def __init__(self, key):
        self.key = key


def ring(name, i, size, turn=None):
    if i >= size:
        return (name, i - size)
    return Prev((name, i - size + turn)) if turn else None


class Stage:

    def __init__(self, counters, ticks=None):
        self.counters = counters
        self.ticks = ticks or {}
        self.queues = {name: [] for name in ("sync", "scalar", "vector", "gpsimd", "tensor")}
        self.steps = {}

    def wait(self, engine, *keys):
        for key in keys:
            if key is not None:
                self.queues[engine].append(("wait", key))

    def do(self, engine, key, fn, *after, by=1, counter=None):
        self.wait(engine, *after)
        c = self.counters[counter or engine]
        c.value += by
        self.queues[engine].append(("do", fn, c, by))
        if key is not None:
            self.steps[key] = (c, c.value)

    def dma(self, engine, key, counter, fn, *after):
        self.do(engine, key, fn, *after, by=16, counter=counter)

    def straight(self, nc):
        with nc.Block() as block:
            for name, queue in self.queues.items():
                if queue:
                    getter = {"sync": block.sync, "scalar": block.scalar, "vector": block.vector,
                              "gpsimd": block.gpsimd, "tensor": block.tensor}[name]

                    @getter
                    def _(e, queue=queue):
                        seen = {}
                        for item in queue:
                            if item[0] == "wait":
                                c, value = self.steps[item[1]]
                                if seen.get(c, 0) < value:
                                    e.wait_ge(c.sem, value)
                                    seen[c] = value
                            else:
                                _, fn, c, by = item
                                fn(e).then_inc(c.sem, by)

    def turn(self, e, engine, it):
        seen, pending = {}, {}
        for item in self.queues[engine]:
            if item[0] == "wait":
                prev = isinstance(item[1], Prev)
                c, value = self.steps[item[1].key if prev else item[1]]
                assert c.credit or not prev
                at = value + c.value if c.credit and not prev else value
                if seen.get(c, 0) < at:
                    seen[c] = pending[c] = at
                continue
            values = [(c.sem, e.snap(it * c.value + at)) for c, at in pending.items()]
            for sem, value in values:
                e.wait_ge(sem, value)
            if pending and engine in self.ticks:
                e.sem_inc(self.ticks[engine], 1)
            pending = {}
            _, fn, c, by = item
            fn(e, it).then_inc(c.sem, by)


def build(nc, a, out, shapes):
    N, E = shapes
    NT = -(-N // P)
    REST = N - (NT - 1) * P
    TURNS = -(-E // TURN_EDGES)
    BATCHES = TURN_BATCHES * TURNS
    GROUPS = TURNS * TURN_GROUPS
    TILES = TURNS * TURN_TILES
    MOST_PASSES = -(-N // WINDOW)
    ACC = (NT + 1) * P

    top = ExitStack()
    with top:
        def dram(name, shape, dt=F32):
            return nc.dram_tensor(name, shape, dt, kind="Internal").ap()

        names = {}

        def own(name):
            names[name] = names.get(name, 0) + 1
            return name if names[name] == 1 else f"{name}_{names[name]}"

        def sb(stack, name, shape, dt=F32):
            return stack.enter_context(nc.sbuf_tensor(own(name), shape, dt))

        def ps(stack, name, shape):
            return stack.enter_context(nc.psum_tensor(own(name), shape, F32))

        table = dram("table", (N, P))
        rel_table = dram("rel_table", (REL * N, P))
        window_table = dram("window_table", (ACC, P))
        base_dram = dram("base_dram", (1, GROUPS))
        span_dram = dram("span_dram", (1, BATCHES))
        local_cols = dram("local_cols", (P, TILES))
        local_rows = dram("local_rows", (BATCHES, BATCH_EDGES))
        rel_cols = dram("rel_cols", (P, TILES), I32)

        x = sb(top, "x", [P, NT, P])
        acc = sb(top, "acc", [P, 2, ACC])
        ident = sb(top, "ident", [P, P])
        ones = sb(top, "ones", [P, P])
        zero = sb(top, "zero", [P, P])
        iota = sb(top, "iota", [P, WINDOW])
        iota_col = sb(top, "iota_col", [P, 1])
        iota_pass = sb(top, "iota_pass", [P, WINDOW])
        iota_col_pass = sb(top, "iota_col_pass", [P, 1])
        base_row = sb(top, "base_row", [1, GROUPS])
        base_pass = sb(top, "base_pass", [1, GROUPS])
        address = sb(top, "address", [1, GROUPS], I32)
        passes = sb(top, "passes", [1, 1], I32)
        rcount = sb(top, "rcount", [P, NT])
        species = sb(top, "species", [P, NT, SPECIES])
        gate = sb(top, "gate", [P, NT])
        stat = sb(top, "stat", [P, NT, 2])
        rstd = sb(top, "rstd", [P, NT])
        shift = sb(top, "shift", [P, NT])

        straight = {n: Counter(top.enter_context(nc.semaphore(f"done_{n}")))
                    for n in ("sync", "scalar", "vector", "gpsimd", "tensor")}
        NLOAD = 12
        for n in [f"load{i}" for i in range(NLOAD)] + [f"store{i}" for i in range(4)]:
            straight[n] = Counter(top.enter_context(nc.semaphore(n)))
        loop_sems = {n: top.enter_context(nc.semaphore(f"turn_{n}"))
                     for n in ["scalar", "vector", "tensor"] + [f"slot{i}" for i in range(SLOTS)]
                     + [f"idx{i}" for i in range(TURN_BATCHES)] + [f"edge{i}" for i in range(TURN_BATCHES)]
                     + [f"near{i}" for i in range(4)]}
        arrived = top.enter_context(nc.semaphore("arrived"))
        ticks = {n: top.enter_context(nc.semaphore(f"waited_{n}")) for n in ("gpsimd", "sync")}

        stores = [0]

        def store(s, key, fn, *after):
            i = stores[0] % 4
            stores[0] += 1
            s.dma("sync", key, f"store{i}", fn, *after, *( [last_store[i]] if last_store.get(i) in s.steps else []))
            last_store[i] = key

        last_store = {}

        def rms_inverse(s, tag, last_stat):
            s.do("vector", (tag, "eps"), lambda e: e.tensor_scalar(
                rstd[:, :], stat[:, :, 1], EPS, None, ALU.add), last_stat)
            s.do("scalar", (tag, "std"), lambda e: e.activation(
                rstd[:, :], rstd[:, :], ACT.Sqrt), (tag, "eps"))
            s.do("vector", (tag, "rstd"), lambda e: e.reciprocal(rstd[:, :], rstd[:, :]), (tag, "std"))
            s.do("vector", (tag, "norm"), lambda e: e.scalar_tensor_tensor(
                out=shift[:, :], in0=stat[:, :, 0], scalar=-1.0, in1=rstd[:, :], op0=ALU.mult,
                op1=ALU.mult), (tag, "rstd"))

        def statistics(s, bn, i, src, ready, tag="x"):
            s.do("vector", (tag, "bn", i), lambda e: e.bn_stats(bn[:, i % 4, :], src), ready)
            s.do("vector", (tag, "stat", i), lambda e: e.bn_aggr(stat[:, i, :], bn[:, i % 4, :]),
                 (tag, "bn", i))

        def vectors_last(ap):
            return ap.rearrange("p (c k) -> p k c", k=3)

        def normed(s, h, pT, hT, i, by_component=False, user=None):
            def relu(dst, src):
                return lambda e: e.activation(dst, src, ACT.Relu, bias=shift[:, i:i + 1],
                                              scale=rstd[:, i:i + 1])
            used = [ring("h_turned", i, 3)] + ([ring(user, i, 3)] if user else [])
            if not by_component:
                s.do("scalar", ("h", i), relu(h[:, i % 3, :], x[:, i, :]), ("x", "norm"), *used)
            else:
                s.do("scalar", None, relu(h[:, i % 3, 0:C], x[:, i, 0:C]), ("x", "norm"), *used)
                s.do("scalar", ("h", i), relu(
                    h[:, i % 3, C:P].rearrange("p (k c) -> p k c", k=3),
                    vectors_last(x[:, i, C:P])))
            s.do("tensor", ("h_turned", i), lambda e: e.transpose(
                pT[:, i % 2, :], h[:, i % 3, :], ident[:, :]), ("h", i), ring("hT", i, 2))
            s.do("vector", ("hT", i), lambda e: e.tensor_copy(hT[:, i % 2, :], pT[:, i % 2, :]),
                 ("h_turned", i), ring("hT_used", i, 2))

        def rows(i):
            return REST if i == NT - 1 else P

        def load_weights(st, specs):
            tiles, s = {}, Stage(straight)
            for n, (name, shape, parts) in enumerate(specs):
                tiles[name] = t = sb(st, name, shape)
                if parts[0][2] is not None:
                    s.do("gpsimd", ("zeroed", name), lambda e, t=t: e.memset(t[:], 0.0))
                for m, (dst, src, _) in enumerate(parts):
                    s.dma("sync", ("loaded", name), f"load{n % NLOAD}",
                          lambda e, d=dst, q=src, t=t: e.dma_start(d(t), q),
                          *([("zeroed", name)] if parts[0][2] is not None else []))
            for name, *_ in specs:
                s.wait("sync", ("loaded", name))
            s.straight(nc)
            return tiles

        def whole(name, shape, src):
            return (name, shape, [(lambda t: t[:], src, None)])

        def message_stage(name, body, source, index_cols, extra_cols, st, near=False):
            s = Stage(straight)
            s.do("vector", ("base", name), lambda e: e.tensor_copy(base_pass[:, :], base_row[:, :]))
            s.do("vector", ("address", name), lambda e: e.tensor_scalar(
                address[:, :], base_pass[:, :], float(N), None, ALU.min), ("base", name))
            s.do("vector", None, lambda e: e.tensor_copy(iota_pass[:, :], iota[:, :]))
            s.do("vector", ("reset", name), lambda e: e.tensor_copy(iota_col_pass[:, :], iota_col[:, :]))
            s.wait("vector", ("reset", name))
            s.straight(nc)

            engines = ("scalar", "vector", "tensor")
            counters = {n: Counter(v, n in engines) for n, v in loop_sems.items()}
            s = Stage(counters, ticks)
            gathered = sb(st, "gathered_" + name, [P, SLOTS, GROUP, P])
            index = sb(st, "index_" + name, [P, TURN_BATCHES, BATCH_TILES], I32)

            def stage_edges(b):
                groups = range(b * BATCH_GROUPS, (b + 1) * BATCH_GROUPS)
                s.dma("sync", ("index", b), f"idx{b}", lambda e, it: e.dma_start(
                    index[:, b, :], index_cols[:, bass.ds(it * TURN_TILES + b * BATCH_TILES, BATCH_TILES)]),
                    *[Prev(("rows_used", g)) for g in groups])
                s.wait("sync", *[Prev(("edges_used", g)) for g in groups])
                for tile, src in extra_cols:
                    s.dma("sync", ("edges", b), f"edge{b}",
                          lambda e, it, tile=tile, src=src: e.dma_start(tile[:, b], src(it, b)))

            def gather(g):
                b, k = g // BATCH_GROUPS, g % BATCH_GROUPS
                s.wait("gpsimd", ("index", b), ring("rows_used", g, SLOTS, TURN_GROUPS))
                for t in range(GROUP):
                    s.dma("gpsimd", ("gathered", g), f"slot{g % SLOTS}", lambda e, it, t=t: e.indirect_dma_start(
                        gathered[:, g % SLOTS, t, :], None, source[:, :], bass.IndirectOffsetOnAxis(
                            ap=index[:, b, k * GROUP + t:k * GROUP + t + 1], axis=0)))

            for b in range(TURN_BATCHES + 1):
                if b < TURN_BATCHES:
                    stage_edges(b)
                if near and b:
                    for g in range((b - 1) * BATCH_GROUPS, b * BATCH_GROUPS):
                        near(s, g)
            for g in range(TURN_GROUPS):
                gather(g)
            body(s, gathered)
            used = [n for n, c in counters.items() if c.value]

            go = top.enter_context(nc.semaphore("go_" + name))
            with nc.Block() as block:
                getters = {"sync": block.sync, "scalar": block.scalar, "vector": block.vector,
                           "gpsimd": block.gpsimd, "tensor": block.tensor}
                for engine in getters:
                    @getters[engine]
                    def _(e, engine=engine):
                        count = e.value_load(passes[0:1, 0:1], min_val=1, max_val=MOST_PASSES)
                        with e.Fori(0, count) as turn_of_pass:
                            if engine in engines and counters[engine].value:
                                e.sem_inc(counters[engine].sem, counters[engine].value)
                            with e.Fori(0, TURNS) as it:
                                s.turn(e, engine, it)
                            if engine in engines and counters[engine].value:
                                e.wait_ge(counters[engine].sem, counters[engine].value * (TURNS + 1))
                            if engine == "vector":
                                e.tensor_scalar(iota_pass[:, :], iota_pass[:, :], float(WINDOW), None, ALU.add).then_inc(counters["vector"].sem, 1)
                                e.tensor_scalar(iota_col_pass[:, :], iota_col_pass[:, :], float(WINDOW), None, ALU.add).then_inc(counters["vector"].sem, 1)
                                e.tensor_scalar(base_pass[:, :], base_pass[:, :], float(WINDOW), None, ALU.add).then_inc(counters["vector"].sem, 1)
                                at = counters["vector"].value * (TURNS + 1)
                                e.wait_ge(counters["vector"].sem, at + 3)
                                e.tensor_scalar(address[:, :], base_pass[:, :], float(N), None, ALU.min).then_inc(counters["vector"].sem, 1)
                                e.wait_ge(counters["vector"].sem, at + 4)
                            if engine == "gpsimd":
                                slots = [loop_sems[f"slot{k}"] for k in range(SLOTS)]
                                for slot in slots:
                                    e.wait_ge(slot, 16 * GROUP * (TURN_GROUPS // SLOTS) * TURNS)
                                e.dma_reset(range(slots[0].num, slots[-1].num + 1))
                            if engine != "sync":
                                e.sem_inc(arrived, 1)
                                e.wait_ge(go, turn_of_pass + 1)
                            else:
                                e.wait_ge(arrived, 4)
                                for n in used:
                                    e.sem_clear(counters[n].sem)
                                e.sem_clear(arrived)
                                for tick in ticks.values():
                                    e.sem_clear(tick)
                                e.sem_inc(go, 1)

        def column(src):
            return lambda it, b: src[:, bass.ds(it * TURN_TILES + b * BATCH_TILES, BATCH_TILES)]

        def place(g):
            return g // BATCH_GROUPS, (g % BATCH_GROUPS) * GROUP

        def select(s, sel, local, weight, g):
            b, at = place(g)
            s.wait("vector", ("edges", b), ring("summed", g, 4, TURN_GROUPS))
            for t in range(GROUP):
                s.do("vector", ("selected", g), lambda e, it, t=t: e.tensor_scalar(
                    sel[:, g % 4, t, :], iota_pass[:, :], local[:, b, at + t:at + t + 1],
                    weight[:, b, at + t:at + t + 1] if weight is not None else None,
                    ALU.is_equal, *([ALU.mult] if weight is not None else [])))

        def accumulate(s, psum, g, n=1):
            def add(e, it):
                at = e.value_load(address[0:1, bass.ds(it * TURN_GROUPS + g, 1)], min_val=0, max_val=N)
                sums = acc[:, 0:n, bass.ds(at, WINDOW)]
                return e.tensor_tensor(sums, sums, psum, ALU.add)
            s.do("vector", ("added", g), add, ("summed", g), ring("added", g, 1, TURN_GROUPS))

        def staggered(*steps):
            for k in range(TURN_GROUPS + max(lag for lag, _ in steps)):
                for lag, step in steps:
                    if 0 <= k - lag < TURN_GROUPS:
                        step(k - lag)

        def plain_messages(name, source, index_cols, weight_cols=None, counts=False):
            with ExitStack() as st:
                local = sb(st, "local_" + name, [P, TURN_BATCHES, BATCH_TILES])
                weight = sb(st, "weight_" + name, [P, TURN_BATCHES, BATCH_TILES]) if weight_cols is not None else None
                sel = sb(st, "select_" + name, [P, 4, GROUP, WINDOW])
                sums = ps(st, "sums_" + name, [P, 4, 512])
                extra = [(local, column(local_cols))]
                if weight is not None:
                    extra.append((weight, column(weight_cols)))
                n = 2 if counts else 1

                def body(s, gathered):
                    def multiply(g):
                        s.wait("tensor", ("gathered", g), ("selected", g), ring("added", g, 4, TURN_GROUPS))
                        for t in range(GROUP):
                            s.do("tensor", ("summed", g), lambda e, it, t=t: e.matmul(
                                sums[:, g % 4, 0:WINDOW], gathered[:, g % SLOTS, t, :], sel[:, g % 4, t, :],
                                start=t == 0, stop=t == GROUP - 1))
                        s.steps[("rows_used", g)] = s.steps[("summed", g)]
                        if counts:
                            for t in range(GROUP):
                                s.do("tensor", ("summed", g), lambda e, it, t=t: e.matmul(
                                    sums[:, g % 4, WINDOW:2 * WINDOW], ones[:, :], sel[:, g % 4, t, :],
                                    start=t == 0, stop=t == GROUP - 1))
                        s.steps[("edges_used", g)] = s.steps[("summed", g)]

                    staggered((0, lambda g: select(s, sel, local, weight, g)), (0, multiply),
                              (2, lambda g: accumulate(s, sums[:, g % 4, 0:n * WINDOW].rearrange(
                                  "p (n w) -> p n w", n=n), g, n)))

                message_stage(name, body, source, index_cols, extra, st)

        def clear_accumulator(s, n, key):
            for k in range(n):
                s.do("gpsimd", key, lambda e, k=k: e.memset(acc[:, k, :], 0.0))

        with ExitStack() as st:
            dst_i = sb(st, "dst_i", [BATCHES, BATCH_EDGES], I32)
            dst_f = sb(st, "dst_f", [BATCHES, BATCH_EDGES])
            dst_far = sb(st, "dst_far", [BATCHES, BATCH_EDGES])
            base_g = sb(st, "base_g", [BATCHES, BATCH_GROUPS])
            last_g = sb(st, "last_g", [BATCHES, BATCH_GROUPS])
            span_g = sb(st, "span_g", [BATCHES, 1])
            span_row = sb(st, "span_row", [1, BATCHES])
            firsts = sb(st, "firsts", [1, MOST_PASSES])
            span_f = sb(st, "span_f", [1, 1])
            s = Stage(straight)
            s.do("gpsimd", None, lambda e: e.memset(x[:, NT - 1, :], 0.0))
            s.do("gpsimd", "ident0", lambda e: e.memset(ident[:, :], 0.0))
            s.do("gpsimd", "ident", lambda e: e.affine_select(
                out=ident[:, :], in_=ident[:, :], compare_op=ALU.not_equal, fill=1.0, base=0,
                pattern=[[-1, P]], channel_multiplier=1), "ident0")
            s.do("gpsimd", None, lambda e: e.memset(ones[:, :], 1.0))
            s.do("gpsimd", None, lambda e: e.memset(zero[:, :], 0.0))
            s.do("gpsimd", None, lambda e: e.iota(iota[:, :], [[1, WINDOW]], base=0, channel_multiplier=0,
                                                  allow_small_or_imprecise_dtypes=True))
            s.do("gpsimd", "constants", lambda e: e.iota(iota_col[:, :], [[0, 1]], base=0,
                                                         channel_multiplier=1,
                                                         allow_small_or_imprecise_dtypes=True))
            s.do("gpsimd", "firsts", lambda e: e.iota(
                firsts[:, :], [[WINDOW, MOST_PASSES]], base=0, channel_multiplier=0,
                allow_small_or_imprecise_dtypes=True))
            clear_accumulator(s, 2, "cleared")
            s.dma("sync", "dst_g", "load0", lambda e: e.dma_start(dst_i[:, :], a["dst_rows"]))
            s.dma("sync", "x", "load5", lambda e: e.dma_start(
                x[:, 0:NT - 1, :], a["x"][0:(NT - 1) * P, :].rearrange("(t p) f -> p t f", p=P)))
            s.dma("sync", "x", "load5", lambda e: e.dma_start(
                x[0:REST, NT - 1, :], a["x"][(NT - 1) * P:N, :]), "constants")
            grouped = lambda t: t[:, :].rearrange("h (g e) -> h g e", g=BATCH_GROUPS)
            s.do("vector", "dst_f", lambda e: e.tensor_copy(dst_f[:, :], dst_i[:, :]), "dst_g")
            s.do("vector", "far", lambda e: e.tensor_scalar(
                dst_far[:, :], dst_f[:, :], 0.0, FAR, ALU.is_lt, ALU.mult), "dst_f")
            s.do("vector", "dst_far", lambda e: e.tensor_tensor(
                dst_far[:, :], dst_far[:, :], dst_f[:, :], ALU.add), "far")
            s.do("vector", "base_g", lambda e: e.tensor_reduce(
                base_g[:, :], grouped(dst_far), AX, ALU.min), "dst_far")
            s.do("vector", "last_g", lambda e: e.tensor_reduce(
                last_g[:, :], grouped(dst_f), AX, ALU.max), "dst_f")
            s.do("vector", "last_less", lambda e: e.tensor_tensor(
                last_g[:, :], last_g[:, :], base_g[:, :], ALU.subtract), "base_g", "last_g")
            s.do("vector", "span_g", lambda e: e.tensor_reduce(
                span_g[:, :], last_g[:, :], AX, ALU.max), "last_less")
            s.do("vector", "local_rows", lambda e: e.tensor_tensor(
                grouped(dst_far), grouped(dst_f),
                base_g[:, :].unsqueeze(2).to_broadcast([BATCHES, BATCH_GROUPS, GROUP_EDGES]),
                ALU.subtract), "base_g")
            s.dma("sync", "base_out", "store0", lambda e: e.dma_start(
                base_dram[0, :].rearrange("(h g) -> h g", g=BATCH_GROUPS), base_g[:, :]), "base_g")
            s.dma("sync", "span_out", "store1", lambda e: e.dma_start(
                span_dram[0, :].unsqueeze(1), span_g[:, :]), "span_g")
            s.dma("sync", "rows_out", "store2", lambda e: e.dma_start(local_rows, dst_far[:, :]), "local_rows")
            s.dma("sync", "base_row", "load7", lambda e: e.dma_start(base_row[:, :], base_dram), "base_out")
            s.dma("sync", "span_row", "load8", lambda e: e.dma_start(span_row[:, :], span_dram), "span_out")
            s.do("vector", "span_f", lambda e: e.tensor_reduce(span_f[:, :], span_row[:, :], AX, ALU.max), "span_row")
            s.do("vector", "reached", lambda e: e.tensor_scalar(
                firsts[:, :], firsts[:, :], span_f[:, 0:1], None, ALU.is_le), "span_f", "firsts")
            s.do("vector", "reached_n", lambda e: e.tensor_reduce(
                span_f[:, :], firsts[:, :], AX, ALU.add), "reached")
            s.do("vector", "passes", lambda e: e.tensor_scalar(
                passes[:, :], span_f[:, :], 1.0, None, ALU.max), "reached_n")
            s.wait("vector", "passes", "local_rows")
            s.wait("sync", "rows_out", "span_out", "base_out", "base_row", "x")
            s.wait("gpsimd", "cleared")
            s.straight(nc)

        with ExitStack() as st:
            col_i = sb(st, "col_i", [P, TILES], I32)
            type_i = sb(st, "type_i", [P, TILES], I32)
            src_i = sb(st, "src_i", [P, TILES], I32)
            col_f = sb(st, "col_f", [P, TILES])
            src_f = sb(st, "src_f", [P, TILES])
            base_all = sb(st, "base_all", [P, GROUPS])
            kind_i = sb(st, "kind_i", [P, NT], I32)
            bn = sb(st, "bn0", [P, 4, 6])
            s = Stage(straight)
            s.dma("sync", "dst_c", "load1", lambda e: e.dma_start(col_i[:, :], a["dst_cols"]))
            s.dma("sync", "type_c", "load2", lambda e: e.dma_start(type_i[:, :], a["type_cols"]))
            s.dma("sync", "src_c", "load3", lambda e: e.dma_start(src_i[:, :], a["src_cols"]))
            s.dma("sync", "kind", "load4", lambda e: e.dma_start(kind_i[:, :], a["node_type"]))
            s.dma("sync", "base_all", "load6", lambda e: e.dma_start(
                base_all[:, :], base_dram[0, :].partition_broadcast(P)))
            s.do("vector", "col_f", lambda e: e.tensor_copy(col_f[:, :], col_i[:, :]), "dst_c")
            s.do("vector", "local_cols", lambda e: e.tensor_tensor(
                col_f[:, :].rearrange("p (g t) -> p g t", t=GROUP),
                col_f[:, :].rearrange("p (g t) -> p g t", t=GROUP),
                base_all[:, :].unsqueeze(2).to_broadcast([P, GROUPS, GROUP]), ALU.subtract), "col_f", "base_all")
            s.dma("sync", "cols_out", "store3", lambda e: e.dma_start(local_cols, col_f[:, :]), "local_cols")
            s.do("vector", "src_f", lambda e: e.tensor_copy(src_f[:, :], src_i[:, :]), "src_c")
            s.do("vector", "rel", lambda e: e.scalar_tensor_tensor(
                out=type_i[:, :], in0=type_i[:, :], scalar=float(N), in1=src_f[:, :],
                op0=ALU.mult, op1=ALU.add), "src_f", "type_c")
            s.dma("sync", "rel_out", "store0", lambda e: e.dma_start(rel_cols, type_i[:, :]), "rel")
            for k in range(SPECIES):
                s.do("vector", None, lambda e, k=k: e.tensor_scalar(
                    species[:, :, k], kind_i[:, :], float(k), None, ALU.is_equal), "kind")
            for i in range(NT):
                statistics(s, bn, i, x[:, i, :], None)
            rms_inverse(s, "x", ("x", "stat", NT - 1))
            s.wait("vector", ("x", "norm"))
            s.wait("sync", "cols_out", "rel_out")
            s.straight(nc)

        with ExitStack() as st:
            w = load_weights(st, [whole("root0", [P, P], a["L0_root_t"]), whole("brel", [1, P], a["L0_gnn_b_rel"])])
            h, hT = sb(st, "h", [P, 3, P]), sb(st, "hT", [P, 2, P])
            pT, pm = ps(st, "pT", [P, 2, P]), ps(st, "pm", [P, 2, 512])
            s = Stage(straight)
            s.steps[("x", "norm")] = (straight["vector"], straight["vector"].value)
            for i in range(NT):
                normed(s, h, pT, hT, i, user="h_used")
                store(s, ("h_used", i), lambda e, i=i: e.dma_start(
                    table[i * P:i * P + rows(i), :], h[0:rows(i), i % 3, :]), ("h", i))
                s.do("tensor", None, lambda e, i=i: e.matmul(
                    pm[:, i % 2, 0:P], hT[:, i % 2, :], w["root0"][:, :], start=True, stop=False),
                    ("hT", i), ring("root", i, 2))
                s.do("tensor", ("hT_used", i), lambda e, i=i: e.matmul(
                    pm[:, i % 2, 0:P], ones[0:1, :], w["brel"][0:1, :], start=False, stop=True))
                s.do("vector", ("root", i), lambda e, i=i: e.tensor_tensor(
                    x[:, i, :], x[:, i, :], pm[:, i % 2, 0:P], ALU.add), ("hT_used", i))
            s.wait("sync", *[("h_used", i) for i in range(max(0, NT - 4), NT)])
            s.wait("vector", ("root", NT - 1))
            s.straight(nc)

        plain_messages("sum0", table, a["src_cols"], counts=True)

        with ExitStack() as st:
            w = load_weights(st, [
                whole("rel0", [P, P], a["L0_rel_t"]),
                ("up", [P, P], [(lambda t: t[0:C, 0:C], a["L1_gnn_W_up_s"], 0)] + [
                    (lambda t, k=k: t[C * k:C * (k + 1), C * k:C * (k + 1)], a["L1_gnn_W_up_v"], 0)
                    for k in (1, 2, 3)])])
            h, hT = sb(st, "h", [P, 3, P]), sb(st, "hT", [P, 2, P])
            rowbuf = sb(st, "rowbuf", [P, 3, P])
            cnt = sb(st, "cnt", [P, NT])
            bn = sb(st, "bn1", [P, 4, 6])
            pT, pm, pc = ps(st, "pT", [P, 2, P]), ps(st, "pm", [P, 2, 512]), ps(st, "pc", [P, NT])
            s = Stage(straight)
            s.do("vector", "up_scaled", lambda e: e.tensor_scalar(w["up"][:, :], w["up"][:, :], C ** -0.5, None, ALU.mult))
            for i in range(NT):
                nodes = slice(i * P, (i + 1) * P)
                s.do("tensor", ("rel", i), lambda e, i=i, nodes=nodes: e.matmul(
                    pm[:, i % 2, 0:P], acc[:, 0, nodes], w["rel0"][:, :], start=True, stop=True),
                    ring("x1", i, 2))
                s.do("tensor", ("count", i), lambda e, i=i, nodes=nodes: e.matmul(
                    pc[:, i:i + 1], acc[0:1, 1, nodes], ones[0:1, 0:1], start=True, stop=True))
                s.do("vector", ("x1", i), lambda e, i=i: e.tensor_tensor(
                    x[:, i, :], x[:, i, :], pm[:, i % 2, 0:P], ALU.add), ("rel", i))
                statistics(s, bn, i, x[:, i, :], ("x1", i))
            s.do("vector", "cnt", lambda e: e.tensor_scalar(cnt[:, :], pc[:, :], 1e-8, None, ALU.add), ("count", NT - 1))
            s.do("vector", "rcnt", lambda e: e.reciprocal(rcount[:, :], cnt[:, :]), "cnt")
            s.do("vector", "valid", lambda e: e.tensor_scalar(cnt[:, :], pc[:, :], 0.0, None, ALU.is_gt), "rcnt")
            s.do("vector", "rcount", lambda e: e.tensor_tensor(rcount[:, :], rcount[:, :], cnt[:, :], ALU.mult), "valid")
            s.wait("gpsimd", ("count", NT - 1))
            clear_accumulator(s, 2, "cleared")
            rms_inverse(s, "x", ("x", "stat", NT - 1))
            for i in range(NT):
                normed(s, h, pT, hT, i, by_component=True)
                s.do("tensor", ("hT_used", i), lambda e, i=i: e.matmul(
                    pm[:, i % 2, 0:P], hT[:, i % 2, :], w["up"][:, :], start=True, stop=True),
                    ("hT", i), "up_scaled", ring("row", i, 2) or ("x1", NT - 1))
                s.do("vector", ("row", i), lambda e, i=i: e.tensor_copy(
                    rowbuf[:, i % 3, :], pm[:, i % 2, 0:P]), ("hT_used", i), ring("row_out", i, 3))
                store(s, ("row_out", i), lambda e, i=i: e.dma_start(
                    table[i * P:i * P + rows(i), :], rowbuf[0:rows(i), i % 3, :]), ("row", i))
            s.wait("sync", *[("row_out", i) for i in range(max(0, NT - 4), NT)])
            s.wait("gpsimd", "cleared")
            s.straight(nc)

        with ExitStack() as st:
            w = load_weights(st, [
                ("radial", [P, P], [(lambda t, k=k: t[R * k:R * (k + 1), R * k:R * (k + 1)], a["L1_gnn_W_r1"], 0)
                                    for k in range(BATCH_TILES)]),
                ("paths", [P, GROUP, 4 * C], [(lambda t, k=k: t[R * k:R * (k + 1), k % GROUP, :], a["L1_gnn_W_r2"], 0)
                                              for k in range(BATCH_TILES)])])
            local = sb(st, "local_1", [P, TURN_BATCHES, BATCH_TILES])
            sh = sb(st, "sh", [P, TURN_BATCHES, BATCH_TILES * 4])
            radial_in = sb(st, "radial_in", [P, TURN_BATCHES, P])
            hidden = sb(st, "hidden", [P, 2, P])
            hit = sb(st, "hit", [P, 2, GROUP, WINDOW])
            sel = sb(st, "sel_1", [P, 3, GROUP, 4, WINDOW])
            mess = sb(st, "mess", [P, 2, GROUP, 2 * P])
            p_hidden = ps(st, "p_hidden", [P, 512])
            p_path = ps(st, "p_path", [P, 2, GROUP, 4 * C])
            sums = ps(st, "sums_1", [P, 2, 2, 512])
            s = Stage(straight)
            s.do("vector", "p", lambda e: e.tensor_scalar(w["paths"][:, :, :], w["paths"][:, :, :], R ** -0.5, None, ALU.mult))
            s.do("vector", "p3", lambda e: e.tensor_scalar(w["paths"][:, :, 3 * C:], w["paths"][:, :, 3 * C:], 3.0 ** -0.5, None, ALU.mult), "p")
            s.wait("vector", "p3")
            s.straight(nc)

            def body(s, gathered):
                def radial(b):
                    s.do("tensor", ("radial", b), lambda e, it: e.matmul(
                        p_hidden[:, 0:P], w["radial"][:, :], radial_in[:, b, :], start=True, stop=True),
                        ("edges", b), ring("hidden", b, 1, TURN_BATCHES))
                    s.do("scalar", ("hidden", b), lambda e, it: e.activation(
                        hidden[:, b % 2, :], p_hidden[:, 0:P], ACT.Silu, scale=R ** -0.5), ("radial", b),
                        ring("hidden_used", b, 2, TURN_BATCHES))

                def paths(g):
                    b, _ = place(g)
                    if g % BATCH_GROUPS == 0:
                        radial(b)
                    part = slice(32 * (g % BATCH_GROUPS), 32 * (g % BATCH_GROUPS) + 32)
                    s.wait("tensor", ("hidden", b), ring("product", g, 2, TURN_GROUPS))
                    for t in range(GROUP):
                        s.do("tensor", ("paths", g), lambda e, it, t=t: e.matmul(
                            p_path[:, g % 2, t, :], hidden[part, b % 2, :], w["paths"][part, t, :],
                            start=True, stop=True))
                    s.steps[("hidden_used", b)] = s.steps[("paths", g)]

                def selections(g):
                    b, at = place(g)
                    s.do("vector", ("hit", g), lambda e, it: e.tensor_tensor(
                        hit[:, g % 2, :, :], iota_pass[:, :].unsqueeze(1).to_broadcast([P, GROUP, WINDOW]),
                        local[:, b, at:at + GROUP].unsqueeze(2).to_broadcast([P, GROUP, WINDOW]), ALU.is_equal),
                        ("edges", b), ring("selected0", g, 2, TURN_GROUPS))
                    s.wait("scalar", ("hit", g), ring("summed", g, 3, TURN_GROUPS))
                    for t in range(GROUP):
                        s.do("scalar", ("selected0", g), lambda e, it, t=t: e.activation(
                            sel[:, g % 3, t, 0, :], hit[:, g % 2, t, :], ACT.Copy,
                            scale=sh[:, b, 4 * (at + t):4 * (at + t) + 1]))
                    s.do("vector", ("selected", g), lambda e, it: e.tensor_tensor(
                        sel[:, g % 3, :, 1:4, :],
                        hit[:, g % 2, :, :].unsqueeze(2).to_broadcast([P, GROUP, 3, WINDOW]),
                        sh[:, b, 4 * at:4 * (at + GROUP)].rearrange("p (t k) -> p t k", k=4)[:, :, 1:4]
                        .unsqueeze(3).to_broadcast([P, GROUP, 3, WINDOW]), ALU.mult),
                        ("hit", g), ring("summed", g, 3, TURN_GROUPS))

                def products(g):
                    rows_ = gathered[:, g % SLOTS, :, :]
                    vec = rows_[:, :, C:].rearrange("p t (k c) -> p t k c", k=3)
                    m = mess[:, g % 2, :, :]
                    pw = p_path[:, g % 2, :, :]
                    s.do("vector", None, lambda e, it: e.tensor_tensor(
                        m.rearrange("p t (n c) -> p t n c", n=2)[:, :, :, 0:C],
                        rows_[:, :, 0:C].unsqueeze(2).to_broadcast([P, GROUP, 2, C]),
                        pw[:, :, 0:2 * C].rearrange("p t (n c) -> p t n c", n=2), ALU.mult),
                        ("paths", g), ("gathered", g), ring("summed", g, 2, TURN_GROUPS))
                    for n in range(2):
                        s.do("vector", ("product", g), lambda e, it, n=n: e.tensor_tensor(
                            m[:, :, n * P + C:(n + 1) * P].rearrange("p t (k c) -> p t k c", k=3), vec,
                            pw[:, :, (2 + n) * C:(3 + n) * C].unsqueeze(2).to_broadcast([P, GROUP, 3, C]), ALU.mult))
                    s.steps[("rows_used", g)] = s.steps[("product", g)]

                def multiply(g):
                    s.wait("tensor", ("product", g), ("selected", g), ("selected0", g),
                           ring("added", g, 2, TURN_GROUPS))
                    for t in range(GROUP):
                        first, last = t == 0, t == GROUP - 1
                        s.do("tensor", None, lambda e, it, t=t, f=first, l=last: e.matmul(
                            sums[:, g % 2, 0, 0:WINDOW], mess[:, g % 2, t, 0:P], sel[:, g % 3, t, 0, :], start=f, stop=l))
                        for k in range(3):
                            s.do("tensor", None, lambda e, it, t=t, k=k, f=first, l=last: e.matmul(
                                sums[C * k:C * (k + 1), g % 2, 1, 0:WINDOW], mess[:, g % 2, t, P:P + C],
                                sel[:, g % 3, t, 1 + k, :], start=f, stop=l))
                            s.do("tensor", ("summed", g), lambda e, it, t=t, k=k, f=first and k == 0, l=last and k == 2: e.matmul(
                                sums[3 * C:P, g % 2, 1, 0:WINDOW], mess[:, g % 2, t, P + C * (k + 1):P + C * (k + 2)],
                                sel[:, g % 3, t, 1 + k, :], start=f, stop=l))
                    s.steps[("edges_used", g)] = s.steps[("summed", g)]

                staggered((0, paths), (1, multiply), (0, selections), (0, products),
                          (1, lambda g: accumulate(s, sums[:, g % 2, :, 0:WINDOW], g, 2)))

            message_stage("messages1", body, table, a["src_cols"], [
                (local, column(local_cols)),
                (sh, lambda it, b: a["sh_cols"][:, bass.ds((it * TURN_TILES + b * BATCH_TILES) * 4, BATCH_TILES * 4)]),
                (radial_in, lambda it, b: a["radial_cols"][:, bass.ds((it * TURN_BATCHES + b) * P, P)])], st)

        local_term = acc[:, 1, 0:NT * P].rearrange("p (t f) -> p t f", f=P)
        with ExitStack() as st:
            down_s, down_v = a["L1_gnn_W_down_s"], a["L1_gnn_W_down_v"]
            specs = [("down_a", [P, SKIP], [(lambda t: t[0:C, 0:2 * C], down_s[0:C, :], 0)] + [
                        (lambda t, k=k: t[C * (k + 1):C * (k + 2), 2 * C + C * k:2 * C + C * (k + 1)], down_v[C:2 * C, :], 0)
                        for k in range(3)]),
                     ("down_b", [P, SKIP], [(lambda t: t[3 * C:P, 0:2 * C], down_s[C:2 * C, :], 0)] + [
                        (lambda t, k=k: t[C * k:C * (k + 1), 2 * C + C * k:2 * C + C * (k + 1)], down_v[0:C, :], 0)
                        for k in range(3)]),
                     ("skip", [P, SPECIES, SKIP], [
                         (lambda t, q=q: t[0:C, q, 0:2 * C], a["L1_gnn_W_skip_s"][q], 0) for q in range(SPECIES)] + [
                         (lambda t, q=q, k=k: t[C * (k + 1):C * (k + 2), q, 2 * C + C * k:2 * C + C * (k + 1)],
                          a["L1_gnn_W_skip_v"][q], 0) for q in range(SPECIES) for k in range(3)]),
                     whole("msg_src", [P, P], a["L2_gnn_msg_w"][0:P, :]),
                     whole("msg_dst", [P, P], a["L2_gnn_msg_w"][P:2 * P, :]),
                     whole("msg_b", [1, P], a["L2_gnn_msg_b"]),
                     whole("upd_h", [P, P], a["L2_gnn_upd_w"][0:P, :]),
                     whole("upd_b", [1, P], a["L2_gnn_upd_b"]),
                     whole("gate_w", [P, 1], a["L2_gnn_gate_w"]),
                     whole("gate_b", [1, 1], a["L2_gnn_gate_b"])]
            w = load_weights(st, specs)
            h, hT = sb(st, "h", [P, 3, P]), sb(st, "hT", [P, 2, P])
            mean = sb(st, "mean", [P, 4])
            bn = sb(st, "bn2", [P, 4, 6])
            both = sb(st, "both", [P, 2, SKIP])
            silu = sb(st, "silu", [P, 2, 2 * C])
            gated = sb(st, "gated", [P, 2, 3 * C])
            rowbuf = sb(st, "rowbuf", [P, 3, 2, P])
            keep = sb(st, "keep", [P, 3, P])
            gatec = sb(st, "gatec", [P, 2, 2])
            pT, p_sum = ps(st, "pT", [P, 2, P]), ps(st, "p_sum", [P, 2, 512])
            p_skip = ps(st, "p_skip", [P, 2, 1024])
            pm, pg = p_skip, ps(st, "pg", [P, 2, 2])
            s = Stage(straight)
            s.steps[("x", "norm")] = (straight["vector"], straight["vector"].value)
            agg_scale = 0.5 * (2 * C) ** -0.5 * DEG ** -0.5
            for n in ("down_a", "down_b"):
                s.do("vector", "scaled", lambda e, n=n: e.tensor_scalar(w[n][:, :], w[n][:, :], agg_scale, None, ALU.mult))
            s.do("vector", "scaled", lambda e: e.tensor_scalar(w["skip"][:, :, :], w["skip"][:, :, :], 0.5 * C ** -0.5, None, ALU.mult))
            for n, (name, r) in enumerate((("msg_src", P), ("msg_dst", P), ("msg_b", 1))):
                s.do("vector", ("m", n), lambda e, n=n, name=name, r=r: e.tensor_reduce(
                    mean[0:r, n:n + 1], w[name][0:r, :], AX, ALU.add))
                s.do("vector", ("m1", n), lambda e, n=n, r=r: e.tensor_scalar(
                    mean[0:r, n:n + 1], mean[0:r, n:n + 1], 1.0 / P, None, ALU.mult), ("m", n))
                s.do("vector", "scaled", lambda e, n=n, name=name, r=r: e.tensor_scalar(
                    w[name][0:r, :], w[name][0:r, :], mean[0:r, n:n + 1], None, ALU.subtract), ("m1", n))
            PER = 3
            for i in range(NT):
                nodes = slice(i * P, (i + 1) * P)
                normed(s, h, pT, hT, i, by_component=True)
                s.do("tensor", None, lambda e, i=i, nodes=nodes: e.matmul(
                    p_sum[:, i % 2, 0:SKIP], acc[:, 0, nodes], w["down_a"][:, :], start=True, stop=False),
                    "scaled", ring("both", i, 2))
                s.do("tensor", ("down", i), lambda e, i=i, nodes=nodes: e.matmul(
                    p_sum[:, i % 2, 0:SKIP], acc[:, 1, nodes], w["down_b"][:, :], start=False, stop=True))
                s.wait("tensor", ("hT", i))
                for q0 in (0, PER):
                    q1 = min(q0 + PER, SPECIES)
                    s.do("tensor", ("hT_used", i), lambda e, i=i, q0=q0, q1=q1: e.matmul(
                        p_skip[:, i % 2, 512 * (q0 // PER):512 * (q0 // PER) + (q1 - q0) * SKIP],
                        hT[:, i % 2, :], w["skip"][:, q0:q1, :].rearrange("p q f -> p (q f)"), start=True, stop=True))
                s.do("scalar", ("both0", i), lambda e, i=i: e.activation(
                    both[:, i % 2, :], p_sum[:, i % 2, 0:SKIP], ACT.Copy), ("down", i), ring("x2", i, 2))
                for q in range(SPECIES):
                    off = 512 * (q // PER) + (q % PER) * SKIP
                    s.do("vector", ("both", i) if q == SPECIES - 1 else ("skip", i, q),
                         lambda e, i=i, q=q, off=off: e.scalar_tensor_tensor(
                             out=both[:, i % 2, :], in0=p_skip[:, i % 2, off:off + SKIP],
                             scalar=species[:, i, q:q + 1], in1=both[:, i % 2, :], op0=ALU.mult, op1=ALU.add),
                         ("hT_used", i), ("both0", i) if q == 0 else ("skip", i, q - 1))
                s.do("scalar", ("silu", i), lambda e, i=i: e.activation(
                    silu[:, i % 2, :], both[:, i % 2, 0:2 * C], ACT.Silu), ("both", i))
                s.do("vector", ("gated", i), lambda e, i=i: e.tensor_tensor(
                    gated[:, i % 2, :].rearrange("p (k c) -> p k c", k=3),
                    both[:, i % 2, 2 * C:].rearrange("p (k c) -> p k c", k=3),
                    silu[:, i % 2, C:2 * C].unsqueeze(1).to_broadcast([P, 3, C]), ALU.mult), ("silu", i))
                s.do("vector", ("x2s", i), lambda e, i=i: e.tensor_tensor(
                    x[:, i, 0:C], x[:, i, 0:C], silu[:, i % 2, 0:C], ALU.add), ("h", i))
                s.do("vector", ("x2", i), lambda e, i=i: e.tensor_tensor(
                    vectors_last(x[:, i, C:P]), vectors_last(x[:, i, C:P]),
                    gated[:, i % 2, :].rearrange("p (k c) -> p k c", k=3), ALU.add), ("gated", i), ("x2s", i))
                statistics(s, bn, i, x[:, i, :], ("x2", i))
            s.wait("gpsimd", ("down", NT - 1))
            clear_accumulator(s, 1, "cleared")
            s.dma("sync", "tail", "load0", lambda e: e.dma_start(window_table[NT * P:ACC, :], zero[:, :]))
            s.straight(nc)

            s = Stage(straight)
            s.steps["scaled"] = (straight["vector"], straight["vector"].value)
            rms_inverse(s, "x", "scaled")
            for i in range(NT):
                normed(s, h, pT, hT, i, user="h_used")
                s.wait("tensor", ("hT", i), ring("row", i, 2), ring("term", i, 2))
                for off, name in ((0, "msg_src"), (P, "msg_dst"), (512, "upd_h")):
                    bias = {"msg_dst": "msg_b", "upd_h": "upd_b"}.get(name)
                    s.do("tensor", ("wide", i), lambda e, i=i, n=off, name=name, b=bias: e.matmul(
                        pm[:, i % 2, n:n + P], hT[:, i % 2, :], w[name][:, :], start=True, stop=b is None))
                    if bias:
                        s.do("tensor", ("wide", i), lambda e, i=i, n=off, b=bias: e.matmul(
                            pm[:, i % 2, n:n + P], ones[0:1, :], w[b][0:1, :], start=False, stop=True))
                s.do("tensor", None, lambda e, i=i: e.matmul(
                    pg[:, i % 2, 0:1], hT[:, i % 2, :], w["gate_w"][:, :], start=True, stop=False), ring("gate", i, 2))
                s.do("tensor", ("hT_used", i), lambda e, i=i: e.matmul(
                    pg[:, i % 2, 0:1], ones[0:1, :], w["gate_b"][0:1, :], start=False, stop=True))
                s.do("scalar", ("gate", i), lambda e, i=i: e.activation(
                    gate[:, i:i + 1], pg[:, i % 2, 0:1], ACT.Sigmoid), ("hT_used", i))
                s.do("scalar", ("term", i), lambda e, i=i: e.activation(
                    local_term[:, i, :], pm[:, i % 2, 512:512 + P], ACT.Copy), ("wide", i))
                s.do("vector", ("row", i), lambda e, i=i: e.tensor_copy(
                    rowbuf[:, i % 3, :, :].rearrange("p n f -> p (n f)"), pm[:, i % 2, 0:2 * P]), ("wide", i),
                    ring("src_out", i, 3), ring("dst_out", i, 3))
                store(s, ("src_out", i), lambda e, i=i: e.dma_start(
                    table[i * P:i * P + rows(i), :], rowbuf[0:rows(i), i % 3, 0, :]), ("row", i))
                store(s, ("dst_out", i), lambda e, i=i: e.dma_start(
                    window_table[i * P:(i + 1) * P, :], rowbuf[:, i % 3, 1, :]), ("row", i))
                s.do("vector", ("gate1", i), lambda e, i=i: e.tensor_scalar(
                    gatec[:, i % 2, 0:1], gate[:, i:i + 1], -1.0, 1.0, ALU.mult, ALU.add), ("gate", i))
                s.do("vector", ("h_used", i), lambda e, i=i: e.scalar_tensor_tensor(
                    out=x[:, i, :], in0=h[:, i % 3, :], scalar=gatec[:, i % 2, 0:1], in1=x[:, i, :],
                    op0=ALU.mult, op1=ALU.add), ("gate1", i))
            s.wait("sync", *[(n, i) for i in range(max(0, NT - 4), NT) for n in ("src_out", "dst_out")])
            s.wait("vector", ("h_used", NT - 1))
            s.straight(nc)

        with ExitStack() as st:
            w = load_weights(st, [whole("msg_g", [P, P], a["L2_gnn_msg_g"].partition_broadcast(P)),
                                  whole("msg_beta", [P, P], a["L2_gnn_msg_beta"].partition_broadcast(P))])
            local = sb(st, "local_2", [P, TURN_BATCHES, BATCH_TILES])
            weight = sb(st, "weight_2", [P, TURN_BATCHES, BATCH_TILES])
            sel = sb(st, "sel_2", [P, 4, GROUP, WINDOW])
            near_rows = sb(st, "near_rows", [WINDOW, 4, P])
            near_dst = sb(st, "near_dst", [WINDOW, 4, GROUP_EDGES])
            spread = sb(st, "spread", [WINDOW, 2, GROUP_EDGES])
            z = sb(st, "z", [P, 3, GROUP, P])
            sq = sb(st, "sq", [P, 4, GROUP])
            eps = sb(st, "eps", [P, 1])
            y = sb(st, "y", [P, 3, GROUP, P])
            p_near = ps(st, "p_near", [P, 2, GROUP, P])
            sums = ps(st, "sums_2", [P, 4, 512])
            s = Stage(straight)
            s.do("vector", "eps", lambda e: e.memset(eps[:, :], EPS))
            s.wait("vector", "eps")
            s.straight(nc)

            def near(s, g):
                b, at = place(g)

                def load(e, it):
                    at = e.value_load(address[0:1, bass.ds(it * TURN_GROUPS + g, 1)], min_val=0, max_val=N)
                    return e.dma_start(near_rows[:, g % 4, :], window_table[bass.ds(at, WINDOW), :])
                s.wait("sync", ring("spread_out", g, 4, TURN_GROUPS))
                s.dma("sync", ("near", g), f"near{g % 4}", load)
                s.dma("sync", ("near", g), f"near{g % 4}", lambda e, it: e.dma_start(
                    near_dst[:, g % 4, :], local_rows[bass.ds(it * TURN_BATCHES + b, 1), at * P:at * P + GROUP_EDGES]
                    .to_broadcast([WINDOW, GROUP_EDGES])))

            def body(s, gathered):
                def spread_near(g):
                    s.do("vector", ("spread", g), lambda e, it: e.tensor_scalar(
                        spread[:, g % 2, :], near_dst[:, g % 4, :], iota_col_pass[0:WINDOW, :], None, ALU.is_equal),
                        ("near", g), ring("spread_out", g, 2, TURN_GROUPS))
                    s.wait("tensor", ("spread", g), ring("z", g, 2, TURN_GROUPS))
                    for t in range(GROUP):
                        s.do("tensor", ("spread_out", g), lambda e, it, t=t: e.matmul(
                            p_near[:, g % 2, t, :], spread[:, g % 2, t * P:(t + 1) * P], near_rows[:, g % 4, :],
                            start=True, stop=True))

                def combine(g):
                    s.do("vector", ("z", g), lambda e, it: e.tensor_tensor(
                        z[:, g % 3, :, :], gathered[:, g % SLOTS, :, :], p_near[:, g % 2, :, :], ALU.add),
                        ("spread_out", g), ("gathered", g), ring("scaled", g, 3, TURN_GROUPS))
                    s.steps[("rows_used", g)] = s.steps[("z", g)]
                    s.wait("scalar", ("z", g), ring("summed", g, 3, TURN_GROUPS))
                    for t in range(GROUP):
                        s.do("scalar", ("sq", g), lambda e, it, t=t: e.activation(
                            y[:, g % 3, t, :], z[:, g % 3, t, :], ACT.Square, accum_out=sq[:, g % 4, t:t + 1]))
                    s.do("scalar", ("std", g), lambda e, it: e.activation(
                        sq[:, g % 4, :], sq[:, g % 4, :], ACT.Sqrt, scale=1.0 / P, bias=eps[:, 0:1]), ("sq", g))

                def normalise(g):
                    s.do("vector", ("rstd", g), lambda e, it: e.reciprocal(
                        sq[:, g % 4, :], sq[:, g % 4, :]), ("std", g))
                    s.wait("vector", ("rstd", g))
                    for t in range(GROUP):
                        s.do("vector", ("scaled", g), lambda e, it, t=t: e.scalar_tensor_tensor(
                            out=y[:, g % 3, t, :], in0=z[:, g % 3, t, :], scalar=sq[:, g % 4, t:t + 1],
                            in1=w["msg_g"][:, :], op0=ALU.mult, op1=ALU.mult))
                    s.do("vector", ("shifted", g), lambda e, it: e.tensor_tensor(
                        y[:, g % 3, :, :], y[:, g % 3, :, :],
                        w["msg_beta"][:, :].unsqueeze(1).to_broadcast([P, GROUP, P]), ALU.add), ("scaled", g))
                    s.do("scalar", ("relu", g), lambda e, it: e.activation(
                        y[:, g % 3, :, :], y[:, g % 3, :, :], ACT.Relu), ("shifted", g))

                def multiply(g):
                    s.wait("tensor", ("relu", g), ("selected", g), ring("added", g, 4, TURN_GROUPS))
                    for t in range(GROUP):
                        s.do("tensor", ("summed", g), lambda e, it, t=t: e.matmul(
                            sums[:, g % 4, 0:WINDOW], y[:, g % 3, t, :], sel[:, g % 4, t, :],
                            start=t == 0, stop=t == GROUP - 1))
                    s.steps[("edges_used", g)] = s.steps[("summed", g)]

                staggered((0, spread_near), (0, lambda g: select(s, sel, local, weight, g)),
                          (2, normalise), (2, multiply), (0, combine),
                          (3, lambda g: accumulate(s, sums[:, g % 4, 0:WINDOW].unsqueeze(1), g)))

            message_stage("messages2", body, table, a["src_cols"], [
                (local, column(local_cols)), (weight, column(a["weight_cols"]))], st, near=near)

        with ExitStack() as st:
            w = load_weights(st, [
                whole("upd_m", [P, P], a["L2_gnn_upd_w"][P:2 * P, :]),
                whole("upd_g", [P, P], a["L2_gnn_upd_g"].partition_broadcast(P)),
                whole("upd_beta", [P, P], a["L2_gnn_upd_beta"].partition_broadcast(P)),
                whole("rel", [P, REL, P], a["L3_gnn_w_rel"][0].rearrange("r d e -> d r e")),
                whole("root", [P, P], a["L3_gnn_w_root"][0]),
                whole("skip0", [P, P], a["L3_gnn_w_skip"][0]),
                whole("skip1", [P, P], a["L3_gnn_w_skip"][1]),
                whole("b_col", [P, 2], a["L3_b_cols"]),
                whole("b_conv1", [1, P], a["L3_gnn_b_conv"][1:2, :]),
                whole("b_skip1", [1, P], a["L3_gnn_b_skip"][1:2, :])])
            h, hT = sb(st, "h", [P, 3, P]), sb(st, "hT", [P, 2, P])
            bn = sb(st, "bn3", [P, 4, 6])
            u = sb(st, "u", [P, 3, P])
            rowbuf = sb(st, "rowbuf", [P, 3, REL, P])
            pT, pm = ps(st, "pT", [P, 2, P]), ps(st, "pm", [P, 2, 512])
            pl, px = ps(st, "pl", [P, 2, 512]), ps(st, "px", [P, 2, 512])
            s = Stage(straight)
            for i in range(NT):
                nodes = slice(i * P, (i + 1) * P)
                s.do("tensor", ("upd", i), lambda e, i=i, nodes=nodes: e.matmul(
                    pm[:, i % 2, 0:P], acc[:, 0, nodes], w["upd_m"][:, :], start=True, stop=True), ring("z", i, 2))
                s.do("vector", ("z", i), lambda e, i=i: e.scalar_tensor_tensor(
                    out=local_term[:, i, :], in0=pm[:, i % 2, 0:P], scalar=rcount[:, i:i + 1],
                    in1=local_term[:, i, :], op0=ALU.mult, op1=ALU.add), ("upd", i))
                statistics(s, bn, i, local_term[:, i, :], ("z", i), "z")
            rms_inverse(s, "z", ("z", "stat", NT - 1))
            for i in range(NT):
                s.do("scalar", ("u", i), lambda e, i=i: e.activation(
                    u[:, i % 3, :], local_term[:, i, :], ACT.Identity, bias=shift[:, i:i + 1],
                    scale=rstd[:, i:i + 1]), ("z", "norm"), ring("x3", i, 3))
                s.do("vector", ("ug", i), lambda e, i=i: e.tensor_tensor(
                    u[:, i % 3, :], u[:, i % 3, :], w["upd_g"][:, :], ALU.mult), ("u", i))
                s.do("vector", ("ub", i), lambda e, i=i: e.tensor_tensor(
                    u[:, i % 3, :], u[:, i % 3, :], w["upd_beta"][:, :], ALU.add), ("ug", i))
                s.do("vector", ("ur", i), lambda e, i=i: e.tensor_scalar(
                    u[:, i % 3, :], u[:, i % 3, :], 0.0, gate[:, i:i + 1], ALU.max, ALU.mult), ("ub", i))
                s.do("vector", ("x3", i), lambda e, i=i: e.tensor_tensor(
                    x[:, i, :], x[:, i, :], u[:, i % 3, :], ALU.add), ("ur", i))
                statistics(s, bn, i, x[:, i, :], ("x3", i), "x")
            s.steps["u_done"] = s.steps[("u", NT - 1)]
            s.wait("vector", "u_done")
            rms_inverse(s, "x", ("x", "stat", NT - 1))
            s.do("vector", "root_sum", lambda e: e.tensor_tensor(w["root"][:, :], w["root"][:, :], w["skip0"][:, :], ALU.add))
            s.do("vector", "b_sum", lambda e: e.tensor_tensor(w["b_col"][:, 0:1], w["b_col"][:, 0:1], w["b_col"][:, 1:2], ALU.add))
            s.do("gpsimd", "acc_tail", lambda e: e.memset(acc[:, 0, NT * P:ACC], 0.0), ("upd", NT - 1))

            def relation_tables(i, lhs, after):
                s.wait("tensor", after, ring("rel_row", i, 2) or s_first)
                for r in range(REL):
                    s.do("tensor", ("rel", i), lambda e, i=i, r=r: e.matmul(
                        pm[:, i % 2, r * P:(r + 1) * P], lhs, w["rel"][:, r, :], start=True, stop=True))
                s.do("vector", ("rel_row", i), lambda e, i=i: e.tensor_copy(
                    rowbuf[:, i % 3, :, :].rearrange("p r f -> p (r f)"), pm[:, i % 2, 0:REL * P]), ("rel", i),
                    *[ring(("rel_out", r), i, 3) for r in range(REL)])
                for r in range(REL):
                    store(s, (("rel_out", r), i), lambda e, i=i, r=r: e.dma_start(
                        rel_table[r * N + i * P:r * N + i * P + rows(i), :], rowbuf[0:rows(i), i % 3, r, :]), ("rel_row", i))

            s_first = ("z", NT - 1)
            for i in range(NT):
                nodes = slice(i * P, (i + 1) * P)
                normed(s, h, pT, hT, i)
                relation_tables(i, hT[:, i % 2, :], ("hT", i))
                s.do("tensor", ("local", i), lambda e, i=i: e.matmul(
                    pl[:, i % 2, 0:P], w["root"][:, :], hT[:, i % 2, :], start=True, stop=True),
                    "root_sum", ring("acc", i, 2))
                s.do("scalar", ("acc", i), lambda e, i=i, nodes=nodes: e.activation(
                    acc[:, 0, nodes], pl[:, i % 2, 0:P], ACT.Identity, bias=w["b_col"][:, 0:1]), ("local", i), "b_sum")
                s.do("tensor", None, lambda e, i=i: e.matmul(
                    px[:, i % 2, 0:P], hT[:, i % 2, :], w["skip1"][:, :], start=True, stop=False), ring("x4", i, 2))
                for b in ("b_conv1", "b_skip1"):
                    s.do("tensor", ("hT_used", i), lambda e, i=i, b=b: e.matmul(
                        px[:, i % 2, 0:P], ones[0:1, :], w[b][0:1, :], start=False, stop=b == "b_skip1"))
                s.do("vector", ("x4", i), lambda e, i=i: e.tensor_tensor(
                    x[:, i, :], x[:, i, :], px[:, i % 2, 0:P], ALU.add), ("hT_used", i), ("h", i))
            s.wait("sync", *[(("rel_out", r), i) for i in range(max(0, NT - 4), NT) for r in range(REL)])
            s.wait("gpsimd", "acc_tail")
            s.straight(nc)

        plain_messages("conv0", rel_table, rel_cols, a["weight_cols"])

        with ExitStack() as st:
            w = load_weights(st, [
                whole("rel", [P, REL, P], a["L3_gnn_w_rel"][1].rearrange("r d e -> d r e")),
                whole("root1", [P, P], a["L3_gnn_w_root"][1])])
            rowbuf = sb(st, "rowbuf", [P, 3, REL, P])
            pm, px = ps(st, "pm", [P, 2, 512]), ps(st, "px", [P, 2, 512])
            s = Stage(straight)
            s_first = None
            for i in range(NT):
                nodes = slice(i * P, (i + 1) * P)
                relation_tables(i, acc[:, 0, nodes], None)
                s.do("tensor", ("root", i), lambda e, i=i, nodes=nodes: e.matmul(
                    px[:, i % 2, 0:P], acc[:, 0, nodes], w["root1"][:, :], start=True, stop=True), ring("x5", i, 2))
                s.do("vector", ("x5", i), lambda e, i=i: e.tensor_tensor(
                    x[:, i, :], x[:, i, :], px[:, i % 2, 0:P], ALU.add), ("root", i))
                s.wait("gpsimd", ("root", i))
                s.do("gpsimd", "cleared", lambda e, nodes=nodes: e.memset(acc[:, 0, nodes], 0.0))
            s.do("gpsimd", "cleared", lambda e: e.memset(acc[:, 0, NT * P:ACC], 0.0))
            s.wait("sync", *[(("rel_out", r), i) for i in range(max(0, NT - 4), NT) for r in range(REL)])
            s.wait("gpsimd", "cleared")
            s.straight(nc)

        plain_messages("conv1", rel_table, rel_cols, a["weight_cols"])

        with ExitStack() as st:
            pm = ps(st, "pm", [P, 4, 512])
            s = Stage(straight)
            for i in range(NT):
                s.do("tensor", ("agg", i), lambda e, i=i: e.transpose(
                    pm[:, i % 4, 0:P], acc[:, 0, i * P:(i + 1) * P], ident[:, :]), ring("x6", i, 4))
                s.do("vector", ("x6", i), lambda e, i=i: e.tensor_tensor(
                    x[:, i, :], x[:, i, :], pm[:, i % 4, 0:P], ALU.add), ("agg", i))
                store(s, ("out", i), lambda e, i=i: e.dma_start(
                    out[i * P:i * P + rows(i), :], x[0:rows(i), i, :]), ("x6", i))
            s.wait("sync", *[("out", i) for i in range(NT)])
            s.straight(nc)


def kernel(**inputs):
    import concourse.bacc as bacc
    from concourse.bass_utils import run_bass_kernel_spmd

    v = {k: np.asarray(q) for k, q in inputs.items()}
    N, E = v["x"].shape[0], v["src"].shape[0]
    turns = -(-E // TURN_EDGES)
    pad = turns * TURN_EDGES - E
    nt = -(-N // P)

    def edges(q, fill=0):
        return np.concatenate([q, np.full((pad,) + q.shape[1:], fill, q.dtype)])

    def cols(q):
        return np.ascontiguousarray(q.reshape((-1, P) + q.shape[1:]).swapaxes(0, 1).reshape(P, -1))

    arrays = {
        "x": v["x"],
        "src_cols": cols(edges(v["src"])),
        "dst_cols": cols(edges(v["dst"], -1)),
        "dst_rows": edges(v["dst"], -1).reshape(-1, BATCH_EDGES),
        "type_cols": cols(edges(v["edge_type_3"])),
        "weight_cols": cols(edges(v["edge_weight"])),
        "sh_cols": cols(edges(v["edge_attr_4"])),
        "radial_cols": np.ascontiguousarray(
            edges(v["edge_attr_8"]).reshape(-1, BATCH_TILES, P, R).transpose(1, 3, 0, 2).reshape(P, -1)),
        "node_type": np.ascontiguousarray(np.concatenate(
            [v["node_type_5"], np.zeros(nt * P - N, v["node_type_5"].dtype)]).reshape(nt, P).T),
        "L0_rel_t": np.ascontiguousarray(v["L0_gnn_W_rel"].T),
        "L0_root_t": np.ascontiguousarray(v["L0_gnn_W_root"].T),
        "L3_b_cols": np.ascontiguousarray(np.stack([v["L3_gnn_b_conv"][0], v["L3_gnn_b_skip"][0]], 1)),
    }
    for n in ("L0_gnn_b_rel", "L2_gnn_msg_b", "L2_gnn_upd_b", "L2_gnn_gate_b"):
        arrays[n] = v[n].reshape(1, -1)
    for n in ("L1_gnn_W_up_s", "L1_gnn_W_up_v", "L1_gnn_W_r1", "L1_gnn_W_r2", "L1_gnn_W_down_s",
              "L1_gnn_W_down_v", "L1_gnn_W_skip_s", "L1_gnn_W_skip_v", "L2_gnn_msg_w", "L2_gnn_msg_g",
              "L2_gnn_msg_beta", "L2_gnn_upd_w", "L2_gnn_upd_g", "L2_gnn_upd_beta", "L2_gnn_gate_w",
              "L3_gnn_w_rel", "L3_gnn_w_root", "L3_gnn_w_skip", "L3_gnn_b_conv", "L3_gnn_b_skip"):
        arrays[n] = v[n]

    nc = bacc.Bacc("TRN2", target_bir_lowering=False, num_devices=1)
    aps, feed = {}, {}
    for n, q in arrays.items():
        feed["in_" + n] = q
        aps[n] = nc.dram_tensor("in_" + n, q.shape, mybir.dt.from_np(q.dtype), kind="ExternalInput").ap()
    result = nc.dram_tensor("out", (N, P), F32, kind="ExternalOutput").ap()
    build(nc, aps, result, (N, E))
    r = run_bass_kernel_spmd(nc, [feed], core_ids=[0])
    return r.results[0]["out"]
```

```python
from contextlib import ExitStack

import numpy as np

import concourse.bass as bass
from concourse import mybir

P = 128
GROUP = 4
BATCH_GROUPS = 4
SLOTS = 8
TURN_BATCHES = 4
TURN_GROUPS = TURN_BATCHES * BATCH_GROUPS
BATCH_TILES = BATCH_GROUPS * GROUP
TURN_TILES = TURN_GROUPS * GROUP
WINDOW = 48
GROUP_EDGES = GROUP * P
BATCH_EDGES = BATCH_TILES * P
TURN_EDGES = TURN_TILES * P
FAR = float(1 << 21)
EPS = 1e-5

C = 32
R = 8
SPECIES = 5
SKIP = 2 * C + 3 * C
DEG = 16.0
REL = 3

F32 = mybir.dt.float32
I32 = mybir.dt.int32
ALU = mybir.AluOpType
ACT = mybir.ActivationFunctionType
AX = mybir.AxisListType.X


class Counter:

    def __init__(self, sem, credit=False):
        self.sem = sem
        self.value = 0
        self.credit = credit


class Prev:

    def __init__(self, key):
        self.key = key


def ring(name, i, size, turn=None):
    name = name if isinstance(name, tuple) else (name,)
    if i >= size:
        return (*name, i - size)
    return Prev((*name, i - size + turn)) if turn else None


class Stage:

    def __init__(self, counters, ticks=None):
        self.counters = counters
        self.ticks = ticks or {}
        self.queues = {name: [] for name in ("sync", "scalar", "vector", "gpsimd", "tensor")}
        self.steps = {}

    def wait(self, engine, *keys):
        for key in keys:
            if key is not None:
                self.queues[engine].append(("wait", key))

    def do(self, engine, key, fn, *after, by=1, counter=None):
        self.wait(engine, *after)
        c = self.counters[counter or engine]
        c.value += by
        self.queues[engine].append(("do", fn, c, by))
        if key is not None:
            self.steps[key] = (c, c.value)

    def dma(self, engine, key, counter, fn, *after):
        self.do(engine, key, fn, *after, by=16, counter=counter)

    def straight(self, nc):
        with nc.Block() as block:
            for name, queue in self.queues.items():
                if queue:
                    getter = {"sync": block.sync, "scalar": block.scalar, "vector": block.vector,
                              "gpsimd": block.gpsimd, "tensor": block.tensor}[name]

                    @getter
                    def _(e, queue=queue):
                        seen = {}
                        for item in queue:
                            if item[0] == "wait":
                                c, value = self.steps[item[1]]
                                if seen.get(c, 0) < value:
                                    e.wait_ge(c.sem, value)
                                    seen[c] = value
                            else:
                                _, fn, c, by = item
                                fn(e).then_inc(c.sem, by)

    def turn(self, e, engine, it):
        seen, pending = {}, {}
        for item in self.queues[engine]:
            if item[0] == "wait":
                prev = isinstance(item[1], Prev)
                c, value = self.steps[item[1].key if prev else item[1]]
                assert c.credit or not prev
                at = value + c.value if c.credit and not prev else value
                if seen.get(c, 0) < at:
                    seen[c] = pending[c] = at
                continue
            values = [(c.sem, e.snap(it * c.value + at)) for c, at in pending.items()]
            for sem, value in values:
                e.wait_ge(sem, value)
            if pending and engine in self.ticks:
                e.sem_inc(self.ticks[engine], 1)
            pending = {}
            _, fn, c, by = item
            fn(e, it).then_inc(c.sem, by)


def build(nc, a, out, shapes):
    N, E = shapes
    NT = -(-N // P)
    REST = N - (NT - 1) * P
    TURNS = -(-E // TURN_EDGES)
    BATCHES = TURN_BATCHES * TURNS
    GROUPS = TURNS * TURN_GROUPS
    TILES = TURNS * TURN_TILES
    MOST_PASSES = -(-N // WINDOW)
    ACC = (NT + 1) * P

    top = ExitStack()
    with top:
        def dram(name, shape, dt=F32):
            return nc.dram_tensor(name, shape, dt, kind="Internal").ap()

        names = {}

        def own(name):
            names[name] = names.get(name, 0) + 1
            return name if names[name] == 1 else f"{name}_{names[name]}"

        def sb(stack, name, shape, dt=F32):
            return stack.enter_context(nc.sbuf_tensor(own(name), shape, dt))

        def ps(stack, name, shape):
            return stack.enter_context(nc.psum_tensor(own(name), shape, F32))

        table = dram("table", (N, P))
        rel_table = dram("rel_table", (REL * N, P))
        window_table = dram("window_table", (ACC, P))
        base_dram = dram("base_dram", (1, GROUPS))
        span_dram = dram("span_dram", (1, BATCHES))
        local_cols = dram("local_cols", (P, TILES))
        local_rows = dram("local_rows", (BATCHES, BATCH_EDGES))
        rel_cols = dram("rel_cols", (P, TILES), I32)

        x = sb(top, "x", [P, NT, P])
        acc = sb(top, "acc", [P, 2, ACC])
        ident = sb(top, "ident", [P, P])
        ones = sb(top, "ones", [P, P])
        zero = sb(top, "zero", [P, P])
        iota = sb(top, "iota", [P, WINDOW])
        iota_col = sb(top, "iota_col", [P, 1])
        iota_pass = sb(top, "iota_pass", [P, WINDOW])
        iota_col_pass = sb(top, "iota_col_pass", [P, 1])
        base_row = sb(top, "base_row", [1, GROUPS])
        base_pass = sb(top, "base_pass", [1, GROUPS])
        address = sb(top, "address", [1, GROUPS], I32)
        passes = sb(top, "passes", [1, 1], I32)
        rcount = sb(top, "rcount", [P, NT])
        species = sb(top, "species", [P, NT, SPECIES])
        gate = sb(top, "gate", [P, NT])
        stat = sb(top, "stat", [P, NT, 2])
        rstd = sb(top, "rstd", [P, NT])
        shift = sb(top, "shift", [P, NT])

        straight = {n: Counter(top.enter_context(nc.semaphore(f"done_{n}")))
                    for n in ("sync", "scalar", "vector", "gpsimd", "tensor")}
        NLOAD = 12
        for n in [f"load{i}" for i in range(NLOAD)] + [f"store{i}" for i in range(4)]:
            straight[n] = Counter(top.enter_context(nc.semaphore(n)))
        loop_sems = {n: top.enter_context(nc.semaphore(f"turn_{n}"))
                     for n in ["scalar", "vector", "tensor"] + [f"slot{i}" for i in range(SLOTS)]
                     + [f"idx{i}" for i in range(TURN_BATCHES)] + [f"edge{i}" for i in range(TURN_BATCHES)]
                     + [f"near{i}" for i in range(4)]}
        arrived = top.enter_context(nc.semaphore("arrived"))
        ticks = {n: top.enter_context(nc.semaphore(f"waited_{n}")) for n in ("gpsimd", "sync")}

        stores = [0]

        def store(s, key, fn, *after):
            i = stores[0] % 4
            stores[0] += 1
            s.dma("sync", key, f"store{i}", fn, *after, *( [last_store[i]] if last_store.get(i) in s.steps else []))
            last_store[i] = key

        last_store = {}

        def staggered(*steps, count=TURN_GROUPS):
            for k in range(count + max(lag for lag, _ in steps)):
                for lag, step in steps:
                    if 0 <= k - lag < count:
                        step(k - lag)

        CHUNK = 14

        def invert_deviations(s, tag, i):
            if (i + 1) % CHUNK and i != NT - 1:
                return
            t = slice(i // CHUNK * CHUNK, i + 1)
            s.do("vector", (tag, "eps", i), lambda e: e.tensor_scalar(
                rstd[:, t], stat[:, t, 1], EPS, None, ALU.add), (tag, "stat", i))
            s.do("scalar", (tag, "std", i), lambda e: e.activation(
                rstd[:, t], rstd[:, t], ACT.Sqrt), (tag, "eps", i))
            s.do("vector", (tag, "rstd", i), lambda e: e.reciprocal(rstd[:, t], rstd[:, t]), (tag, "std", i))
            s.do("vector", None, lambda e: e.scalar_tensor_tensor(
                out=shift[:, t], in0=stat[:, t, 0], scalar=-1.0, in1=rstd[:, t], op0=ALU.mult,
                op1=ALU.mult), (tag, "rstd", i))
            for k in range(t.start, t.stop):
                s.steps[(tag, "norm", k)] = (straight["vector"], straight["vector"].value)

        def statistics(s, bn, i, src, ready, tag="x"):
            s.do("vector", (tag, "bn", i), lambda e: e.bn_stats(bn[:, i % 4, :], src), ready,
                 ring((tag, "stat"), i, 4))

        def aggregate(s, bn, i, tag="x"):
            s.do("vector", (tag, "stat", i), lambda e: e.bn_aggr(stat[:, i, :], bn[:, i % 4, :]),
                 (tag, "bn", i))
            invert_deviations(s, tag, i)

        def vectors_last(ap):
            return ap.rearrange("p (c k) -> p k c", k=3)

        HR = 5

        def normed(s, h, i, by_component=False, user=None, tag="x"):
            def relu(dst, src):
                return lambda e: e.activation(dst, src, ACT.Relu, bias=shift[:, i:i + 1],
                                              scale=rstd[:, i:i + 1])
            s.wait("scalar", (tag, "norm", i) if (tag, "norm", i) in s.steps else None,
                   ring("h_turned", i, HR), ring(user, i, HR) if user else None)
            if not by_component:
                s.do("scalar", ("h", i), relu(h[:, i % HR, :], x[:, i, :]))
            else:
                s.do("scalar", None, relu(h[:, i % HR, 0:C], x[:, i, 0:C]))
                s.do("scalar", ("h", i), relu(
                    h[:, i % HR, C:P].rearrange("p (k c) -> p k c", k=3),
                    vectors_last(x[:, i, C:P])))

        def turn_h(s, h, pT, i):
            s.do("tensor", ("h_turned", i), lambda e: e.transpose(
                pT[:, i % 2, 0:P], h[:, i % HR, :], ident[:, :]), ("h", i), ring("hT", i, 2))

        def keep_hT(s, pT, hT, i):
            s.do("vector", ("hT", i), lambda e: e.tensor_copy(hT[:, i % 3, :], pT[:, i % 2, 0:P]),
                 ("h_turned", i), ring("hT_used", i, 3))

        def rows(i):
            return REST if i == NT - 1 else P

        def load_weights(st, specs):
            tiles, s = {}, Stage(straight)
            for n, (name, shape, parts) in enumerate(specs):
                tiles[name] = t = sb(st, name, shape)
                if parts[0][2] is not None:
                    s.do("gpsimd", ("zeroed", name), lambda e, t=t: e.memset(t[:], 0.0))
                for m, (dst, src, _) in enumerate(parts):
                    s.dma("sync", ("loaded", name), f"load{n % NLOAD}",
                          lambda e, d=dst, q=src, t=t: e.dma_start(d(t), q),
                          *([("zeroed", name)] if parts[0][2] is not None else []))
            for name, *_ in specs:
                s.wait("sync", ("loaded", name))
            s.straight(nc)
            return tiles

        def whole(name, shape, src):
            return (name, shape, [(lambda t: t[:], src, None)])

        def message_stage(name, body, source, index_cols, extra_cols, st, near=False):
            s = Stage(straight)
            s.do("vector", ("base", name), lambda e: e.tensor_copy(base_pass[:, :], base_row[:, :]))
            s.do("vector", ("address", name), lambda e: e.tensor_scalar(
                address[:, :], base_pass[:, :], float(N), None, ALU.min), ("base", name))
            s.do("vector", None, lambda e: e.tensor_copy(iota_pass[:, :], iota[:, :]))
            s.do("vector", ("reset", name), lambda e: e.tensor_copy(iota_col_pass[:, :], iota_col[:, :]))
            s.wait("vector", ("reset", name))
            s.straight(nc)

            engines = ("scalar", "vector", "tensor")
            counters = {n: Counter(v, n in engines) for n, v in loop_sems.items()}
            s = Stage(counters, ticks)
            gathered = sb(st, "gathered_" + name, [P, SLOTS, GROUP, P])
            index = sb(st, "index_" + name, [P, TURN_BATCHES, BATCH_TILES], I32)

            def stage_edges(b):
                groups = range(b * BATCH_GROUPS, (b + 1) * BATCH_GROUPS)
                s.dma("sync", ("index", b), f"idx{b}", lambda e, it: e.dma_start(
                    index[:, b, :], index_cols[:, bass.ds(it * TURN_TILES + b * BATCH_TILES, BATCH_TILES)]),
                    *[Prev(("rows_used", g)) for g in groups])
                s.wait("sync", *[Prev(("edges_used", g)) for g in groups])
                for tile, src in extra_cols:
                    s.dma("sync", ("edges", b), f"edge{b}",
                          lambda e, it, tile=tile, src=src: e.dma_start(tile[:, b], src(it, b)))

            def gather(g):
                b, k = g // BATCH_GROUPS, g % BATCH_GROUPS
                s.wait("gpsimd", ("index", b), ring("rows_used", g, SLOTS, TURN_GROUPS))
                for t in range(GROUP):
                    s.dma("gpsimd", ("gathered", g), f"slot{g % SLOTS}", lambda e, it, t=t: e.indirect_dma_start(
                        gathered[:, g % SLOTS, t, :], None, source[:, :], bass.IndirectOffsetOnAxis(
                            ap=index[:, b, k * GROUP + t:k * GROUP + t + 1], axis=0)))

            for b in range(TURN_BATCHES + 1):
                if b < TURN_BATCHES:
                    stage_edges(b)
                if near and b:
                    for g in range((b - 1) * BATCH_GROUPS, b * BATCH_GROUPS):
                        near(s, g)
            for g in range(TURN_GROUPS):
                gather(g)
            body(s, gathered)
            used = [n for n, c in counters.items() if c.value]

            go = top.enter_context(nc.semaphore("go_" + name))
            with nc.Block() as block:
                getters = {"sync": block.sync, "scalar": block.scalar, "vector": block.vector,
                           "gpsimd": block.gpsimd, "tensor": block.tensor}
                for engine in getters:
                    @getters[engine]
                    def _(e, engine=engine):
                        count = e.value_load(passes[0:1, 0:1], min_val=1, max_val=MOST_PASSES)
                        with e.Fori(0, count) as turn_of_pass:
                            if engine in engines and counters[engine].value:
                                e.sem_inc(counters[engine].sem, counters[engine].value)
                            with e.Fori(0, TURNS) as it:
                                s.turn(e, engine, it)
                            if engine in engines and counters[engine].value:
                                e.wait_ge(counters[engine].sem, counters[engine].value * (TURNS + 1))
                            if engine == "vector":
                                e.tensor_scalar(iota_pass[:, :], iota_pass[:, :], float(WINDOW), None, ALU.add).then_inc(counters["vector"].sem, 1)
                                e.tensor_scalar(iota_col_pass[:, :], iota_col_pass[:, :], float(WINDOW), None, ALU.add).then_inc(counters["vector"].sem, 1)
                                e.tensor_scalar(base_pass[:, :], base_pass[:, :], float(WINDOW), None, ALU.add).then_inc(counters["vector"].sem, 1)
                                at = counters["vector"].value * (TURNS + 1)
                                e.wait_ge(counters["vector"].sem, at + 3)
                                e.tensor_scalar(address[:, :], base_pass[:, :], float(N), None, ALU.min).then_inc(counters["vector"].sem, 1)
                                e.wait_ge(counters["vector"].sem, at + 4)
                            if engine == "gpsimd":
                                slots = [loop_sems[f"slot{k}"] for k in range(SLOTS)]
                                for slot in slots:
                                    e.wait_ge(slot, 16 * GROUP * (TURN_GROUPS // SLOTS) * TURNS)
                                e.dma_reset(range(slots[0].num, slots[-1].num + 1))
                            if engine != "sync":
                                e.sem_inc(arrived, 1)
                                e.wait_ge(go, turn_of_pass + 1)
                            else:
                                e.wait_ge(arrived, 4)
                                for n in used:
                                    e.sem_clear(counters[n].sem)
                                e.sem_clear(arrived)
                                for tick in ticks.values():
                                    e.sem_clear(tick)
                                e.sem_inc(go, 1)

        def column(src):
            return lambda it, b: src[:, bass.ds(it * TURN_TILES + b * BATCH_TILES, BATCH_TILES)]

        def place(g):
            return g // BATCH_GROUPS, (g % BATCH_GROUPS) * GROUP

        def select(s, sel, local, g):
            b, at = place(g)
            s.do("vector", ("hit", g), lambda e, it: e.tensor_tensor(
                sel[:, g % 4, :, :], iota_pass[:, :].unsqueeze(1).to_broadcast([P, GROUP, WINDOW]),
                local[:, b, at:at + GROUP].unsqueeze(2).to_broadcast([P, GROUP, WINDOW]), ALU.is_equal),
                ("edges", b), ring("summed", g, 4, TURN_GROUPS))

        def weigh(s, sel, weight, g):
            b, at = place(g)
            s.do("vector", ("weighed", g), lambda e, it: e.tensor_tensor(
                sel[:, g % 4, :, :], sel[:, g % 4, :, :],
                weight[:, b, at:at + GROUP].unsqueeze(2).to_broadcast([P, GROUP, WINDOW]), ALU.mult),
                ("hit", g))

        def accumulate(s, psum, g, n=1):
            def add(e, it):
                at = e.value_load(address[0:1, bass.ds(it * TURN_GROUPS + g, 1)], min_val=0, max_val=N)
                sums = acc[:, 0:n, bass.ds(at, WINDOW)]
                return e.tensor_tensor(sums, sums, psum, ALU.add)
            s.do("vector", ("added", g), add, ("summed", g), ring("added", g, 1, TURN_GROUPS))


        def plain_messages(name, source, index_cols, weight_cols=None, counts=False):
            with ExitStack() as st:
                local = sb(st, "local_" + name, [P, TURN_BATCHES, BATCH_TILES])
                weight = sb(st, "weight_" + name, [P, TURN_BATCHES, BATCH_TILES]) if weight_cols is not None else None
                sel = sb(st, "select_" + name, [P, 4, GROUP, WINDOW])
                sums = ps(st, "sums_" + name, [P, 4, 512])
                extra = [(local, column(local_cols))]
                if weight is not None:
                    extra.append((weight, column(weight_cols)))
                n = 2 if counts else 1

                def body(s, gathered):
                    def multiply(g):
                        s.wait("tensor", ("gathered", g), ("hit", g) if weight is None else ("weighed", g),
                               ring("added", g, 4, TURN_GROUPS))
                        for t in range(GROUP):
                            s.do("tensor", ("summed", g), lambda e, it, t=t: e.matmul(
                                sums[:, g % 4, 0:WINDOW], gathered[:, g % SLOTS, t, :], sel[:, g % 4, t, :],
                                start=t == 0, stop=t == GROUP - 1))
                        s.steps[("rows_used", g)] = s.steps[("summed", g)]
                        if counts:
                            for t in range(GROUP):
                                s.do("tensor", ("summed", g), lambda e, it, t=t: e.matmul(
                                    sums[:, g % 4, WINDOW:2 * WINDOW], ones[:, :], sel[:, g % 4, t, :],
                                    start=t == 0, stop=t == GROUP - 1))
                        s.steps[("edges_used", g)] = s.steps[("summed", g)]

                    steps = [(0, lambda g: select(s, sel, local, g))]
                    if weight is not None:
                        steps.append((1, lambda g: weigh(s, sel, weight, g)))
                    staggered(*steps, (1, multiply),
                              (3, lambda g: accumulate(s, sums[:, g % 4, 0:n * WINDOW].rearrange(
                                  "p (n w) -> p n w", n=n), g, n)))

                message_stage(name, body, source, index_cols, extra, st)

        def clear_accumulator(s, n, key):
            for k in range(n):
                s.do("gpsimd", key, lambda e, k=k: e.memset(acc[:, k, :], 0.0))

        with ExitStack() as st:
            dst_i = sb(st, "dst_i", [BATCHES, BATCH_EDGES], I32)
            dst_f = sb(st, "dst_f", [BATCHES, BATCH_EDGES])
            dst_far = sb(st, "dst_far", [BATCHES, BATCH_EDGES])
            base_g = sb(st, "base_g", [BATCHES, BATCH_GROUPS])
            last_g = sb(st, "last_g", [BATCHES, BATCH_GROUPS])
            span_g = sb(st, "span_g", [BATCHES, 1])
            span_row = sb(st, "span_row", [1, BATCHES])
            firsts = sb(st, "firsts", [1, MOST_PASSES])
            span_f = sb(st, "span_f", [1, 1])
            s = Stage(straight)
            s.do("gpsimd", None, lambda e: e.memset(x[:, NT - 1, :], 0.0))
            s.do("gpsimd", "ident0", lambda e: e.memset(ident[:, :], 0.0))
            s.do("gpsimd", "ident", lambda e: e.affine_select(
                out=ident[:, :], in_=ident[:, :], compare_op=ALU.not_equal, fill=1.0, base=0,
                pattern=[[-1, P]], channel_multiplier=1), "ident0")
            s.do("gpsimd", None, lambda e: e.memset(ones[:, :], 1.0))
            s.do("gpsimd", None, lambda e: e.memset(zero[:, :], 0.0))
            s.do("gpsimd", None, lambda e: e.iota(iota[:, :], [[1, WINDOW]], base=0, channel_multiplier=0,
                                                  allow_small_or_imprecise_dtypes=True))
            s.do("gpsimd", "constants", lambda e: e.iota(iota_col[:, :], [[0, 1]], base=0,
                                                         channel_multiplier=1,
                                                         allow_small_or_imprecise_dtypes=True))
            s.do("gpsimd", "firsts", lambda e: e.iota(
                firsts[:, :], [[WINDOW, MOST_PASSES]], base=0, channel_multiplier=0,
                allow_small_or_imprecise_dtypes=True))
            clear_accumulator(s, 2, "cleared")
            s.dma("sync", "dst_g", "load0", lambda e: e.dma_start(dst_i[:, :], a["dst_rows"]))
            s.dma("sync", "x", "load5", lambda e: e.dma_start(
                x[:, 0:NT - 1, :], a["x"][0:(NT - 1) * P, :].rearrange("(t p) f -> p t f", p=P)))
            s.dma("sync", "x", "load5", lambda e: e.dma_start(
                x[0:REST, NT - 1, :], a["x"][(NT - 1) * P:N, :]), "constants")
            grouped = lambda t: t[:, :].rearrange("h (g e) -> h g e", g=BATCH_GROUPS)
            s.do("vector", "dst_f", lambda e: e.tensor_copy(dst_f[:, :], dst_i[:, :]), "dst_g")
            s.do("vector", "far", lambda e: e.tensor_scalar(
                dst_far[:, :], dst_f[:, :], 0.0, FAR, ALU.is_lt, ALU.mult), "dst_f")
            s.do("vector", "dst_far", lambda e: e.tensor_tensor(
                dst_far[:, :], dst_far[:, :], dst_f[:, :], ALU.add), "far")
            s.do("vector", "base_g", lambda e: e.tensor_reduce(
                base_g[:, :], grouped(dst_far), AX, ALU.min), "dst_far")
            s.do("vector", "last_g", lambda e: e.tensor_reduce(
                last_g[:, :], grouped(dst_f), AX, ALU.max), "dst_f")
            s.do("vector", "last_less", lambda e: e.tensor_tensor(
                last_g[:, :], last_g[:, :], base_g[:, :], ALU.subtract), "base_g", "last_g")
            s.do("vector", "span_g", lambda e: e.tensor_reduce(
                span_g[:, :], last_g[:, :], AX, ALU.max), "last_less")
            s.do("vector", "local_rows", lambda e: e.tensor_tensor(
                grouped(dst_far), grouped(dst_f),
                base_g[:, :].unsqueeze(2).to_broadcast([BATCHES, BATCH_GROUPS, GROUP_EDGES]),
                ALU.subtract), "base_g")
            s.dma("sync", "base_out", "store0", lambda e: e.dma_start(
                base_dram[0, :].rearrange("(h g) -> h g", g=BATCH_GROUPS), base_g[:, :]), "base_g")
            s.dma("sync", "span_out", "store1", lambda e: e.dma_start(
                span_dram[0, :].unsqueeze(1), span_g[:, :]), "span_g")
            s.dma("sync", "rows_out", "store2", lambda e: e.dma_start(local_rows, dst_far[:, :]), "local_rows")
            s.dma("sync", "base_row", "load7", lambda e: e.dma_start(base_row[:, :], base_dram), "base_out")
            s.dma("sync", "span_row", "load8", lambda e: e.dma_start(span_row[:, :], span_dram), "span_out")
            s.do("vector", "span_f", lambda e: e.tensor_reduce(span_f[:, :], span_row[:, :], AX, ALU.max), "span_row")
            s.do("vector", "reached", lambda e: e.tensor_scalar(
                firsts[:, :], firsts[:, :], span_f[:, 0:1], None, ALU.is_le), "span_f", "firsts")
            s.do("vector", "reached_n", lambda e: e.tensor_reduce(
                span_f[:, :], firsts[:, :], AX, ALU.add), "reached")
            s.do("vector", "passes", lambda e: e.tensor_scalar(
                passes[:, :], span_f[:, :], 1.0, None, ALU.max), "reached_n")
            s.wait("vector", "passes", "local_rows")
            s.wait("sync", "rows_out", "span_out", "base_out", "base_row", "x")
            s.wait("gpsimd", "cleared")
            s.straight(nc)

        with ExitStack() as st:
            col_i = sb(st, "col_i", [P, TILES], I32)
            type_i = sb(st, "type_i", [P, TILES], I32)
            src_i = sb(st, "src_i", [P, TILES], I32)
            col_f = sb(st, "col_f", [P, TILES])
            src_f = sb(st, "src_f", [P, TILES])
            base_all = sb(st, "base_all", [P, GROUPS])
            kind_i = sb(st, "kind_i", [P, NT], I32)
            bn = sb(st, "bn0", [P, 4, 6])
            s = Stage(straight)
            s.dma("sync", "dst_c", "load1", lambda e: e.dma_start(col_i[:, :], a["dst_cols"]))
            s.dma("sync", "type_c", "load2", lambda e: e.dma_start(type_i[:, :], a["type_cols"]))
            s.dma("sync", "src_c", "load3", lambda e: e.dma_start(src_i[:, :], a["src_cols"]))
            s.dma("sync", "kind", "load4", lambda e: e.dma_start(kind_i[:, :], a["node_type"]))
            s.dma("sync", "base_all", "load6", lambda e: e.dma_start(
                base_all[:, :], base_dram[0, :].partition_broadcast(P)))
            s.do("vector", "col_f", lambda e: e.tensor_copy(col_f[:, :], col_i[:, :]), "dst_c")
            s.do("vector", "local_cols", lambda e: e.tensor_tensor(
                col_f[:, :].rearrange("p (g t) -> p g t", t=GROUP),
                col_f[:, :].rearrange("p (g t) -> p g t", t=GROUP),
                base_all[:, :].unsqueeze(2).to_broadcast([P, GROUPS, GROUP]), ALU.subtract), "col_f", "base_all")
            s.dma("sync", "cols_out", "store3", lambda e: e.dma_start(local_cols, col_f[:, :]), "local_cols")
            s.do("vector", "src_f", lambda e: e.tensor_copy(src_f[:, :], src_i[:, :]), "src_c")
            s.do("vector", "rel", lambda e: e.scalar_tensor_tensor(
                out=type_i[:, :], in0=type_i[:, :], scalar=float(N), in1=src_f[:, :],
                op0=ALU.mult, op1=ALU.add), "src_f", "type_c")
            s.dma("sync", "rel_out", "store0", lambda e: e.dma_start(rel_cols, type_i[:, :]), "rel")
            for k in range(SPECIES):
                s.do("vector", None, lambda e, k=k: e.tensor_scalar(
                    species[:, :, k], kind_i[:, :], float(k), None, ALU.is_equal), "kind")
            staggered((0, lambda i: statistics(s, bn, i, x[:, i, :], None)),
                      (2, lambda i: aggregate(s, bn, i)), count=NT)
            s.wait("vector", ("x", "norm", NT - 1))
            s.wait("sync", "cols_out", "rel_out")
            s.straight(nc)

        with ExitStack() as st:
            w = load_weights(st, [whole("root0", [P, P], a["L0_root_t"]),
                                  whole("brel", [P, P], a["L0_gnn_b_rel"].partition_broadcast(P))])
            h, hT = sb(st, "h", [P, HR, P]), sb(st, "hT", [P, 3, P])
            pT, pm = ps(st, "pT", [P, 2, 512]), ps(st, "pm", [P, 4, 512])
            s = Stage(straight)

            def normalise(i):
                normed(s, h, i, user="h_out")
                store(s, ("h_out", i), lambda e: e.dma_start(
                    table[i * P:i * P + rows(i), :], h[0:rows(i), i % HR, :]), ("h", i))
                s.do("gpsimd", ("biased", i), lambda e: e.tensor_tensor(
                    x[:, i, :], x[:, i, :], w["brel"][:, :], ALU.add), ("h", i))

            def multiply(i):
                s.do("tensor", ("hT_used", i), lambda e: e.matmul(
                    pm[:, i % 4, 0:P], hT[:, i % 3, :], w["root0"][:, :], start=True, stop=True),
                    ("hT", i), ring("root", i, 4))

            def add(i):
                s.do("vector", ("root", i), lambda e: e.tensor_tensor(
                    x[:, i, :], x[:, i, :], pm[:, i % 4, 0:P], ALU.add), ("hT_used", i), ("biased", i))

            staggered((0, normalise), (1, lambda i: turn_h(s, h, pT, i)), (3, add),
                      (1, lambda i: keep_hT(s, pT, hT, i)), (2, multiply), count=NT)
            s.wait("sync", *[("h_out", i) for i in range(max(0, NT - 4), NT)])
            s.wait("vector", ("root", NT - 1))
            s.straight(nc)

        plain_messages("sum0", table, a["src_cols"], counts=True)

        with ExitStack() as st:
            w = load_weights(st, [
                whole("rel0", [P, P], a["L0_rel_t"]),
                ("up", [P, P], [(lambda t: t[0:C, 0:C], a["L1_gnn_W_up_s"], 0)] + [
                    (lambda t, k=k: t[C * k:C * (k + 1), C * k:C * (k + 1)], a["L1_gnn_W_up_v"], 0)
                    for k in (1, 2, 3)])])
            h, hT = sb(st, "h", [P, HR, P]), sb(st, "hT", [P, 3, P])
            rowbuf = sb(st, "rowbuf", [P, 4, P])
            cnt = sb(st, "cnt", [P, NT])
            bn = sb(st, "bn1", [P, 4, 6])
            pT, pm = ps(st, "pT", [P, 2, 512]), ps(st, "pm", [P, 2, 512])
            pr, pc = ps(st, "pr", [P, 3, 512]), ps(st, "pc", [P, NT])
            s = Stage(straight)
            s.do("vector", "up_scaled", lambda e: e.tensor_scalar(w["up"][:, :], w["up"][:, :], C ** -0.5, None, ALU.mult))

            def relate(i):
                nodes = slice(i * P, (i + 1) * P)
                s.do("tensor", ("rel", i), lambda e: e.matmul(
                    pr[:, i % 3, 0:P], acc[:, 0, nodes], w["rel0"][:, :], start=True, stop=True),
                    ring("x1", i, 3))
                s.do("tensor", ("count", i), lambda e: e.matmul(
                    pc[:, i:i + 1], acc[0:1, 1, nodes], ones[0:1, 0:1], start=True, stop=True))

            def add(i):
                s.do("vector", ("x1", i), lambda e: e.tensor_tensor(
                    x[:, i, :], x[:, i, :], pr[:, i % 3, 0:P], ALU.add), ("rel", i))

            def up(i):
                s.do("tensor", ("hT_used", i), lambda e: e.matmul(
                    pm[:, i % 2, 0:P], hT[:, i % 3, :], w["up"][:, :], start=True, stop=True),
                    ("hT", i), "up_scaled", ring("row", i, 2))

            def send(i):
                s.do("vector", ("row", i), lambda e: e.tensor_copy(
                    rowbuf[:, i % 4, :], pm[:, i % 2, 0:P]), ("hT_used", i), ring("row_out", i, 4))
                store(s, ("row_out", i), lambda e: e.dma_start(
                    table[i * P:i * P + rows(i), :], rowbuf[0:rows(i), i % 4, :]), ("row", i))

            L = CHUNK + 4
            staggered((0, relate), (1, add), (2, lambda i: statistics(s, bn, i, x[:, i, :], ("x1", i))),
                      (L, lambda i: normed(s, h, i, by_component=True)),
                      (L + 1, lambda i: turn_h(s, h, pT, i)), (L + 2, up), (L + 3, send),
                      (3, lambda i: aggregate(s, bn, i)),
                      (L + 1, lambda i: keep_hT(s, pT, hT, i)), count=NT)
            s.do("vector", "cnt", lambda e: e.tensor_scalar(cnt[:, :], pc[:, :], 1e-8, None, ALU.add), ("count", NT - 1))
            s.do("vector", "rcnt", lambda e: e.reciprocal(rcount[:, :], cnt[:, :]), "cnt")
            s.do("vector", "valid", lambda e: e.tensor_scalar(cnt[:, :], pc[:, :], 0.0, None, ALU.is_gt), "rcnt")
            s.do("vector", "rcount", lambda e: e.tensor_tensor(rcount[:, :], rcount[:, :], cnt[:, :], ALU.mult), "valid")
            for i in range(CHUNK - 1, NT, CHUNK):
                s.wait("gpsimd", ("count", i))
                for k in range(2):
                    s.do("gpsimd", "cleared", lambda e, i=i, k=k: e.memset(acc[:, k, (i + 1 - CHUNK) * P:(i + 1) * P], 0.0))
            s.wait("gpsimd", ("count", NT - 1))
            for k in range(2):
                s.do("gpsimd", "cleared", lambda e, k=k: e.memset(acc[:, k, NT // CHUNK * CHUNK * P:ACC], 0.0))
            s.wait("sync", *[("row_out", i) for i in range(max(0, NT - 4), NT)])
            s.wait("gpsimd", "cleared")
            s.straight(nc)

        with ExitStack() as st:
            w = load_weights(st, [
                ("radial", [P, P], [(lambda t, k=k: t[R * k:R * (k + 1), R * k:R * (k + 1)], a["L1_gnn_W_r1"], 0)
                                    for k in range(BATCH_TILES)]),
                ("paths", [P, GROUP, 4 * C], [(lambda t, k=k: t[R * k:R * (k + 1), k % GROUP, :], a["L1_gnn_W_r2"], 0)
                                              for k in range(BATCH_TILES)])])
            local = sb(st, "local_1", [P, TURN_BATCHES, BATCH_TILES])
            sh = sb(st, "sh", [P, TURN_BATCHES, BATCH_TILES * 4])
            radial_in = sb(st, "radial_in", [P, TURN_BATCHES, P])
            hidden = sb(st, "hidden", [P, 2, P])
            hit = sb(st, "hit", [P, 2, GROUP, WINDOW])
            sel = sb(st, "sel_1", [P, 3, GROUP, 4, WINDOW])
            mess = sb(st, "mess", [P, 2, GROUP, 2 * P])
            PART = 64
            p_hidden = ps(st, "p_hidden", [P, 512])
            p_path = ps(st, "p_path", [P, GROUP, 512])
            sums = ps(st, "sums_1", [P, 3, 512])
            s = Stage(straight)
            s.do("vector", "p", lambda e: e.tensor_scalar(w["paths"][:, :, :], w["paths"][:, :, :], R ** -0.5, None, ALU.mult))
            s.do("vector", "p3", lambda e: e.tensor_scalar(w["paths"][:, :, 3 * C:], w["paths"][:, :, 3 * C:], 3.0 ** -0.5, None, ALU.mult), "p")
            s.wait("vector", "p3")
            s.straight(nc)

            def body(s, gathered):
                def radial(b):
                    s.do("tensor", ("radial", b), lambda e, it: e.matmul(
                        p_hidden[:, 0:P], w["radial"][:, :], radial_in[:, b, :], start=True, stop=True),
                        ("edges", b), ring("hidden", b, 1, TURN_BATCHES))
                    s.do("scalar", ("hidden", b), lambda e, it: e.activation(
                        hidden[:, b % 2, :], p_hidden[:, 0:P], ACT.Silu, scale=R ** -0.5), ("radial", b),
                        ring("hidden_used", b, 2, TURN_BATCHES))

                def paths(g):
                    b, k = g // BATCH_GROUPS, g % BATCH_GROUPS
                    if k == 0:
                        radial(b)
                    s.wait("tensor", ("hidden", b), ring("product", g, 1, TURN_GROUPS))
                    for t in range(GROUP):
                        part = slice(32 * t, 32 * t + 32)
                        s.do("tensor", ("paths", g), lambda e, it, t=t, part=part: e.matmul(
                            p_path[:, t, 0:4 * C], hidden[part, b % 2, :],
                            w["paths"][part, k, :], start=True, stop=True))
                    s.steps[("hidden_used", b)] = s.steps[("paths", g)]

                def find(g):
                    b, at = place(g)
                    s.do("vector", ("hit", g), lambda e, it: e.tensor_tensor(
                        hit[:, g % 2, :, :], iota_pass[:, :].unsqueeze(1).to_broadcast([P, GROUP, WINDOW]),
                        local[:, b, at:at + GROUP].unsqueeze(2).to_broadcast([P, GROUP, WINDOW]), ALU.is_equal),
                        ("edges", b), ring("selected0", g, 2, TURN_GROUPS))
                    s.wait("scalar", ("hit", g), ring("summed", g, 3, TURN_GROUPS))
                    for t in range(GROUP):
                        s.do("scalar", ("selected0", g), lambda e, it, t=t: e.activation(
                            sel[:, g % 3, t, 0, :], hit[:, g % 2, t, :], ACT.Copy,
                            scale=sh[:, b, 4 * (at + t):4 * (at + t) + 1]))

                def selections(g):
                    b, at = place(g)
                    s.do("vector", ("selected", g), lambda e, it: e.tensor_tensor(
                        sel[:, g % 3, :, 1:4, :],
                        hit[:, g % 2, :, :].unsqueeze(2).to_broadcast([P, GROUP, 3, WINDOW]),
                        sh[:, b, 4 * at:4 * (at + GROUP)].rearrange("p (t k) -> p t k", k=4)[:, :, 1:4]
                        .unsqueeze(3).to_broadcast([P, GROUP, 3, WINDOW]), ALU.mult),
                        ("hit", g), ring("summed", g, 3, TURN_GROUPS))

                def products(g):
                    rows_ = gathered[:, g % SLOTS, :, :]
                    vec = rows_[:, :, C:].rearrange("p t (k c) -> p t k c", k=3)
                    m = mess[:, g % 2, :, :]
                    pw = p_path[:, :, 0:4 * C]
                    s.do("vector", None, lambda e, it: e.tensor_tensor(
                        m.rearrange("p t (n c) -> p t n c", n=2)[:, :, :, 0:C],
                        rows_[:, :, 0:C].unsqueeze(2).to_broadcast([P, GROUP, 2, C]),
                        pw[:, :, 0:2 * C].rearrange("p t (n c) -> p t n c", n=2), ALU.mult),
                        ("paths", g), ("gathered", g), ring("summed", g, 2, TURN_GROUPS))
                    for n in range(2):
                        s.do("vector", ("product", g), lambda e, it, n=n: e.tensor_tensor(
                            m[:, :, n * P + C:(n + 1) * P].rearrange("p t (k c) -> p t k c", k=3), vec,
                            pw[:, :, (2 + n) * C:(3 + n) * C].unsqueeze(2).to_broadcast([P, GROUP, 3, C]), ALU.mult))
                    s.steps[("rows_used", g)] = s.steps[("product", g)]

                def multiply(g):
                    s.wait("tensor", ("product", g), ("selected", g), ("selected0", g),
                           ring("added", g, 3, TURN_GROUPS))
                    second = slice(PART, PART + WINDOW)
                    for t in range(GROUP):
                        first, last = t == 0, t == GROUP - 1
                        s.do("tensor", None, lambda e, it, t=t, f=first, l=last: e.matmul(
                            sums[:, g % 3, 0:WINDOW], mess[:, g % 2, t, 0:P], sel[:, g % 3, t, 0, :], start=f, stop=l))
                        for k in range(3):
                            s.do("tensor", None, lambda e, it, t=t, k=k, l=last: e.matmul(
                                sums[C * k:C * (k + 1), g % 3, second], mess[:, g % 2, t, P:P + C],
                                sel[:, g % 3, t, 1 + k, :], start=False, stop=l, skip_group_check=True))
                            s.do("tensor", ("summed", g), lambda e, it, t=t, k=k, l=last and k == 2: e.matmul(
                                sums[3 * C:P, g % 3, second], mess[:, g % 2, t, P + C * (k + 1):P + C * (k + 2)],
                                sel[:, g % 3, t, 1 + k, :], start=False, stop=l, skip_group_check=True))
                    s.steps[("edges_used", g)] = s.steps[("summed", g)]

                staggered((0, paths), (1, multiply), (0, find),
                          (2, lambda g: accumulate(s, sums[:, g % 3, 0:2 * PART].rearrange(
                              "p (n w) -> p n w", n=2)[:, :, 0:WINDOW], g, 2)),
                          (0, selections), (0, products))

            message_stage("messages1", body, table, a["src_cols"], [
                (local, column(local_cols)),
                (sh, lambda it, b: a["sh_cols"][:, bass.ds((it * TURN_TILES + b * BATCH_TILES) * 4, BATCH_TILES * 4)]),
                (radial_in, lambda it, b: a["radial_cols"][:, bass.ds((it * TURN_BATCHES + b) * P, P)])], st)

        local_term = acc[:, 1, 0:NT * P].rearrange("p (t f) -> p t f", f=P)
        with ExitStack() as st:
            down_s, down_v = a["L1_gnn_W_down_s"], a["L1_gnn_W_down_v"]
            specs = [("down_a", [P, SKIP], [(lambda t: t[0:C, 0:2 * C], down_s[0:C, :], 0)] + [
                        (lambda t, k=k: t[C * (k + 1):C * (k + 2), 2 * C + C * k:2 * C + C * (k + 1)], down_v[C:2 * C, :], 0)
                        for k in range(3)]),
                     ("down_b", [P, SKIP], [(lambda t: t[3 * C:P, 0:2 * C], down_s[C:2 * C, :], 0)] + [
                        (lambda t, k=k: t[C * k:C * (k + 1), 2 * C + C * k:2 * C + C * (k + 1)], down_v[0:C, :], 0)
                        for k in range(3)]),
                     ("skip", [P, SPECIES, SKIP], [
                         (lambda t, q=q: t[0:C, q, 0:2 * C], a["L1_gnn_W_skip_s"][q], 0) for q in range(SPECIES)] + [
                         (lambda t, q=q, k=k: t[C * (k + 1):C * (k + 2), q, 2 * C + C * k:2 * C + C * (k + 1)],
                          a["L1_gnn_W_skip_v"][q], 0) for q in range(SPECIES) for k in range(3)]),
                     whole("msg_src", [P, P], a["L2_gnn_msg_w"][0:P, :]),
                     whole("msg_dst", [P, P], a["L2_gnn_msg_w"][P:2 * P, :]),
                     whole("msg_b", [P, P], a["L2_gnn_msg_b"].partition_broadcast(P)),
                     whole("upd_h", [P, P], a["L2_gnn_upd_w"][0:P, :]),
                     whole("upd_b", [P, P], a["L2_gnn_upd_b"].partition_broadcast(P)),
                     whole("gate_w", [P, 1], a["L2_gnn_gate_w"]),
                     whole("gate_b", [P, 1], a["L2_gnn_gate_b"].partition_broadcast(P))]
            w = load_weights(st, specs)
            h, hT = sb(st, "h", [P, HR, P]), sb(st, "hT", [P, 3, P])
            mean = sb(st, "mean", [P, 4])
            bn = sb(st, "bn2", [P, 4, 6])
            both = sb(st, "both", [P, 3, SKIP])
            silu = sb(st, "silu", [P, 3, 2 * C])
            gated = sb(st, "gated", [P, 2, 3 * C])
            rowbuf = sb(st, "rowbuf", [P, 3, 2, P])
            gatec = sb(st, "gatec", [P, 2, 1])
            pT, p_sum = ps(st, "pT", [P, 2, 512]), ps(st, "p_sum", [P, 2, 512])
            p_skip = ps(st, "p_skip", [P, 2, 1024])
            pm, pg = p_skip, p_sum
            s = Stage(straight)
            agg_scale = 0.5 * (2 * C) ** -0.5 * DEG ** -0.5
            for n in ("down_a", "down_b"):
                s.do("vector", "scaled", lambda e, n=n: e.tensor_scalar(w[n][:, :], w[n][:, :], agg_scale, None, ALU.mult))
            s.do("vector", "scaled", lambda e: e.tensor_scalar(w["skip"][:, :, :], w["skip"][:, :, :], 0.5 * C ** -0.5, None, ALU.mult))
            for n, (name, r) in enumerate((("msg_src", P), ("msg_dst", P), ("msg_b", P))):
                s.do("vector", ("m", n), lambda e, n=n, name=name, r=r: e.tensor_reduce(
                    mean[0:r, n:n + 1], w[name][0:r, :], AX, ALU.add))
                s.do("vector", ("m1", n), lambda e, n=n, r=r: e.tensor_scalar(
                    mean[0:r, n:n + 1], mean[0:r, n:n + 1], 1.0 / P, None, ALU.mult), ("m", n))
                s.do("vector", "scaled", lambda e, n=n, name=name, r=r: e.tensor_scalar(
                    w[name][0:r, :], w[name][0:r, :], mean[0:r, n:n + 1], None, ALU.subtract), ("m1", n))
            PER = 3

            def down(i):
                nodes = slice(i * P, (i + 1) * P)
                s.do("tensor", None, lambda e: e.matmul(
                    p_sum[:, i % 2, 0:SKIP], acc[:, 0, nodes], w["down_a"][:, :], start=True, stop=False),
                    "scaled", ring("both0", i, 2))
                s.do("tensor", ("down", i), lambda e: e.matmul(
                    p_sum[:, i % 2, 0:SKIP], acc[:, 1, nodes], w["down_b"][:, :], start=False, stop=True))

            def skip(i):
                s.wait("tensor", ("hT", i), ring("both", i, 2))
                for q0 in (0, PER):
                    q1 = min(q0 + PER, SPECIES)
                    s.do("tensor", ("hT_used", i), lambda e, q0=q0, q1=q1: e.matmul(
                        p_skip[:, i % 2, 512 * (q0 // PER):512 * (q0 // PER) + (q1 - q0) * SKIP],
                        hT[:, i % 3, :], w["skip"][:, q0:q1, :].rearrange("p q f -> p (q f)"), start=True, stop=True))

            def keep_sum(i):
                s.do("scalar", ("both0", i), lambda e: e.activation(
                    both[:, i % 3, :], p_sum[:, i % 2, 0:SKIP], ACT.Copy), ("down", i), ring("gated", i, 3))

            def add_skip(i):
                for q in range(SPECIES):
                    off = 512 * (q // PER) + (q % PER) * SKIP
                    s.do("vector", ("both", i) if q == SPECIES - 1 else ("skip", i, q),
                         lambda e, q=q, off=off: e.scalar_tensor_tensor(
                             out=both[:, i % 3, :], in0=p_skip[:, i % 2, off:off + SKIP],
                             scalar=species[:, i, q:q + 1], in1=both[:, i % 3, :], op0=ALU.mult, op1=ALU.add),
                         ("hT_used", i), ("both0", i) if q == 0 else ("skip", i, q - 1))

            def activate(i):
                s.do("scalar", ("silu", i), lambda e: e.activation(
                    silu[:, i % 3, :], both[:, i % 3, 0:2 * C], ACT.Silu), ("both", i), ring("x2", i, 3))

            def gating(i):
                s.do("gpsimd", ("gated", i), lambda e: e.tensor_tensor(
                    gated[:, i % 2, :].rearrange("p (k c) -> p k c", k=3),
                    both[:, i % 3, 2 * C:].rearrange("p (k c) -> p k c", k=3),
                    silu[:, i % 3, C:2 * C].unsqueeze(1).to_broadcast([P, 3, C]), ALU.mult),
                    ("silu", i), ring("x2", i, 2))
                s.do("gpsimd", ("x2s", i), lambda e: e.tensor_tensor(
                    x[:, i, 0:C], x[:, i, 0:C], silu[:, i % 3, 0:C], ALU.add), ("h", i))

            def add(i):
                s.do("vector", ("x2", i), lambda e: e.tensor_tensor(
                    vectors_last(x[:, i, C:P]), vectors_last(x[:, i, C:P]),
                    gated[:, i % 2, :].rearrange("p (k c) -> p k c", k=3), ALU.add), ("gated", i), ("x2s", i))

            staggered((0, lambda i: normed(s, h, i, by_component=True)), (0, down),
                      (1, lambda i: turn_h(s, h, pT, i)), (2, skip),
                      (1, keep_sum), (5, add), (6, lambda i: statistics(s, bn, i, x[:, i, :], ("x2", i))),
                      (1, lambda i: keep_hT(s, pT, hT, i)),
                      (3, add_skip), (3, activate), (4, gating),
                      (7, lambda i: aggregate(s, bn, i)), count=NT)
            s.wait("gpsimd", ("down", NT - 1))
            clear_accumulator(s, 1, "cleared")
            s.dma("sync", "tail", "load0", lambda e: e.dma_start(window_table[NT * P:ACC, :], zero[:, :]))
            s.straight(nc)

            s = Stage(straight)

            def widen(i):
                s.wait("tensor", ("hT", i), ring("row", i, 2), ring("term", i, 2))
                for off, name in ((0, "msg_src"), (P, "msg_dst"), (512, "upd_h")):
                    s.do("tensor", ("wide", i), lambda e, off=off, name=name: e.matmul(
                        pm[:, i % 2, off:off + P], hT[:, i % 3, :], w[name][:, :], start=True, stop=True))
                s.do("tensor", ("hT_used", i), lambda e: e.matmul(
                    pg[:, i % 2, 0:1], hT[:, i % 3, :], w["gate_w"][:, :], start=True, stop=True), ring("gate", i, 2))
                s.do("scalar", ("gate", i), lambda e: e.activation(
                    gate[:, i:i + 1], pg[:, i % 2, 0:1], ACT.Sigmoid, bias=w["gate_b"][:, 0:1]), ("hT_used", i))

            def send(i):
                s.do("scalar", ("row_src", i), lambda e: e.activation(
                    rowbuf[:, i % 3, 0, :], pm[:, i % 2, 0:P], ACT.Copy), ("wide", i), ring("src_out", i, 3))
                s.do("vector", ("row", i), lambda e: e.tensor_tensor(
                    rowbuf[:, i % 3, 1, :], pm[:, i % 2, P:2 * P], w["msg_b"][:, :], ALU.add), ("row_src", i),
                    ring("dst_out", i, 3))
                s.do("vector", ("term", i), lambda e: e.tensor_tensor(
                    local_term[:, i, :], pm[:, i % 2, 512:512 + P], w["upd_b"][:, :], ALU.add))
                store(s, ("src_out", i), lambda e: e.dma_start(
                    table[i * P:i * P + rows(i), :], rowbuf[0:rows(i), i % 3, 0, :]), ("row_src", i))
                store(s, ("dst_out", i), lambda e: e.dma_start(
                    window_table[i * P:(i + 1) * P, :], rowbuf[:, i % 3, 1, :]), ("row", i))

            def mix(i):
                s.do("vector", ("gate1", i), lambda e: e.tensor_scalar(
                    gatec[:, i % 2, :], gate[:, i:i + 1], -1.0, 1.0, ALU.mult, ALU.add), ("gate", i))

            def mixed(i):
                s.do("vector", ("h_mixed", i), lambda e: e.scalar_tensor_tensor(
                    out=x[:, i, :], in0=h[:, i % HR, :], scalar=gatec[:, i % 2, 0:1], in1=x[:, i, :],
                    op0=ALU.mult, op1=ALU.add), ("gate1", i))

            staggered((0, lambda i: normed(s, h, i, user="h_mixed")), (1, lambda i: turn_h(s, h, pT, i)),
                      (1, lambda i: keep_hT(s, pT, hT, i)), (2, widen), (3, mix), (3, send), (3, mixed), count=NT)
            s.wait("sync", *[(n, i) for i in range(max(0, NT - 4), NT) for n in ("src_out", "dst_out")])
            s.wait("vector", ("h_mixed", NT - 1))
            s.straight(nc)

        with ExitStack() as st:
            w = load_weights(st, [whole("msg_g", [P, P], a["L2_gnn_msg_g"].partition_broadcast(P)),
                                  whole("msg_beta", [P, P], a["L2_gnn_msg_beta"].partition_broadcast(P))])
            local = sb(st, "local_2", [P, TURN_BATCHES, BATCH_TILES])
            weight = sb(st, "weight_2", [P, TURN_BATCHES, BATCH_TILES])
            sel = sb(st, "sel_2", [P, 4, GROUP, WINDOW])
            near_rows = sb(st, "near_rows", [WINDOW, 4, P])
            near_dst = sb(st, "near_dst", [WINDOW, 4, GROUP_EDGES])
            spread = sb(st, "spread", [WINDOW, 2, GROUP_EDGES])
            sq = sb(st, "sq", [P, 4, GROUP])
            eps = sb(st, "eps", [P, 1])
            y = sb(st, "y", [P, 4, GROUP, P])
            p_near = ps(st, "p_near", [P, 2, GROUP, P])
            sums = ps(st, "sums_2", [P, 4, 512])
            s = Stage(straight)
            s.do("vector", "eps", lambda e: e.memset(eps[:, :], EPS))
            s.wait("vector", "eps")
            s.straight(nc)

            def near(s, g):
                b, at = place(g)

                def load(e, it):
                    at = e.value_load(address[0:1, bass.ds(it * TURN_GROUPS + g, 1)], min_val=0, max_val=N)
                    return e.dma_start(near_rows[:, g % 4, :], window_table[bass.ds(at, WINDOW), :])
                s.wait("sync", ring("spread_out", g, 4, TURN_GROUPS))
                s.dma("sync", ("near", g), f"near{g % 4}", load)
                s.dma("sync", ("near", g), f"near{g % 4}", lambda e, it: e.dma_start(
                    near_dst[:, g % 4, :], local_rows[bass.ds(it * TURN_BATCHES + b, 1), at * P:at * P + GROUP_EDGES]
                    .to_broadcast([WINDOW, GROUP_EDGES])))

            def body(s, gathered):
                def spread_near(g):
                    s.do("vector", ("spread", g), lambda e, it: e.tensor_scalar(
                        spread[:, g % 2, :], near_dst[:, g % 4, :], iota_col_pass[0:WINDOW, :], None, ALU.is_equal),
                        ("near", g), ring("spread_out", g, 2, TURN_GROUPS))
                    s.wait("tensor", ("spread", g), ring("z", g, 2, TURN_GROUPS))
                    for t in range(GROUP):
                        s.do("tensor", ("spread_out", g), lambda e, it, t=t: e.matmul(
                            p_near[:, g % 2, t, :], spread[:, g % 2, t * P:(t + 1) * P], near_rows[:, g % 4, :],
                            start=True, stop=True))

                def combine(g):
                    s.do("vector", ("z", g), lambda e, it: e.tensor_tensor(
                        gathered[:, g % SLOTS, :, :], gathered[:, g % SLOTS, :, :], p_near[:, g % 2, :, :], ALU.add),
                        ("spread_out", g), ("gathered", g))
                    s.wait("scalar", ("z", g), ring("summed", g, 4, TURN_GROUPS))
                    for t in range(GROUP):
                        s.do("scalar", ("sq", g), lambda e, it, t=t: e.activation(
                            y[:, g % 4, t, :], gathered[:, g % SLOTS, t, :], ACT.Square, accum_out=sq[:, g % 4, t:t + 1]))
                    s.do("scalar", ("std", g), lambda e, it: e.activation(
                        sq[:, g % 4, :], sq[:, g % 4, :], ACT.Sqrt, scale=1.0 / P, bias=eps[:, 0:1]), ("sq", g))

                def invert(g):
                    s.do("vector", ("rstd", g), lambda e, it: e.reciprocal(
                        sq[:, g % 4, :], sq[:, g % 4, :]), ("std", g))

                def scale(g):
                    s.wait("vector", ("rstd", g))
                    for t in range(GROUP):
                        s.do("vector", ("scaled", g), lambda e, it, t=t: e.scalar_tensor_tensor(
                            out=y[:, g % 4, t, :], in0=gathered[:, g % SLOTS, t, :], scalar=sq[:, g % 4, t:t + 1],
                            in1=w["msg_g"][:, :], op0=ALU.mult, op1=ALU.mult))
                    s.steps[("rows_used", g)] = s.steps[("scaled", g)]

                def bias_relu(g):
                    s.do("vector", ("shifted", g), lambda e, it: e.tensor_tensor(
                        y[:, g % 4, :, :], y[:, g % 4, :, :],
                        w["msg_beta"][:, :].unsqueeze(1).to_broadcast([P, GROUP, P]), ALU.add), ("scaled", g))
                    s.do("scalar", ("relu", g), lambda e, it: e.activation(
                        y[:, g % 4, :, :], y[:, g % 4, :, :], ACT.Relu), ("shifted", g))

                def multiply(g):
                    s.wait("tensor", ("relu", g), ("weighed", g), ring("added", g, 4, TURN_GROUPS))
                    for t in range(GROUP):
                        s.do("tensor", ("summed", g), lambda e, it, t=t: e.matmul(
                            sums[:, g % 4, 0:WINDOW], y[:, g % 4, t, :], sel[:, g % 4, t, :],
                            start=t == 0, stop=t == GROUP - 1))
                    s.steps[("edges_used", g)] = s.steps[("summed", g)]

                staggered((2, invert), (0, lambda g: select(s, sel, local, g)), (0, spread_near),
                          (0, lambda g: weigh(s, sel, weight, g)), (2, scale),
                          (4, lambda g: accumulate(s, sums[:, g % 4, 0:WINDOW].unsqueeze(1), g)),
                          (2, bias_relu), (3, multiply), (0, combine))

            message_stage("messages2", body, table, a["src_cols"], [
                (local, column(local_cols)), (weight, column(a["weight_cols"]))], st, near=near)

        with ExitStack() as st:
            w = load_weights(st, [
                whole("upd_m", [P, P], a["L2_gnn_upd_w"][P:2 * P, :]),
                whole("upd_g", [P, P], a["L2_gnn_upd_g"].partition_broadcast(P)),
                whole("upd_beta", [P, P], a["L2_gnn_upd_beta"].partition_broadcast(P)),
                whole("rel", [P, REL, P], a["L3_gnn_w_rel"][0].rearrange("r d e -> d r e")),
                whole("root", [P, P], a["L3_gnn_w_root"][0]),
                whole("skip0", [P, P], a["L3_gnn_w_skip"][0]),
                whole("skip1", [P, P], a["L3_gnn_w_skip"][1]),
                whole("b_col", [P, 2], a["L3_b_cols"]),
                whole("b_conv1", [P, P], a["L3_gnn_b_conv"][1, :].partition_broadcast(P)),
                whole("b_skip1", [P, P], a["L3_gnn_b_skip"][1, :].partition_broadcast(P))])
            h, hT = sb(st, "h", [P, HR, P]), sb(st, "hT", [P, 3, P])
            bn_z, bn = sb(st, "bn_z", [P, 4, 6]), sb(st, "bn3", [P, 4, 6])
            u = sb(st, "u", [P, 6, P])
            rowbuf = sb(st, "rowbuf", [P, 3, REL, P])
            pT, pm = ps(st, "pT", [P, 2, 512]), ps(st, "pm", [P, 2, 512])
            pl, px = ps(st, "pl", [P, 2, 512]), ps(st, "px", [P, 1, 512])
            pu = ps(st, "pu", [P, 1, 512])
            s = Stage(straight)
            s.do("vector", "root_sum", lambda e: e.tensor_tensor(w["root"][:, :], w["root"][:, :], w["skip0"][:, :], ALU.add))
            s.do("vector", "b_sum", lambda e: e.tensor_tensor(w["b_col"][:, 0:1], w["b_col"][:, 0:1], w["b_col"][:, 1:2], ALU.add))
            s.do("vector", "b_row", lambda e: e.tensor_tensor(w["b_conv1"][:, :], w["b_conv1"][:, :], w["b_skip1"][:, :], ALU.add))
            s.do("gpsimd", "acc_tail", lambda e: e.memset(acc[:, 0, NT * P:ACC], 0.0))

            def update(i):
                nodes = slice(i * P, (i + 1) * P)
                s.do("tensor", ("upd", i), lambda e: e.matmul(
                    pu[:, 0, 0:P], acc[:, 0, nodes], w["upd_m"][:, :], start=True, stop=True), ring("z", i, 1))

            def updated(i):
                s.do("vector", ("z", i), lambda e: e.scalar_tensor_tensor(
                    out=local_term[:, i, :], in0=pu[:, 0, 0:P], scalar=rcount[:, i:i + 1],
                    in1=local_term[:, i, :], op0=ALU.mult, op1=ALU.add), ("upd", i))

            def normal(i):
                s.do("scalar", ("u", i), lambda e: e.activation(
                    u[:, i % 6, :], local_term[:, i, :], ACT.Identity, bias=shift[:, i:i + 1],
                    scale=rstd[:, i:i + 1]), ("z", "norm", i), ring("x3", i, 6))

            def affine(i):
                s.do("gpsimd", ("ug", i), lambda e: e.tensor_tensor(
                    u[:, i % 6, :], u[:, i % 6, :], w["upd_g"][:, :], ALU.mult), ("u", i))
                s.do("gpsimd", ("ub", i), lambda e: e.tensor_tensor(
                    u[:, i % 6, :], u[:, i % 6, :], w["upd_beta"][:, :], ALU.add), ("ug", i))

            def gating(i):
                s.do("vector", ("ur", i), lambda e: e.tensor_scalar(
                    u[:, i % 6, :], u[:, i % 6, :], 0.0, gate[:, i:i + 1], ALU.max, ALU.mult), ("ub", i))

            def add(i):
                s.do("vector", ("x3", i), lambda e: e.tensor_tensor(
                    x[:, i, :], x[:, i, :], u[:, i % 6, :], ALU.add), ("ur", i))

            def multiply_relations(i, lhs, after):
                s.wait("tensor", after, ring("rel_row", i, 2))
                for r in range(REL):
                    s.do("tensor", ("rel", i), lambda e, r=r: e.matmul(
                        pm[:, i % 2, r * P:(r + 1) * P], lhs, w["rel"][:, r, :], start=True, stop=True))

            def send_relations(i):
                s.do("vector", ("rel_row", i), lambda e: e.tensor_copy(
                    rowbuf[:, i % 3, :, :].rearrange("p r f -> p (r f)"), pm[:, i % 2, 0:REL * P]), ("rel", i),
                    *[ring(("rel_out", r), i, 3) for r in range(REL)])
                for r in range(REL):
                    store(s, ("rel_out", r, i), lambda e, r=r: e.dma_start(
                        rel_table[r * N + i * P:r * N + i * P + rows(i), :], rowbuf[0:rows(i), i % 3, r, :]), ("rel_row", i))

            def convolve(i):
                multiply_relations(i, hT[:, i % 3, :], ("hT", i))
                s.do("tensor", ("local", i), lambda e: e.matmul(
                    pl[:, i % 2, 0:P], w["root"][:, :], hT[:, i % 3, :], start=True, stop=True),
                    "root_sum", ring("acc", i, 2))
                s.do("tensor", ("hT_used", i), lambda e: e.matmul(
                    px[:, 0, 0:P], hT[:, i % 3, :], w["skip1"][:, :], start=True, stop=True), ring("x4", i, 1))

            def keep_local(i):
                nodes = slice(i * P, (i + 1) * P)
                s.do("gpsimd", ("biased", i), lambda e: e.tensor_tensor(
                    x[:, i, :], x[:, i, :], w["b_conv1"][:, :], ALU.add), ("h", i), "b_row")
                s.do("scalar", ("acc", i), lambda e: e.activation(
                    acc[:, 0, nodes], pl[:, i % 2, 0:P], ACT.Identity, bias=w["b_col"][:, 0:1]), ("local", i), "b_sum")

            def add_skip(i):
                s.do("vector", ("x4", i), lambda e: e.tensor_tensor(
                    x[:, i, :], x[:, i, :], px[:, 0, 0:P], ALU.add), ("hT_used", i), ("biased", i))

            A, B = CHUNK + 4, 2 * CHUNK + 12
            staggered((0, update), (0, updated), (1, lambda i: statistics(s, bn_z, i, local_term[:, i, :], ("z", i), "z")),
                      (A, normal), (A + 1, affine), (A + 2, gating), (B + 2, add_skip), (A + 3, add),
                      (B, lambda i: normed(s, h, i)), (B + 1, lambda i: turn_h(s, h, pT, i)),
                      (B + 2, convolve), (B + 3, keep_local),
                      (2, lambda i: aggregate(s, bn_z, i, "z")),
                      (A + 4, lambda i: statistics(s, bn, i, x[:, i, :], ("x3", i))),
                      (B + 3, send_relations),
                      (B + 1, lambda i: keep_hT(s, pT, hT, i)),
                      (A + 5, lambda i: aggregate(s, bn, i)), count=NT)
            s.wait("sync", *[("rel_out", r, i) for i in range(max(0, NT - 4), NT) for r in range(REL)])
            s.wait("gpsimd", "acc_tail")
            s.straight(nc)

        plain_messages("conv0", rel_table, rel_cols, a["weight_cols"])

        with ExitStack() as st:
            w = load_weights(st, [
                whole("rel", [P, REL, P], a["L3_gnn_w_rel"][1].rearrange("r d e -> d r e")),
                whole("root1", [P, P], a["L3_gnn_w_root"][1])])
            rowbuf = sb(st, "rowbuf", [P, 3, REL, P])
            pm, px = ps(st, "pm", [P, 2, 512]), ps(st, "px", [P, 2, 512])
            s = Stage(straight)
            for i in range(NT):
                nodes = slice(i * P, (i + 1) * P)
                multiply_relations(i, acc[:, 0, nodes], None)
                s.do("tensor", ("root", i), lambda e, i=i, nodes=nodes: e.matmul(
                    px[:, i % 2, 0:P], acc[:, 0, nodes], w["root1"][:, :], start=True, stop=True), ring("x5", i, 2))
                send_relations(i)
                s.do("vector", ("x5", i), lambda e, i=i: e.tensor_tensor(
                    x[:, i, :], x[:, i, :], px[:, i % 2, 0:P], ALU.add), ("root", i))
                s.wait("gpsimd", ("root", i))
                s.do("gpsimd", "cleared", lambda e, nodes=nodes: e.memset(acc[:, 0, nodes], 0.0))
            s.do("gpsimd", "cleared", lambda e: e.memset(acc[:, 0, NT * P:ACC], 0.0))
            s.wait("sync", *[("rel_out", r, i) for i in range(max(0, NT - 4), NT) for r in range(REL)])
            s.wait("gpsimd", "cleared")
            s.straight(nc)

        plain_messages("conv1", rel_table, rel_cols, a["weight_cols"])

        with ExitStack() as st:
            pm = ps(st, "pm", [P, 4, 512])
            s = Stage(straight)
            for i in range(NT):
                s.do("tensor", ("agg", i), lambda e, i=i: e.transpose(
                    pm[:, i % 4, 0:P], acc[:, 0, i * P:(i + 1) * P], ident[:, :]), ring("x6", i, 4))
                s.do("vector", ("x6", i), lambda e, i=i: e.tensor_tensor(
                    x[:, i, :], x[:, i, :], pm[:, i % 4, 0:P], ALU.add), ("agg", i))
                store(s, ("out", i), lambda e, i=i: e.dma_start(
                    out[i * P:i * P + rows(i), :], x[0:rows(i), i, :]), ("x6", i))
            s.wait("sync", *[("out", i) for i in range(NT)])
            s.straight(nc)


def kernel(**inputs):
    import concourse.bacc as bacc
    from concourse.bass_utils import run_bass_kernel_spmd

    v = {k: np.asarray(q) for k, q in inputs.items()}
    N, E = v["x"].shape[0], v["src"].shape[0]
    turns = -(-E // TURN_EDGES)
    pad = turns * TURN_EDGES - E
    nt = -(-N // P)

    def edges(q, fill=0):
        return np.concatenate([q, np.full((pad,) + q.shape[1:], fill, q.dtype)])

    def cols(q):
        return np.ascontiguousarray(q.reshape((-1, P) + q.shape[1:]).swapaxes(0, 1).reshape(P, -1))

    arrays = {
        "x": v["x"],
        "src_cols": cols(edges(v["src"])),
        "dst_cols": cols(edges(v["dst"], -1)),
        "dst_rows": edges(v["dst"], -1).reshape(-1, BATCH_EDGES),
        "type_cols": cols(edges(v["edge_type_3"])),
        "weight_cols": cols(edges(v["edge_weight"])),
        "sh_cols": cols(edges(v["edge_attr_4"])),
        "radial_cols": np.ascontiguousarray(
            edges(v["edge_attr_8"]).reshape(-1, BATCH_GROUPS, GROUP, P, R)
            .transpose(2, 1, 4, 0, 3).reshape(P, -1)),
        "node_type": np.ascontiguousarray(np.concatenate(
            [v["node_type_5"], np.zeros(nt * P - N, v["node_type_5"].dtype)]).reshape(nt, P).T),
        "L0_rel_t": np.ascontiguousarray(v["L0_gnn_W_rel"].T),
        "L0_root_t": np.ascontiguousarray(v["L0_gnn_W_root"].T),
        "L3_b_cols": np.ascontiguousarray(np.stack([v["L3_gnn_b_conv"][0], v["L3_gnn_b_skip"][0]], 1)),
    }
    for n in ("L0_gnn_b_rel", "L2_gnn_msg_b", "L2_gnn_upd_b", "L2_gnn_gate_b"):
        arrays[n] = v[n].reshape(1, -1)
    for n in ("L1_gnn_W_up_s", "L1_gnn_W_up_v", "L1_gnn_W_r1", "L1_gnn_W_r2", "L1_gnn_W_down_s",
              "L1_gnn_W_down_v", "L1_gnn_W_skip_s", "L1_gnn_W_skip_v", "L2_gnn_msg_w", "L2_gnn_msg_g",
              "L2_gnn_msg_beta", "L2_gnn_upd_w", "L2_gnn_upd_g", "L2_gnn_upd_beta", "L2_gnn_gate_w",
              "L3_gnn_w_rel", "L3_gnn_w_root", "L3_gnn_w_skip", "L3_gnn_b_conv", "L3_gnn_b_skip"):
        arrays[n] = v[n]

    nc = bacc.Bacc("TRN2", target_bir_lowering=False, num_devices=1)
    aps, feed = {}, {}
    for n, q in arrays.items():
        feed["in_" + n] = q
        aps[n] = nc.dram_tensor("in_" + n, q.shape, mybir.dt.from_np(q.dtype), kind="ExternalInput").ap()
    result = nc.dram_tensor("out", (N, P), F32, kind="ExternalOutput").ap()
    build(nc, aps, result, (N, E))
    r = run_bass_kernel_spmd(nc, [feed], core_ids=[0])
    return r.results[0]["out"]
```

```python
from contextlib import ExitStack

import numpy as np

import concourse.bass as bass
from concourse import mybir

P = 128
GROUP = 4
BATCH_GROUPS = 4
SLOTS = 8
TURN_BATCHES = 4
TURN_GROUPS = TURN_BATCHES * BATCH_GROUPS
BATCH_TILES = BATCH_GROUPS * GROUP
TURN_TILES = TURN_GROUPS * GROUP
WINDOW = 48
GROUP_EDGES = GROUP * P
BATCH_EDGES = BATCH_TILES * P
TURN_EDGES = TURN_TILES * P
FAR = float(1 << 21)
EPS = 1e-5

C = 32
R = 8
SPECIES = 5
SKIP = 2 * C + 3 * C
DEG = 16.0
REL = 3

F32 = mybir.dt.float32
I32 = mybir.dt.int32
BF16 = mybir.dt.bfloat16
ALU = mybir.AluOpType
ACT = mybir.ActivationFunctionType
AX = mybir.AxisListType.X


class Counter:

    def __init__(self, sem, credit=False):
        self.sem = sem
        self.value = 0
        self.credit = credit


class Prev:

    def __init__(self, key):
        self.key = key


def ring(name, i, size, turn=None):
    name = name if isinstance(name, tuple) else (name,)
    if i >= size:
        return (*name, i - size)
    return Prev((*name, i - size + turn)) if turn else None


class Stage:

    def __init__(self, counters, ticks=None):
        self.counters = counters
        self.ticks = ticks or {}
        self.queues = {name: [] for name in ("sync", "scalar", "vector", "gpsimd", "tensor")}
        self.steps = {}

    def wait(self, engine, *keys):
        for key in keys:
            if key is not None:
                self.queues[engine].append(("wait", key))

    def do(self, engine, key, fn, *after, by=1, counter=None):
        self.wait(engine, *after)
        c = self.counters[counter or engine]
        c.value += by
        self.queues[engine].append(("do", fn, c, by))
        if key is not None:
            self.steps[key] = (c, c.value)

    def dma(self, engine, key, counter, fn, *after):
        self.do(engine, key, fn, *after, by=16, counter=counter)

    def straight(self, nc):
        with nc.Block() as block:
            for name, queue in self.queues.items():
                if queue:
                    getter = {"sync": block.sync, "scalar": block.scalar, "vector": block.vector,
                              "gpsimd": block.gpsimd, "tensor": block.tensor}[name]

                    @getter
                    def _(e, queue=queue):
                        seen = {}
                        for item in queue:
                            if item[0] == "wait":
                                c, value = self.steps[item[1]]
                                if seen.get(c, 0) < value:
                                    e.wait_ge(c.sem, value)
                                    seen[c] = value
                            else:
                                _, fn, c, by = item
                                fn(e).then_inc(c.sem, by)

    def turn(self, e, engine, it):
        seen, pending = {}, {}
        for item in self.queues[engine]:
            if item[0] == "wait":
                prev = isinstance(item[1], Prev)
                c, value = self.steps[item[1].key if prev else item[1]]
                assert c.credit or not prev
                at = value + c.value if c.credit and not prev else value
                if seen.get(c, 0) < at:
                    seen[c] = pending[c] = at
                continue
            values = [(c.sem, e.snap(it * c.value + at)) for c, at in pending.items()]
            for sem, value in values:
                e.wait_ge(sem, value)
            if pending and engine in self.ticks:
                e.sem_inc(self.ticks[engine], 1)
            pending = {}
            _, fn, c, by = item
            fn(e, it).then_inc(c.sem, by)


def build(nc, a, out, shapes):
    N, E = shapes
    NT = -(-N // P)
    REST = N - (NT - 1) * P
    TURNS = -(-E // TURN_EDGES)
    BATCHES = TURN_BATCHES * TURNS
    GROUPS = TURNS * TURN_GROUPS
    TILES = TURNS * TURN_TILES
    MOST_PASSES = -(-N // WINDOW)
    ACC = (NT + 1) * P

    top = ExitStack()
    with top:
        def dram(name, shape, dt=F32):
            return nc.dram_tensor(name, shape, dt, kind="Internal").ap()

        names = {}

        def own(name):
            names[name] = names.get(name, 0) + 1
            return name if names[name] == 1 else f"{name}_{names[name]}"

        def sb(stack, name, shape, dt=F32):
            return stack.enter_context(nc.sbuf_tensor(own(name), shape, dt))

        def ps(stack, name, shape):
            return stack.enter_context(nc.psum_tensor(own(name), shape, F32))

        table = dram("table", (N, P))
        rel_table = dram("rel_table", (REL * N, P))
        window_table = dram("window_table", (ACC, P))
        base_dram = dram("base_dram", (1, GROUPS))
        span_dram = dram("span_dram", (1, BATCHES))
        local_cols = dram("local_cols", (P, TILES))
        local_rows = dram("local_rows", (BATCHES, BATCH_EDGES))
        rel_cols = dram("rel_cols", (P, TILES), I32)

        x = sb(top, "x", [P, NT, P])
        acc = sb(top, "acc", [P, 2, ACC])
        ident = sb(top, "ident", [P, P])
        ones = sb(top, "ones", [P, P])
        zero = sb(top, "zero", [P, P])
        iota = sb(top, "iota", [P, WINDOW])
        iota_col = sb(top, "iota_col", [P, 1])
        iota_pass = sb(top, "iota_pass", [P, WINDOW])
        iota_col_pass = sb(top, "iota_col_pass", [P, 1])
        base_row = sb(top, "base_row", [1, GROUPS])
        base_pass = sb(top, "base_pass", [1, GROUPS])
        address = sb(top, "address", [1, GROUPS], I32)
        passes = sb(top, "passes", [1, 1], I32)
        rcount = sb(top, "rcount", [P, NT])
        species = sb(top, "species", [P, NT, SPECIES])
        gate = sb(top, "gate", [P, NT])
        stat = sb(top, "stat", [P, NT, 2])
        rstd = sb(top, "rstd", [P, NT])
        shift = sb(top, "shift", [P, NT])

        straight = {n: Counter(top.enter_context(nc.semaphore(f"done_{n}")))
                    for n in ("sync", "scalar", "vector", "gpsimd", "tensor")}
        NLOAD, STORES = 12, 8
        for n in [f"load{i}" for i in range(NLOAD)] + [f"store{i}" for i in range(STORES)]:
            straight[n] = Counter(top.enter_context(nc.semaphore(n)))
        loop_sems = {n: top.enter_context(nc.semaphore(f"turn_{n}"))
                     for n in ["scalar", "vector", "tensor"] + [f"slot{i}" for i in range(SLOTS)]
                     + [f"idx{i}" for i in range(TURN_BATCHES)] + [f"edge{i}" for i in range(TURN_BATCHES)]
                     + [f"near{i}" for i in range(4)]}
        arrived = top.enter_context(nc.semaphore("arrived"))
        ticks = {n: top.enter_context(nc.semaphore(f"waited_{n}")) for n in ("gpsimd", "sync")}

        stores = [0]

        def store(s, key, fn, *after):
            i = stores[0] % STORES
            stores[0] += 1
            s.dma("sync", key, f"store{i}", fn, *after, *( [last_store[i]] if last_store.get(i) in s.steps else []))
            last_store[i] = key

        last_store = {}

        def staggered(*steps, count=TURN_GROUPS):
            for k in range(count + max(lag for lag, _ in steps)):
                for lag, step in steps:
                    if 0 <= k - lag < count:
                        step(k - lag)

        CHUNK, SMALL_CHUNK = 14, 4

        def invert_deviations(s, tag, i, chunk):
            if (i + 1) % chunk and i != NT - 1:
                return
            t = slice(i // chunk * chunk, i + 1)
            s.do("vector", (tag, "eps", i), lambda e: e.tensor_scalar(
                rstd[:, t], stat[:, t, 1], EPS, None, ALU.add), (tag, "stat", i))
            s.do("scalar", (tag, "std", i), lambda e: e.activation(
                rstd[:, t], rstd[:, t], ACT.Sqrt), (tag, "eps", i))
            s.do("vector", (tag, "rstd", i), lambda e: e.reciprocal(rstd[:, t], rstd[:, t]), (tag, "std", i))
            s.do("vector", None, lambda e: e.scalar_tensor_tensor(
                out=shift[:, t], in0=stat[:, t, 0], scalar=-1.0, in1=rstd[:, t], op0=ALU.mult,
                op1=ALU.mult), (tag, "rstd", i))
            for k in range(t.start, t.stop):
                s.steps[(tag, "norm", k)] = (straight["vector"], straight["vector"].value)

        def statistics(s, bn, i, src, ready, tag="x"):
            s.do("vector", (tag, "bn", i), lambda e: e.bn_stats(bn[:, i % 4, :], src), ready,
                 ring((tag, "stat"), i, 4))

        def aggregate(s, bn, i, tag="x", chunk=CHUNK):
            s.do("vector", (tag, "stat", i), lambda e: e.bn_aggr(stat[:, i, :], bn[:, i % 4, :]),
                 (tag, "bn", i))
            invert_deviations(s, tag, i, chunk)

        def vectors_last(ap):
            return ap.rearrange("p (c k) -> p k c", k=3)

        HR = 5

        def normed(s, h, i, by_component=False, user=None, tag="x"):
            def relu(dst, src):
                return lambda e: e.activation(dst, src, ACT.Relu, bias=shift[:, i:i + 1],
                                              scale=rstd[:, i:i + 1])
            s.wait("scalar", (tag, "norm", i) if (tag, "norm", i) in s.steps else None,
                   ring("h_turned", i, HR), ring(user, i, HR) if user else None)
            if not by_component:
                s.do("scalar", ("h", i), relu(h[:, i % HR, :], x[:, i, :]))
            else:
                s.do("scalar", None, relu(h[:, i % HR, 0:C], x[:, i, 0:C]))
                s.do("scalar", ("h", i), relu(
                    h[:, i % HR, C:P].rearrange("p (k c) -> p k c", k=3),
                    vectors_last(x[:, i, C:P])))

        def turn_h(s, h, pT, i):
            s.do("tensor", ("h_turned", i), lambda e: e.transpose(
                pT[:, i % 2, 0:P], h[:, i % HR, :], ident[:, :]), ("h", i), ring("hT", i, 2))

        def keep_hT(s, pT, hT, i):
            s.do("vector", ("hT", i), lambda e: e.tensor_copy(hT[:, i % 3, :], pT[:, i % 2, 0:P]),
                 ("h_turned", i), ring("hT_used", i, 3))

        def rows(i):
            return REST if i == NT - 1 else P

        def load_weights(st, specs):
            tiles, s = {}, Stage(straight)
            for n, (name, shape, parts) in enumerate(specs):
                tiles[name] = t = sb(st, name, shape)
                if parts[0][2] is not None:
                    s.do("gpsimd", ("zeroed", name), lambda e, t=t: e.memset(t[:], 0.0))
                for m, (dst, src, _) in enumerate(parts):
                    s.dma("sync", ("loaded", name), f"load{n % NLOAD}",
                          lambda e, d=dst, q=src, t=t: e.dma_start(d(t), q),
                          *([("zeroed", name)] if parts[0][2] is not None else []))
            for name, *_ in specs:
                s.wait("sync", ("loaded", name))
            s.straight(nc)
            return tiles

        def whole(name, shape, src):
            return (name, shape, [(lambda t: t[:], src, None)])

        def message_stage(name, body, source, index_cols, extra_cols, st, near=False):
            s = Stage(straight)
            s.do("vector", ("base", name), lambda e: e.tensor_copy(base_pass[:, :], base_row[:, :]))
            s.do("vector", ("address", name), lambda e: e.tensor_scalar(
                address[:, :], base_pass[:, :], float(N), None, ALU.min), ("base", name))
            s.do("vector", None, lambda e: e.tensor_copy(iota_pass[:, :], iota[:, :]))
            s.do("vector", ("reset", name), lambda e: e.tensor_copy(iota_col_pass[:, :], iota_col[:, :]))
            s.wait("vector", ("reset", name))
            s.straight(nc)

            engines = ("scalar", "vector", "tensor")
            counters = {n: Counter(v, n in engines) for n, v in loop_sems.items()}
            s = Stage(counters, ticks)
            gathered = sb(st, "gathered_" + name, [P, SLOTS, GROUP, P])
            index = sb(st, "index_" + name, [P, TURN_BATCHES, BATCH_TILES], I32)

            def stage_edges(b):
                groups = range(b * BATCH_GROUPS, (b + 1) * BATCH_GROUPS)
                s.dma("sync", ("index", b), f"idx{b}", lambda e, it: e.dma_start(
                    index[:, b, :], index_cols[:, bass.ds(it * TURN_TILES + b * BATCH_TILES, BATCH_TILES)]),
                    *[Prev(("rows_used", g)) for g in groups])
                s.wait("sync", *[Prev(("edges_used", g)) for g in groups])
                for tile, src in extra_cols:
                    s.dma("sync", ("edges", b), f"edge{b}",
                          lambda e, it, tile=tile, src=src: e.dma_start(tile[:, b], src(it, b)))

            def gather(g):
                b, k = g // BATCH_GROUPS, g % BATCH_GROUPS
                s.wait("gpsimd", ("index", b), ring("rows_used", g, SLOTS, TURN_GROUPS))
                for t in range(GROUP):
                    s.dma("gpsimd", ("gathered", g), f"slot{g % SLOTS}", lambda e, it, t=t: e.indirect_dma_start(
                        gathered[:, g % SLOTS, t, :], None, source[:, :], bass.IndirectOffsetOnAxis(
                            ap=index[:, b, k * GROUP + t:k * GROUP + t + 1], axis=0)))

            for b in range(TURN_BATCHES + 1):
                if b < TURN_BATCHES:
                    stage_edges(b)
                if near and b:
                    for g in range((b - 1) * BATCH_GROUPS, b * BATCH_GROUPS):
                        near(s, g)
            for g in range(TURN_GROUPS):
                gather(g)
            body(s, gathered)
            used = [n for n, c in counters.items() if c.value]

            go = top.enter_context(nc.semaphore("go_" + name))
            with nc.Block() as block:
                getters = {"sync": block.sync, "scalar": block.scalar, "vector": block.vector,
                           "gpsimd": block.gpsimd, "tensor": block.tensor}
                for engine in getters:
                    @getters[engine]
                    def _(e, engine=engine):
                        count = e.value_load(passes[0:1, 0:1], min_val=1, max_val=MOST_PASSES)
                        with e.Fori(0, count) as turn_of_pass:
                            if engine in engines and counters[engine].value:
                                e.sem_inc(counters[engine].sem, counters[engine].value)
                            with e.Fori(0, TURNS) as it:
                                s.turn(e, engine, it)
                            if engine in engines and counters[engine].value:
                                e.wait_ge(counters[engine].sem, counters[engine].value * (TURNS + 1))
                            if engine == "vector":
                                e.tensor_scalar(iota_pass[:, :], iota_pass[:, :], float(WINDOW), None, ALU.add).then_inc(counters["vector"].sem, 1)
                                e.tensor_scalar(iota_col_pass[:, :], iota_col_pass[:, :], float(WINDOW), None, ALU.add).then_inc(counters["vector"].sem, 1)
                                e.tensor_scalar(base_pass[:, :], base_pass[:, :], float(WINDOW), None, ALU.add).then_inc(counters["vector"].sem, 1)
                                at = counters["vector"].value * (TURNS + 1)
                                e.wait_ge(counters["vector"].sem, at + 3)
                                e.tensor_scalar(address[:, :], base_pass[:, :], float(N), None, ALU.min).then_inc(counters["vector"].sem, 1)
                                e.wait_ge(counters["vector"].sem, at + 4)
                            if engine == "gpsimd":
                                slots = [loop_sems[f"slot{k}"] for k in range(SLOTS)]
                                for slot in slots:
                                    e.wait_ge(slot, 16 * GROUP * (TURN_GROUPS // SLOTS) * TURNS)
                                e.dma_reset(range(slots[0].num, slots[-1].num + 1))
                            if engine != "sync":
                                e.sem_inc(arrived, 1)
                                e.wait_ge(go, turn_of_pass + 1)
                            else:
                                e.wait_ge(arrived, 4)
                                for n in used:
                                    e.sem_clear(counters[n].sem)
                                e.sem_clear(arrived)
                                for tick in ticks.values():
                                    e.sem_clear(tick)
                                e.sem_inc(go, 1)

        def column(src):
            return lambda it, b: src[:, bass.ds(it * TURN_TILES + b * BATCH_TILES, BATCH_TILES)]

        def place(g):
            return g // BATCH_GROUPS, (g % BATCH_GROUPS) * GROUP

        def select(s, sel, local, g):
            b, at = place(g)
            s.do("vector", ("hit", g), lambda e, it: e.tensor_tensor(
                sel[:, g % 4, :, :], iota_pass[:, :].unsqueeze(1).to_broadcast([P, GROUP, WINDOW]),
                local[:, b, at:at + GROUP].unsqueeze(2).to_broadcast([P, GROUP, WINDOW]), ALU.is_equal),
                ("edges", b), ring("summed", g, 4, TURN_GROUPS))

        def weigh(s, sel, weight, g):
            b, at = place(g)
            s.do("vector", ("weighed", g), lambda e, it: e.tensor_tensor(
                sel[:, g % 4, :, :], sel[:, g % 4, :, :],
                weight[:, b, at:at + GROUP].unsqueeze(2).to_broadcast([P, GROUP, WINDOW]), ALU.mult),
                ("hit", g))

        def accumulate(s, psum, g, n=1):
            def add(e, it):
                at = e.value_load(address[0:1, bass.ds(it * TURN_GROUPS + g, 1)], min_val=0, max_val=N)
                sums = acc[:, 0:n, bass.ds(at, WINDOW)]
                return e.tensor_tensor(sums, sums, psum, ALU.add)
            s.do("vector", ("added", g), add, ("summed", g), ring("added", g, 1, TURN_GROUPS))


        def plain_messages(name, source, index_cols, weight_cols=None, counts=False):
            with ExitStack() as st:
                local = sb(st, "local_" + name, [P, TURN_BATCHES, BATCH_TILES])
                weight = sb(st, "weight_" + name, [P, TURN_BATCHES, BATCH_TILES]) if weight_cols is not None else None
                sel = sb(st, "select_" + name, [P, 4, GROUP, WINDOW])
                sums = ps(st, "sums_" + name, [P, 4, 512])
                extra = [(local, column(local_cols))]
                if weight is not None:
                    extra.append((weight, column(weight_cols)))
                n = 2 if counts else 1

                def body(s, gathered):
                    def multiply(g):
                        s.wait("tensor", ("gathered", g), ("hit", g) if weight is None else ("weighed", g),
                               ring("added", g, 4, TURN_GROUPS))
                        for t in range(GROUP):
                            s.do("tensor", ("summed", g), lambda e, it, t=t: e.matmul(
                                sums[:, g % 4, 0:WINDOW], gathered[:, g % SLOTS, t, :], sel[:, g % 4, t, :],
                                start=t == 0, stop=t == GROUP - 1))
                        s.steps[("rows_used", g)] = s.steps[("summed", g)]
                        if counts:
                            for t in range(GROUP):
                                s.do("tensor", ("summed", g), lambda e, it, t=t: e.matmul(
                                    sums[:, g % 4, WINDOW:2 * WINDOW], ones[:, :], sel[:, g % 4, t, :],
                                    start=t == 0, stop=t == GROUP - 1))
                        s.steps[("edges_used", g)] = s.steps[("summed", g)]

                    steps = [(0, lambda g: select(s, sel, local, g))]
                    if weight is not None:
                        steps.append((1, lambda g: weigh(s, sel, weight, g)))
                    staggered(*steps, (1, multiply),
                              (3, lambda g: accumulate(s, sums[:, g % 4, 0:n * WINDOW].rearrange(
                                  "p (n w) -> p n w", n=n), g, n)))

                message_stage(name, body, source, index_cols, extra, st)

        def clear_accumulator(s, n, key):
            for k in range(n):
                s.do("gpsimd", key, lambda e, k=k: e.memset(acc[:, k, :], 0.0))

        with ExitStack() as st:
            dst_i = sb(st, "dst_i", [BATCHES, BATCH_EDGES], I32)
            dst_f = sb(st, "dst_f", [BATCHES, BATCH_EDGES])
            dst_far = sb(st, "dst_far", [BATCHES, BATCH_EDGES])
            base_g = sb(st, "base_g", [BATCHES, BATCH_GROUPS])
            last_g = sb(st, "last_g", [BATCHES, BATCH_GROUPS])
            span_g = sb(st, "span_g", [BATCHES, 1])
            span_row = sb(st, "span_row", [1, BATCHES])
            firsts = sb(st, "firsts", [1, MOST_PASSES])
            span_f = sb(st, "span_f", [1, 1])
            s = Stage(straight)
            s.do("gpsimd", None, lambda e: e.memset(x[:, NT - 1, :], 0.0))
            s.do("gpsimd", "ident0", lambda e: e.memset(ident[:, :], 0.0))
            s.do("gpsimd", "ident", lambda e: e.affine_select(
                out=ident[:, :], in_=ident[:, :], compare_op=ALU.not_equal, fill=1.0, base=0,
                pattern=[[-1, P]], channel_multiplier=1), "ident0")
            s.do("gpsimd", None, lambda e: e.memset(ones[:, :], 1.0))
            s.do("gpsimd", None, lambda e: e.memset(zero[:, :], 0.0))
            s.do("gpsimd", None, lambda e: e.iota(iota[:, :], [[1, WINDOW]], base=0, channel_multiplier=0,
                                                  allow_small_or_imprecise_dtypes=True))
            s.do("gpsimd", "constants", lambda e: e.iota(iota_col[:, :], [[0, 1]], base=0,
                                                         channel_multiplier=1,
                                                         allow_small_or_imprecise_dtypes=True))
            s.do("gpsimd", "firsts", lambda e: e.iota(
                firsts[:, :], [[WINDOW, MOST_PASSES]], base=0, channel_multiplier=0,
                allow_small_or_imprecise_dtypes=True))
            clear_accumulator(s, 2, "cleared")
            s.dma("sync", "dst_g", "load0", lambda e: e.dma_start(dst_i[:, :], a["dst_rows"]))
            s.dma("sync", "x", "load5", lambda e: e.dma_start(
                x[:, 0:NT - 1, :], a["x"][0:(NT - 1) * P, :].rearrange("(t p) f -> p t f", p=P)))
            s.dma("sync", "x", "load5", lambda e: e.dma_start(
                x[0:REST, NT - 1, :], a["x"][(NT - 1) * P:N, :]), "constants")
            grouped = lambda t: t[:, :].rearrange("h (g e) -> h g e", g=BATCH_GROUPS)
            s.do("vector", "dst_f", lambda e: e.tensor_copy(dst_f[:, :], dst_i[:, :]), "dst_g")
            s.do("vector", "far", lambda e: e.tensor_scalar(
                dst_far[:, :], dst_f[:, :], 0.0, FAR, ALU.is_lt, ALU.mult), "dst_f")
            s.do("vector", "dst_far", lambda e: e.tensor_tensor(
                dst_far[:, :], dst_far[:, :], dst_f[:, :], ALU.add), "far")
            s.do("vector", "base_g", lambda e: e.tensor_reduce(
                base_g[:, :], grouped(dst_far), AX, ALU.min), "dst_far")
            s.do("vector", "last_g", lambda e: e.tensor_reduce(
                last_g[:, :], grouped(dst_f), AX, ALU.max), "dst_f")
            s.do("vector", "last_less", lambda e: e.tensor_tensor(
                last_g[:, :], last_g[:, :], base_g[:, :], ALU.subtract), "base_g", "last_g")
            s.do("vector", "span_g", lambda e: e.tensor_reduce(
                span_g[:, :], last_g[:, :], AX, ALU.max), "last_less")
            s.do("vector", "local_rows", lambda e: e.tensor_tensor(
                grouped(dst_far), grouped(dst_f),
                base_g[:, :].unsqueeze(2).to_broadcast([BATCHES, BATCH_GROUPS, GROUP_EDGES]),
                ALU.subtract), "base_g")
            s.dma("sync", "base_out", "store0", lambda e: e.dma_start(
                base_dram[0, :].rearrange("(h g) -> h g", g=BATCH_GROUPS), base_g[:, :]), "base_g")
            s.dma("sync", "span_out", "store1", lambda e: e.dma_start(
                span_dram[0, :].unsqueeze(1), span_g[:, :]), "span_g")
            s.dma("sync", "rows_out", "store2", lambda e: e.dma_start(local_rows, dst_far[:, :]), "local_rows")
            s.dma("sync", "base_row", "load7", lambda e: e.dma_start(base_row[:, :], base_dram), "base_out")
            s.dma("sync", "span_row", "load8", lambda e: e.dma_start(span_row[:, :], span_dram), "span_out")
            s.do("vector", "span_f", lambda e: e.tensor_reduce(span_f[:, :], span_row[:, :], AX, ALU.max), "span_row")
            s.do("vector", "reached", lambda e: e.tensor_scalar(
                firsts[:, :], firsts[:, :], span_f[:, 0:1], None, ALU.is_le), "span_f", "firsts")
            s.do("vector", "reached_n", lambda e: e.tensor_reduce(
                span_f[:, :], firsts[:, :], AX, ALU.add), "reached")
            s.do("vector", "passes", lambda e: e.tensor_scalar(
                passes[:, :], span_f[:, :], 1.0, None, ALU.max), "reached_n")
            s.wait("vector", "passes", "local_rows")
            s.wait("sync", "rows_out", "span_out", "base_out", "base_row", "x")
            s.wait("gpsimd", "cleared")
            s.straight(nc)

        with ExitStack() as st:
            col_i = sb(st, "col_i", [P, TILES], I32)
            type_i = sb(st, "type_i", [P, TILES], I32)
            src_i = sb(st, "src_i", [P, TILES], I32)
            col_f = sb(st, "col_f", [P, TILES])
            src_f = sb(st, "src_f", [P, TILES])
            base_all = sb(st, "base_all", [P, GROUPS])
            kind_i = sb(st, "kind_i", [P, NT], I32)
            bn = sb(st, "bn0", [P, 4, 6])
            s = Stage(straight)
            s.dma("sync", "dst_c", "load1", lambda e: e.dma_start(col_i[:, :], a["dst_cols"]))
            s.dma("sync", "type_c", "load2", lambda e: e.dma_start(type_i[:, :], a["type_cols"]))
            s.dma("sync", "src_c", "load3", lambda e: e.dma_start(src_i[:, :], a["src_cols"]))
            s.dma("sync", "kind", "load4", lambda e: e.dma_start(kind_i[:, :], a["node_type"]))
            s.dma("sync", "base_all", "load6", lambda e: e.dma_start(
                base_all[:, :], base_dram[0, :].partition_broadcast(P)))
            s.do("vector", "col_f", lambda e: e.tensor_copy(col_f[:, :], col_i[:, :]), "dst_c")
            s.do("vector", "local_cols", lambda e: e.tensor_tensor(
                col_f[:, :].rearrange("p (g t) -> p g t", t=GROUP),
                col_f[:, :].rearrange("p (g t) -> p g t", t=GROUP),
                base_all[:, :].unsqueeze(2).to_broadcast([P, GROUPS, GROUP]), ALU.subtract), "col_f", "base_all")
            s.dma("sync", "cols_out", "store3", lambda e: e.dma_start(local_cols, col_f[:, :]), "local_cols")
            s.do("vector", "src_f", lambda e: e.tensor_copy(src_f[:, :], src_i[:, :]), "src_c")
            s.do("vector", "rel", lambda e: e.scalar_tensor_tensor(
                out=type_i[:, :], in0=type_i[:, :], scalar=float(N), in1=src_f[:, :],
                op0=ALU.mult, op1=ALU.add), "src_f", "type_c")
            s.dma("sync", "rel_out", "store0", lambda e: e.dma_start(rel_cols, type_i[:, :]), "rel")
            for k in range(SPECIES):
                s.do("vector", None, lambda e, k=k: e.tensor_scalar(
                    species[:, :, k], kind_i[:, :], float(k), None, ALU.is_equal), "kind")
            staggered((0, lambda i: statistics(s, bn, i, x[:, i, :], None)),
                      (2, lambda i: aggregate(s, bn, i)), count=NT)
            s.wait("vector", ("x", "norm", NT - 1))
            s.wait("sync", "cols_out", "rel_out")
            s.straight(nc)

        with ExitStack() as st:
            w = load_weights(st, [whole("root0", [P, P], a["L0_root_t"]),
                                  whole("brel", [P, P], a["L0_gnn_b_rel"].partition_broadcast(P))])
            h, hT = sb(st, "h", [P, HR, P]), sb(st, "hT", [P, 3, P])
            pT, pm = ps(st, "pT", [P, 2, 512]), ps(st, "pm", [P, 4, 512])
            s = Stage(straight)

            def normalise(i):
                normed(s, h, i, user="h_out")
                store(s, ("h_out", i), lambda e: e.dma_start(
                    table[i * P:i * P + rows(i), :], h[0:rows(i), i % HR, :]), ("h", i))
                s.do("gpsimd", ("biased", i), lambda e: e.tensor_tensor(
                    x[:, i, :], x[:, i, :], w["brel"][:, :], ALU.add), ("h", i))

            def multiply(i):
                s.do("tensor", ("hT_used", i), lambda e: e.matmul(
                    pm[:, i % 4, 0:P], hT[:, i % 3, :], w["root0"][:, :], start=True, stop=True),
                    ("hT", i), ring("root", i, 4))

            def add(i):
                s.do("vector", ("root", i), lambda e: e.tensor_tensor(
                    x[:, i, :], x[:, i, :], pm[:, i % 4, 0:P], ALU.add), ("hT_used", i), ("biased", i))

            staggered((0, normalise), (1, lambda i: turn_h(s, h, pT, i)), (3, add),
                      (1, lambda i: keep_hT(s, pT, hT, i)), (2, multiply), count=NT)
            s.wait("sync", *[("h_out", i) for i in range(max(0, NT - STORES), NT)])
            s.wait("vector", ("root", NT - 1))
            s.straight(nc)

        with ExitStack() as st:
            w = load_weights(st, [
                whole("rel0", [P, P], a["L0_rel_t"]),
                ("up", [P, P], [(lambda t: t[0:C, 0:C], a["L1_gnn_W_up_s"], 0)] + [
                    (lambda t, k=k: t[C * k:C * (k + 1), C * k:C * (k + 1)], a["L1_gnn_W_up_v"], 0)
                    for k in (1, 2, 3)])])
            plain_messages("sum0", table, a["src_cols"], counts=True)

            h, hT = sb(st, "h", [P, HR, P]), sb(st, "hT", [P, 3, P])
            rowbuf = sb(st, "rowbuf", [P, 4, P])
            cnt = sb(st, "cnt", [P, NT])
            bn = sb(st, "bn1", [P, 4, 6])
            pT, pm = ps(st, "pT", [P, 2, 512]), ps(st, "pm", [P, 2, 512])
            pr, pc = ps(st, "pr", [P, 3, 512]), ps(st, "pc", [P, NT])
            s = Stage(straight)
            s.do("vector", "up_scaled", lambda e: e.tensor_scalar(w["up"][:, :], w["up"][:, :], C ** -0.5, None, ALU.mult))

            def relate(i):
                nodes = slice(i * P, (i + 1) * P)
                s.do("tensor", ("rel", i), lambda e: e.matmul(
                    pr[:, i % 3, 0:P], acc[:, 0, nodes], w["rel0"][:, :], start=True, stop=True),
                    ring("x1", i, 3))
                s.do("tensor", ("count", i), lambda e: e.matmul(
                    pc[:, i:i + 1], acc[0:1, 1, nodes], ones[0:1, 0:1], start=True, stop=True))

            def add(i):
                s.do("vector", ("x1", i), lambda e: e.tensor_tensor(
                    x[:, i, :], x[:, i, :], pr[:, i % 3, 0:P], ALU.add), ("rel", i))

            def up(i):
                s.do("tensor", ("hT_used", i), lambda e: e.matmul(
                    pm[:, i % 2, 0:P], hT[:, i % 3, :], w["up"][:, :], start=True, stop=True),
                    ("hT", i), "up_scaled", ring("row", i, 2))

            def send(i):
                s.do("scalar", ("row", i), lambda e: e.activation(
                    rowbuf[:, i % 4, :], pm[:, i % 2, 0:P], ACT.Copy), ("hT_used", i), ring("row_out", i, 4))
                store(s, ("row_out", i), lambda e: e.dma_start(
                    table[i * P:i * P + rows(i), :], rowbuf[0:rows(i), i % 4, :]), ("row", i))

            L = SMALL_CHUNK + 4
            staggered((0, relate), (1, add), (2, lambda i: statistics(s, bn, i, x[:, i, :], ("x1", i))),
                      (L, lambda i: normed(s, h, i, by_component=True)),
                      (L + 1, lambda i: turn_h(s, h, pT, i)), (L + 2, up), (L + 3, send),
                      (3, lambda i: aggregate(s, bn, i, chunk=SMALL_CHUNK)),
                      (L + 1, lambda i: keep_hT(s, pT, hT, i)), count=NT)
            s.do("vector", "cnt", lambda e: e.tensor_scalar(cnt[:, :], pc[:, :], 1e-8, None, ALU.add), ("count", NT - 1))
            s.do("vector", "rcnt", lambda e: e.reciprocal(rcount[:, :], cnt[:, :]), "cnt")
            s.do("vector", "valid", lambda e: e.tensor_scalar(cnt[:, :], pc[:, :], 0.0, None, ALU.is_gt), "rcnt")
            s.do("vector", "rcount", lambda e: e.tensor_tensor(rcount[:, :], rcount[:, :], cnt[:, :], ALU.mult), "valid")
            for i in range(CHUNK - 1, NT, CHUNK):
                s.wait("gpsimd", ("count", i))
                for k in range(2):
                    s.do("gpsimd", "cleared", lambda e, i=i, k=k: e.memset(acc[:, k, (i + 1 - CHUNK) * P:(i + 1) * P], 0.0))
            s.wait("gpsimd", ("count", NT - 1))
            for k in range(2):
                s.do("gpsimd", "cleared", lambda e, k=k: e.memset(acc[:, k, NT // CHUNK * CHUNK * P:ACC], 0.0))
            s.wait("sync", *[("row_out", i) for i in range(max(0, NT - STORES), NT)])
            s.wait("gpsimd", "cleared")
            s.straight(nc)

        with ExitStack() as st:
            w = load_weights(st, [
                ("radial", [P, P], [(lambda t, k=k: t[R * k:R * (k + 1), R * k:R * (k + 1)], a["L1_gnn_W_r1"], 0)
                                    for k in range(BATCH_TILES)]),
                ("paths", [P, GROUP, 4 * C], [(lambda t, k=k: t[R * k:R * (k + 1), k % GROUP, :], a["L1_gnn_W_r2"], 0)
                                              for k in range(BATCH_TILES)])])
            local = sb(st, "local_1", [P, TURN_BATCHES, BATCH_TILES])
            sh = sb(st, "sh", [P, TURN_BATCHES, BATCH_TILES * 4])
            radial_in = sb(st, "radial_in", [P, TURN_BATCHES, P])
            hidden = sb(st, "hidden", [P, 2, P])
            hit = sb(st, "hit", [P, 4, GROUP, WINDOW], BF16)
            sel = sb(st, "sel_1", [P, 4, GROUP, WINDOW])
            mess = sb(st, "mess", [P, 2, GROUP, 2 * P])
            along = sb(st, "along", [P, 2, GROUP, 3 * C])
            dot = sb(st, "dot", [P, 2, GROUP, C])
            rest = sb(st, "rest", [P, 2, GROUP, P])
            last_bits = sb(st, "last_bits", [P, 2, GROUP, P], BF16)

            def high(ap):
                return ap.bitcast(BF16).rearrange("p (f e) -> p f e", e=2)[:, :, 1]

            PART = 64
            p_hidden = ps(st, "p_hidden", [P, 512])
            p_path = ps(st, "p_path", [P, 2, GROUP * 4 * C])
            sums = ps(st, "sums_1", [P, 4, 512])
            s = Stage(straight)
            s.do("vector", "p", lambda e: e.tensor_scalar(w["paths"][:, :, :], w["paths"][:, :, :], R ** -0.5, None, ALU.mult))
            s.do("vector", "p3", lambda e: e.tensor_scalar(w["paths"][:, :, 3 * C:], w["paths"][:, :, 3 * C:], 3.0 ** -0.5, None, ALU.mult), "p")
            s.wait("vector", "p3")
            s.straight(nc)

            def body(s, gathered):
                def radial(g):
                    if g % BATCH_GROUPS:
                        return
                    b = g // BATCH_GROUPS
                    s.do("tensor", ("radial", b), lambda e, it: e.matmul(
                        p_hidden[:, 0:P], w["radial"][:, :], radial_in[:, b, :], start=True, stop=True),
                        ("edges", b), ring("hidden", b, 1, TURN_BATCHES))
                    s.do("scalar", ("hidden", b), lambda e, it: e.activation(
                        hidden[:, b % 2, :], p_hidden[:, 0:P], ACT.Silu, scale=R ** -0.5), ("radial", b),
                        ring("hidden_used", b, 2, TURN_BATCHES))

                def paths(g):
                    b, k = g // BATCH_GROUPS, g % BATCH_GROUPS
                    part = slice(GROUP * R * k, GROUP * R * (k + 1))
                    s.do("tensor", ("paths", g), lambda e, it: e.matmul(
                        p_path[:, g % 2, :], hidden[part, b % 2, :],
                        w["paths"][part, :, :].rearrange("p t c -> p (t c)"), start=True, stop=True),
                        ("hidden", b), ring("second", g, 2, TURN_GROUPS))
                    s.steps[("hidden_used", b)] = s.steps[("paths", g)]

                def find(g):
                    b, at = place(g)
                    s.do("vector", ("hit", g), lambda e, it: e.tensor_tensor(
                        hit[:, g % 4, :, :], iota_pass[:, :].unsqueeze(1).to_broadcast([P, GROUP, WINDOW]),
                        local[:, b, at:at + GROUP].unsqueeze(2).to_broadcast([P, GROUP, WINDOW]), ALU.is_equal),
                        ("edges", b), ring("selected", g, 4, TURN_GROUPS), ring("summed", g, 4, TURN_GROUPS))
                    s.wait("scalar", ("hit", g), ring("summed", g, 4, TURN_GROUPS))
                    for t in range(GROUP):
                        s.do("scalar", ("selected", g), lambda e, it, t=t: e.activation(
                            sel[:, g % 4, t, :], hit[:, g % 4, t, :], ACT.Copy,
                            scale=sh[:, b, 4 * (at + t):4 * (at + t) + 1]))

                def project(g):
                    b, at = place(g)
                    s.wait("scalar", ("gathered", g), ("edges", b), ring("dot", g, 2, TURN_GROUPS))
                    for t in range(GROUP):
                        for k in range(3):
                            col = 4 * (at + t) + 1 + k
                            s.do("scalar", ("along", g), lambda e, it, t=t, k=k, col=col: e.activation(
                                along[:, g % 2, t, C * k:C * (k + 1)],
                                gathered[:, g % SLOTS, t, C * (k + 1):C * (k + 2)], ACT.Copy,
                                scale=sh[:, b, col:col + 1]))

                def products(g):
                    b, at = place(g)
                    rows_ = gathered[:, g % SLOTS, :, :]
                    m = mess[:, g % 2, :, :].rearrange("p t (n f) -> p t n f", n=2)
                    pw = p_path[:, g % 2, :].rearrange("p (t f) -> p t f", t=GROUP)
                    by_component = lambda ap: ap.rearrange("p t (k c) -> p t k c", k=3)
                    each = lambda ap: ap.unsqueeze(2).to_broadcast([P, GROUP, 3, C])
                    y = sh[:, b, 4 * at:4 * (at + GROUP)].rearrange("p (t k) -> p t k", k=4)[:, :, 1:4] \
                        .unsqueeze(3).to_broadcast([P, GROUP, 3, C])
                    s.wait("vector", ("gathered", g), ("edges", b))
                    s.do("vector", ("scalars", g), lambda e, it: e.tensor_tensor(
                        m[:, :, :, 0:C], rows_[:, :, 0:C].unsqueeze(2).to_broadcast([P, GROUP, 2, C]),
                        pw[:, :, 0:2 * C].rearrange("p t (n c) -> p t n c", n=2), ALU.mult),
                        ("paths", g), ring("summed", g, 2, TURN_GROUPS))
                    s.do("vector", ("product", g), lambda e, it: e.tensor_tensor(
                        by_component(m[:, :, 0, C:]), by_component(rows_[:, :, C:]),
                        each(pw[:, :, 2 * C:3 * C]), ALU.mult), ("along", g))
                    s.steps[("rows_used", g)] = s.steps[("product", g)]
                    s.do("vector", ("dot", g), lambda e, it: e.tensor_reduce(
                        dot[:, g % 2, :, :], along[:, g % 2, :, :].rearrange("p t (k c) -> p t c k", k=3),
                        AX, ALU.add), ("along", g), ring("second", g, 2, TURN_GROUPS))
                    s.do("vector", ("spread", g), lambda e, it: e.tensor_tensor(
                        by_component(m[:, :, 1, C:]), each(m[:, :, 1, 0:C]), y, ALU.mult), ("scalars", g))
                    s.do("vector", ("second", g), lambda e, it: e.tensor_tensor(
                        m[:, :, 1, 0:C], dot[:, g % 2, :, :], pw[:, :, 3 * C:], ALU.mult),
                        ("dot", g), ("spread", g))

                def split(g):
                    whole_ = lambda buffer: buffer.rearrange("p t f -> p (t f)")
                    second = mess[:, g % 2, :, P:2 * P]
                    upper = mess[:, g % 2, :, :].rearrange("p t f -> p (t f)").bitcast(BF16) \
                        .rearrange("p (t f e) -> p t f e", t=GROUP, e=2)[:, :, P:2 * P, 1]
                    s.do("vector", ("rest", g), lambda e, it: e.tensor_tensor(
                        rest[:, g % 2, :, :], second, upper, ALU.subtract), ("second", g),
                        ring("summed", g, 2, TURN_GROUPS))
                    s.do("vector", ("last_bits", g), lambda e, it: e.tensor_tensor(
                        whole_(last_bits[:, g % 2, :, :]), whole_(rest[:, g % 2, :, :]),
                        high(whole_(rest[:, g % 2, :, :])), ALU.subtract), ("rest", g))

                def multiply(g):
                    s.wait("tensor", ("product", g), ("selected", g), ring("added", g, 4, TURN_GROUPS))
                    for t in range(GROUP):
                        s.do("tensor", ("first_summed", g), lambda e, it, t=t: e.matmul(
                            sums[:, g % 4, 0:WINDOW], mess[:, g % 2, t, 0:P], sel[:, g % 4, t, :],
                            start=t == 0, stop=t == GROUP - 1))
                    s.wait("tensor", ("last_bits", g))
                    for t in range(GROUP):
                        for n, bits in enumerate((high(mess[:, g % 2, t, P:2 * P]), high(rest[:, g % 2, t, :]),
                                                  last_bits[:, g % 2, t, :])):
                            s.do("tensor", ("summed", g), lambda e, it, bits=bits, t=t, n=n: e.matmul(
                                sums[:, g % 4, PART:PART + WINDOW], bits, hit[:, g % 4, t, :],
                                start=False, stop=t == GROUP - 1 and n == 2, skip_group_check=True))
                    s.steps[("edges_used", g)] = s.steps[("summed", g)]

                staggered((0, radial), (1, project), (1, paths), (3, multiply), (1, find),
                          (4, lambda g: accumulate(s, sums[:, g % 4, 0:2 * PART].rearrange(
                              "p (n w) -> p n w", n=2)[:, :, 0:WINDOW], g, 2)),
                          (2, products), (2, split))

            message_stage("messages1", body, table, a["src_cols"], [
                (local, column(local_cols)),
                (sh, lambda it, b: a["sh_cols"][:, bass.ds((it * TURN_TILES + b * BATCH_TILES) * 4, BATCH_TILES * 4)]),
                (radial_in, lambda it, b: a["radial_cols"][:, bass.ds((it * TURN_BATCHES + b) * P, P)])], st)

        local_term = acc[:, 1, 0:NT * P].rearrange("p (t f) -> p t f", f=P)
        with ExitStack() as st:
            down_s, down_v = a["L1_gnn_W_down_s"], a["L1_gnn_W_down_v"]
            specs = [("down_a", [P, SKIP], [(lambda t: t[0:C, 0:2 * C], down_s[0:C, :], 0)] + [
                        (lambda t, k=k: t[C * (k + 1):C * (k + 2), 2 * C + C * k:2 * C + C * (k + 1)], down_v[C:2 * C, :], 0)
                        for k in range(3)]),
                     ("down_b", [P, SKIP], [(lambda t: t[0:C, 0:2 * C], down_s[C:2 * C, :], 0)] + [
                        (lambda t, k=k: t[C * (k + 1):C * (k + 2), 2 * C + C * k:2 * C + C * (k + 1)], down_v[0:C, :], 0)
                        for k in range(3)]),
                     ("skip", [P, SPECIES, SKIP], [
                         (lambda t, q=q: t[0:C, q, 0:2 * C], a["L1_gnn_W_skip_s"][q], 0) for q in range(SPECIES)] + [
                         (lambda t, q=q, k=k: t[C * (k + 1):C * (k + 2), q, 2 * C + C * k:2 * C + C * (k + 1)],
                          a["L1_gnn_W_skip_v"][q], 0) for q in range(SPECIES) for k in range(3)]),
                     ("msg_gate", [P, 2 * P + 1], [
                         (lambda t: t[:, 0:P], a["L2_gnn_msg_w"][0:P, :], None),
                         (lambda t: t[:, P:2 * P], a["L2_gnn_msg_w"][P:2 * P, :], None),
                         (lambda t: t[:, 2 * P:], a["L2_gnn_gate_w"], None)]),
                     whole("msg_b", [P, P], a["L2_gnn_msg_b"].partition_broadcast(P)),
                     whole("upd_h", [P, P], a["L2_gnn_upd_w"][0:P, :]),
                     whole("upd_b", [P, P], a["L2_gnn_upd_b"].partition_broadcast(P)),
                     whole("gate_b", [P, 1], a["L2_gnn_gate_b"].partition_broadcast(P))]
            w = load_weights(st, specs)
            h, hT = sb(st, "h", [P, HR, P]), sb(st, "hT", [P, 3, P])
            mean = sb(st, "mean", [P, 4])
            bn = sb(st, "bn2", [P, 4, 6])
            both = sb(st, "both", [P, 4, SKIP])
            silu = sb(st, "silu", [P, 3, 2 * C])
            gated = sb(st, "gated", [P, 2, 3 * C])
            rowbuf = sb(st, "rowbuf", [P, 3, 2, P])
            gatec = sb(st, "gatec", [P, 2, 1])
            pT, p_sum = ps(st, "pT", [P, 2, 512]), ps(st, "p_sum", [P, 2, 512])
            p_skip = ps(st, "p_skip", [P, 2, 1024])
            pm = p_skip
            s = Stage(straight)
            agg_scale = 0.5 * (2 * C) ** -0.5 * DEG ** -0.5
            for n in ("down_a", "down_b"):
                s.do("vector", "scaled", lambda e, n=n: e.tensor_scalar(w[n][:, :], w[n][:, :], agg_scale, None, ALU.mult))
            s.do("vector", "scaled", lambda e: e.tensor_scalar(w["skip"][:, :, :], w["skip"][:, :, :], 0.5 * C ** -0.5, None, ALU.mult))
            for n, part in enumerate((w["msg_gate"][:, 0:P], w["msg_gate"][:, P:2 * P], w["msg_b"][:, :])):
                s.do("vector", ("m", n), lambda e, n=n, part=part: e.tensor_reduce(
                    mean[:, n:n + 1], part, AX, ALU.add))
                s.do("vector", ("m1", n), lambda e, n=n: e.tensor_scalar(
                    mean[:, n:n + 1], mean[:, n:n + 1], 1.0 / P, None, ALU.mult), ("m", n))
                s.do("vector", "scaled", lambda e, n=n, part=part: e.tensor_scalar(
                    part, part, mean[:, n:n + 1], None, ALU.subtract), ("m1", n))
            PER = 3

            def down(i):
                nodes = slice(i * P, (i + 1) * P)
                s.do("tensor", None, lambda e: e.matmul(
                    p_sum[:, i % 2, 0:SKIP], acc[:, 0, nodes], w["down_a"][:, :], start=True, stop=False),
                    "scaled", ring("both0", i, 2))
                s.do("tensor", ("down", i), lambda e: e.matmul(
                    p_sum[:, i % 2, 0:SKIP], acc[:, 1, nodes], w["down_b"][:, :], start=False, stop=True))

            def skip(i):
                s.wait("tensor", ("hT", i), ring("both", i, 2))
                for q0 in (0, PER):
                    q1 = min(q0 + PER, SPECIES)
                    s.do("tensor", ("hT_used", i), lambda e, q0=q0, q1=q1: e.matmul(
                        p_skip[:, i % 2, 512 * (q0 // PER):512 * (q0 // PER) + (q1 - q0) * SKIP],
                        hT[:, i % 3, :], w["skip"][:, q0:q1, :].rearrange("p q f -> p (q f)"), start=True, stop=True))

            def keep_sum(i):
                s.do("scalar", ("both0", i), lambda e: e.activation(
                    both[:, i % 4, :], p_sum[:, i % 2, 0:SKIP], ACT.Copy), ("down", i), ring("gated", i, 4))

            def add_skip(i):
                for q in range(SPECIES):
                    off = 512 * (q // PER) + (q % PER) * SKIP
                    s.do("vector", ("both", i) if q == SPECIES - 1 else ("skip", i, q),
                         lambda e, q=q, off=off: e.scalar_tensor_tensor(
                             out=both[:, i % 4, :], in0=p_skip[:, i % 2, off:off + SKIP],
                             scalar=species[:, i, q:q + 1], in1=both[:, i % 4, :], op0=ALU.mult, op1=ALU.add),
                         ("hT_used", i), ("both0", i) if q == 0 else ("skip", i, q - 1))

            def activate(i):
                s.do("scalar", ("silu", i), lambda e: e.activation(
                    silu[:, i % 3, :], both[:, i % 4, 0:2 * C], ACT.Silu), ("both", i), ring("x2", i, 3))

            def gating(i):
                s.do("gpsimd", ("gated", i), lambda e: e.tensor_tensor(
                    gated[:, i % 2, :].rearrange("p (k c) -> p k c", k=3),
                    both[:, i % 4, 2 * C:].rearrange("p (k c) -> p k c", k=3),
                    silu[:, i % 3, C:2 * C].unsqueeze(1).to_broadcast([P, 3, C]), ALU.mult),
                    ("silu", i), ring("x2", i, 2))
                s.do("gpsimd", ("x2s", i), lambda e: e.tensor_tensor(
                    x[:, i, 0:C], x[:, i, 0:C], silu[:, i % 3, 0:C], ALU.add), ("h", i))

            def add(i):
                s.do("vector", ("x2", i), lambda e: e.tensor_tensor(
                    vectors_last(x[:, i, C:P]), vectors_last(x[:, i, C:P]),
                    gated[:, i % 2, :].rearrange("p (k c) -> p k c", k=3), ALU.add), ("gated", i), ("x2s", i))

            staggered((4, activate), (0, lambda i: normed(s, h, i, by_component=True)), (0, down),
                      (1, lambda i: turn_h(s, h, pT, i)), (2, skip),
                      (1, keep_sum), (5, add), (6, lambda i: statistics(s, bn, i, x[:, i, :], ("x2", i))),
                      (1, lambda i: keep_hT(s, pT, hT, i)),
                      (3, add_skip), (4, gating),
                      (7, lambda i: aggregate(s, bn, i)), count=NT)
            s.wait("gpsimd", ("down", NT - 1))
            clear_accumulator(s, 1, "cleared")
            s.dma("sync", "tail", "load0", lambda e: e.dma_start(window_table[NT * P:ACC, :], zero[:, :]))
            s.straight(nc)

            s = Stage(straight)

            def widen(i):
                s.wait("tensor", ("hT", i), ring("row", i, 2), ring("term", i, 2))
                s.do("tensor", None, lambda e: e.matmul(
                    pm[:, i % 2, 0:2 * P + 1], hT[:, i % 3, :], w["msg_gate"][:, :], start=True, stop=True))
                s.do("tensor", ("hT_used", i), lambda e: e.matmul(
                    pm[:, i % 2, 512:512 + P], hT[:, i % 3, :], w["upd_h"][:, :], start=True, stop=True))

            def send(i):
                s.do("scalar", ("row_src", i), lambda e: e.activation(
                    rowbuf[:, i % 3, 0, :], pm[:, i % 2, 0:P], ACT.Copy), ("hT_used", i), ring("src_out", i, 3))
                s.do("scalar", ("gate", i), lambda e: e.activation(
                    gate[:, i:i + 1], pm[:, i % 2, 2 * P:2 * P + 1], ACT.Sigmoid, bias=w["gate_b"][:, 0:1]))
                s.do("vector", ("row", i), lambda e: e.tensor_tensor(
                    rowbuf[:, i % 3, 1, :], pm[:, i % 2, P:2 * P], w["msg_b"][:, :], ALU.add), ("gate", i),
                    ring("dst_out", i, 3))
                s.do("vector", ("term", i), lambda e: e.tensor_tensor(
                    local_term[:, i, :], pm[:, i % 2, 512:512 + P], w["upd_b"][:, :], ALU.add))
                store(s, ("src_out", i), lambda e: e.dma_start(
                    table[i * P:i * P + rows(i), :], rowbuf[0:rows(i), i % 3, 0, :]), ("row_src", i))
                store(s, ("dst_out", i), lambda e: e.dma_start(
                    window_table[i * P:(i + 1) * P, :], rowbuf[:, i % 3, 1, :]), ("row", i))

            def mix(i):
                s.do("vector", ("gate1", i), lambda e: e.tensor_scalar(
                    gatec[:, i % 2, :], gate[:, i:i + 1], -1.0, 1.0, ALU.mult, ALU.add), ("gate", i))

            def mixed(i):
                s.do("vector", ("h_mixed", i), lambda e: e.scalar_tensor_tensor(
                    out=x[:, i, :], in0=h[:, i % HR, :], scalar=gatec[:, i % 2, 0:1], in1=x[:, i, :],
                    op0=ALU.mult, op1=ALU.add), ("gate1", i))

            staggered((4, mixed), (0, lambda i: normed(s, h, i, user="h_mixed")), (1, lambda i: turn_h(s, h, pT, i)),
                      (1, lambda i: keep_hT(s, pT, hT, i)), (2, widen), (3, send), (3, mix), count=NT)
            s.wait("sync", *[(n, i) for i in range(max(0, NT - STORES), NT) for n in ("src_out", "dst_out")])
            s.wait("vector", ("h_mixed", NT - 1))
            s.straight(nc)

        with ExitStack() as st:
            w = load_weights(st, [whole("msg_g", [P, P], a["L2_gnn_msg_g"].partition_broadcast(P)),
                                  whole("msg_beta", [P, P], a["L2_gnn_msg_beta"].partition_broadcast(P))])
            local = sb(st, "local_2", [P, TURN_BATCHES, BATCH_TILES])
            weight = sb(st, "weight_2", [P, TURN_BATCHES, BATCH_TILES])
            sel = sb(st, "sel_2", [P, 4, GROUP, WINDOW])
            near_rows = sb(st, "near_rows", [WINDOW, 4, P])
            near_dst = sb(st, "near_dst", [WINDOW, 4, GROUP_EDGES])
            spread = sb(st, "spread", [WINDOW, 2, GROUP_EDGES])
            sq = sb(st, "sq", [P, 4, GROUP])
            eps = sb(st, "eps", [P, 1])
            y = sb(st, "y", [P, 4, GROUP, P])
            p_near = ps(st, "p_near", [P, 2, GROUP, P])
            sums = ps(st, "sums_2", [P, 4, 512])
            s = Stage(straight)
            s.do("vector", "eps", lambda e: e.memset(eps[:, :], EPS))
            s.wait("vector", "eps")
            s.straight(nc)

            def near(s, g):
                b, at = place(g)

                def load(e, it):
                    at = e.value_load(address[0:1, bass.ds(it * TURN_GROUPS + g, 1)], min_val=0, max_val=N)
                    return e.dma_start(near_rows[:, g % 4, :], window_table[bass.ds(at, WINDOW), :])
                s.wait("sync", ring("spread_out", g, 4, TURN_GROUPS))
                s.dma("sync", ("near", g), f"near{g % 4}", load)
                s.dma("sync", ("near", g), f"near{g % 4}", lambda e, it: e.dma_start(
                    near_dst[:, g % 4, :], local_rows[bass.ds(it * TURN_BATCHES + b, 1), at * P:at * P + GROUP_EDGES]
                    .to_broadcast([WINDOW, GROUP_EDGES])))

            def body(s, gathered):
                def spread_near(g):
                    s.do("vector", ("spread", g), lambda e, it: e.tensor_scalar(
                        spread[:, g % 2, :], near_dst[:, g % 4, :], iota_col_pass[0:WINDOW, :], None, ALU.is_equal),
                        ("near", g), ring("spread_out", g, 2, TURN_GROUPS))
                    s.wait("tensor", ("spread", g), ring("z", g, 2, TURN_GROUPS))
                    for t in range(GROUP):
                        s.do("tensor", ("spread_out", g), lambda e, it, t=t: e.matmul(
                            p_near[:, g % 2, t, :], spread[:, g % 2, t * P:(t + 1) * P], near_rows[:, g % 4, :],
                            start=True, stop=True))

                def combine(g):
                    s.do("vector", ("z", g), lambda e, it: e.tensor_tensor(
                        gathered[:, g % SLOTS, :, :], gathered[:, g % SLOTS, :, :], p_near[:, g % 2, :, :], ALU.add),
                        ("spread_out", g), ("gathered", g))
                    s.wait("scalar", ("z", g), ring("summed", g, 4, TURN_GROUPS))
                    for t in range(GROUP):
                        s.do("scalar", ("sq", g), lambda e, it, t=t: e.activation(
                            y[:, g % 4, t, :], gathered[:, g % SLOTS, t, :], ACT.Square, accum_out=sq[:, g % 4, t:t + 1]))
                    s.do("scalar", ("std", g), lambda e, it: e.activation(
                        sq[:, g % 4, :], sq[:, g % 4, :], ACT.Sqrt, scale=1.0 / P, bias=eps[:, 0:1]), ("sq", g))

                def invert(g):
                    s.do("vector", ("rstd", g), lambda e, it: e.reciprocal(
                        sq[:, g % 4, :], sq[:, g % 4, :]), ("std", g))

                def scale(g):
                    s.wait("vector", ("rstd", g))
                    for t in range(GROUP):
                        s.do("vector", ("scaled", g), lambda e, it, t=t: e.scalar_tensor_tensor(
                            out=y[:, g % 4, t, :], in0=gathered[:, g % SLOTS, t, :], scalar=sq[:, g % 4, t:t + 1],
                            in1=w["msg_g"][:, :], op0=ALU.mult, op1=ALU.mult))
                    s.steps[("rows_used", g)] = s.steps[("scaled", g)]

                def bias_relu(g):
                    s.do("vector", ("shifted", g), lambda e, it: e.tensor_tensor(
                        y[:, g % 4, :, :], y[:, g % 4, :, :],
                        w["msg_beta"][:, :].unsqueeze(1).to_broadcast([P, GROUP, P]), ALU.add), ("scaled", g))
                    s.do("scalar", ("relu", g), lambda e, it: e.activation(
                        y[:, g % 4, :, :], y[:, g % 4, :, :], ACT.Relu), ("shifted", g))

                def multiply(g):
                    s.wait("tensor", ("relu", g), ("weighed", g), ring("added", g, 4, TURN_GROUPS))
                    for t in range(GROUP):
                        s.do("tensor", ("summed", g), lambda e, it, t=t: e.matmul(
                            sums[:, g % 4, 0:WINDOW], y[:, g % 4, t, :], sel[:, g % 4, t, :],
                            start=t == 0, stop=t == GROUP - 1))
                    s.steps[("edges_used", g)] = s.steps[("summed", g)]

                staggered((3, invert), (0, spread_near), (1, lambda g: select(s, sel, local, g)),
                          (1, lambda g: weigh(s, sel, weight, g)), (3, scale),
                          (5, lambda g: accumulate(s, sums[:, g % 4, 0:WINDOW].unsqueeze(1), g)),
                          (3, bias_relu), (4, multiply), (1, combine))

            message_stage("messages2", body, table, a["src_cols"], [
                (local, column(local_cols)), (weight, column(a["weight_cols"]))], st, near=near)

        with ExitStack() as st:
            w = load_weights(st, [
                whole("upd_m", [P, P], a["L2_gnn_upd_w"][P:2 * P, :]),
                whole("upd_g", [P, P], a["L2_gnn_upd_g"].partition_broadcast(P)),
                whole("upd_beta", [P, P], a["L2_gnn_upd_beta"].partition_broadcast(P)),
                whole("rel", [P, REL, P], a["L3_gnn_w_rel"][0].rearrange("r d e -> d r e")),
                whole("root", [P, P], a["L3_gnn_w_root"][0]),
                whole("skip0", [P, P], a["L3_gnn_w_skip"][0]),
                whole("skip1", [P, P], a["L3_gnn_w_skip"][1]),
                whole("b_col", [P, 2], a["L3_b_cols"]),
                whole("b_conv1", [P, P], a["L3_gnn_b_conv"][1, :].partition_broadcast(P)),
                whole("b_skip1", [P, P], a["L3_gnn_b_skip"][1, :].partition_broadcast(P))])
            h, hT = sb(st, "h", [P, HR, P]), sb(st, "hT", [P, 3, P])
            bn_z, bn = sb(st, "bn_z", [P, 4, 6]), sb(st, "bn3", [P, 4, 6])
            u = sb(st, "u", [P, 6, P])
            rowbuf = sb(st, "rowbuf", [P, 3, REL, P])
            pT, pm = ps(st, "pT", [P, 2, 512]), ps(st, "pm", [P, 2, 512])
            pl, px = ps(st, "pl", [P, 2, 512]), ps(st, "px", [P, 1, 512])
            pu = ps(st, "pu", [P, 1, 512])
            s = Stage(straight)
            s.do("vector", "root_sum", lambda e: e.tensor_tensor(w["root"][:, :], w["root"][:, :], w["skip0"][:, :], ALU.add))
            s.do("vector", "b_sum", lambda e: e.tensor_tensor(w["b_col"][:, 0:1], w["b_col"][:, 0:1], w["b_col"][:, 1:2], ALU.add))
            s.do("vector", "b_row", lambda e: e.tensor_tensor(w["b_conv1"][:, :], w["b_conv1"][:, :], w["b_skip1"][:, :], ALU.add))
            s.do("gpsimd", "acc_tail", lambda e: e.memset(acc[:, 0, NT * P:ACC], 0.0))

            def update(i):
                nodes = slice(i * P, (i + 1) * P)
                s.do("tensor", ("upd", i), lambda e: e.matmul(
                    pu[:, 0, 0:P], acc[:, 0, nodes], w["upd_m"][:, :], start=True, stop=True), ring("z", i, 1))

            def updated(i):
                s.do("vector", ("z", i), lambda e: e.scalar_tensor_tensor(
                    out=local_term[:, i, :], in0=pu[:, 0, 0:P], scalar=rcount[:, i:i + 1],
                    in1=local_term[:, i, :], op0=ALU.mult, op1=ALU.add), ("upd", i))

            def normal(i):
                s.do("scalar", ("u", i), lambda e: e.activation(
                    u[:, i % 6, :], local_term[:, i, :], ACT.Identity, bias=shift[:, i:i + 1],
                    scale=rstd[:, i:i + 1]), ("z", "norm", i), ring("x3", i, 6))

            def affine(i):
                s.do("gpsimd", ("ug", i), lambda e: e.tensor_tensor(
                    u[:, i % 6, :], u[:, i % 6, :], w["upd_g"][:, :], ALU.mult), ("u", i))
                s.do("gpsimd", ("ub", i), lambda e: e.tensor_tensor(
                    u[:, i % 6, :], u[:, i % 6, :], w["upd_beta"][:, :], ALU.add), ("ug", i))

            def gating(i):
                s.do("vector", ("ur", i), lambda e: e.tensor_scalar(
                    u[:, i % 6, :], u[:, i % 6, :], 0.0, gate[:, i:i + 1], ALU.max, ALU.mult), ("ub", i))

            def add(i):
                s.do("vector", ("x3", i), lambda e: e.tensor_tensor(
                    x[:, i, :], x[:, i, :], u[:, i % 6, :], ALU.add), ("ur", i))

            def multiply_relations(i, lhs, after):
                s.wait("tensor", after, ring("rel_row", i, 2))
                for r in range(REL):
                    s.do("tensor", ("rel", i), lambda e, r=r: e.matmul(
                        pm[:, i % 2, r * P:(r + 1) * P], lhs, w["rel"][:, r, :], start=True, stop=True))

            def send_relations(i):
                s.do("scalar", ("rel_row", i), lambda e: e.activation(
                    rowbuf[:, i % 3, :, :].rearrange("p r f -> p (r f)"), pm[:, i % 2, 0:REL * P], ACT.Copy),
                    ("rel", i), ring("rel_out", i, 3))
                store(s, ("rel_out", i), lambda e: e.dma_start(
                    rel_table.rearrange("(r n) f -> n r f", r=REL)[i * P:i * P + rows(i), :, :],
                    rowbuf[0:rows(i), i % 3, :, :]), ("rel_row", i))

            def convolve(i):
                multiply_relations(i, hT[:, i % 3, :], ("hT", i))
                s.do("tensor", ("local", i), lambda e: e.matmul(
                    pl[:, i % 2, 0:P], w["root"][:, :], hT[:, i % 3, :], start=True, stop=True),
                    "root_sum", ring("acc", i, 2))
                s.do("tensor", ("hT_used", i), lambda e: e.matmul(
                    px[:, 0, 0:P], hT[:, i % 3, :], w["skip1"][:, :], start=True, stop=True), ring("x4", i, 1))

            def add_bias(i):
                s.do("gpsimd", ("biased", i), lambda e: e.tensor_tensor(
                    x[:, i, :], x[:, i, :], w["b_conv1"][:, :], ALU.add), ("h", i), "b_row")

            def keep_local(i):
                nodes = slice(i * P, (i + 1) * P)
                s.do("scalar", ("acc", i), lambda e: e.activation(
                    acc[:, 0, nodes], pl[:, i % 2, 0:P], ACT.Identity, bias=w["b_col"][:, 0:1]), ("local", i), "b_sum")

            def add_skip(i):
                s.do("vector", ("x4", i), lambda e: e.tensor_tensor(
                    x[:, i, :], x[:, i, :], px[:, 0, 0:P], ALU.add), ("hT_used", i), ("biased", i))

            A, B = SMALL_CHUNK + 4, 2 * SMALL_CHUNK + 12
            staggered((B + 3, add_skip), (0, update), (0, updated), (B + 1, add_bias), (1, lambda i: statistics(s, bn_z, i, local_term[:, i, :], ("z", i), "z")),
                      (A, normal), (A + 1, affine), (A + 2, gating), (A + 3, add),
                      (B, lambda i: normed(s, h, i)), (B + 1, lambda i: turn_h(s, h, pT, i)),
                      (B + 2, convolve), (B + 3, keep_local),
                      (2, lambda i: aggregate(s, bn_z, i, "z", SMALL_CHUNK)),
                      (A + 4, lambda i: statistics(s, bn, i, x[:, i, :], ("x3", i))),
                      (B + 3, send_relations),
                      (B + 1, lambda i: keep_hT(s, pT, hT, i)),
                      (A + 5, lambda i: aggregate(s, bn, i, chunk=SMALL_CHUNK)), count=NT)
            s.wait("sync", *[("rel_out", i) for i in range(max(0, NT - STORES), NT)])
            s.wait("gpsimd", "acc_tail")
            s.straight(nc)

        with ExitStack() as st:
            w = load_weights(st, [
                whole("rel", [P, REL, P], a["L3_gnn_w_rel"][1].rearrange("r d e -> d r e")),
                whole("root1", [P, P], a["L3_gnn_w_root"][1])])
            plain_messages("conv0", rel_table, rel_cols, a["weight_cols"])

            rowbuf = sb(st, "rowbuf", [P, 3, REL, P])
            pm, px = ps(st, "pm", [P, 2, 512]), ps(st, "px", [P, 2, 512])
            s = Stage(straight)
            for i in range(NT):
                nodes = slice(i * P, (i + 1) * P)
                multiply_relations(i, acc[:, 0, nodes], None)
                s.do("tensor", ("root", i), lambda e, i=i, nodes=nodes: e.matmul(
                    px[:, i % 2, 0:P], acc[:, 0, nodes], w["root1"][:, :], start=True, stop=True), ring("x5", i, 2))
                send_relations(i)
                s.do("vector", ("x5", i), lambda e, i=i: e.tensor_tensor(
                    x[:, i, :], x[:, i, :], px[:, i % 2, 0:P], ALU.add), ("root", i))
                s.wait("gpsimd", ("root", i))
                s.do("gpsimd", "cleared", lambda e, nodes=nodes: e.memset(acc[:, 0, nodes], 0.0))
            s.do("gpsimd", "cleared", lambda e: e.memset(acc[:, 0, NT * P:ACC], 0.0))
            s.wait("sync", *[("rel_out", i) for i in range(max(0, NT - STORES), NT)])
            s.wait("gpsimd", "cleared")
            s.straight(nc)

        plain_messages("conv1", rel_table, rel_cols, a["weight_cols"])

        with ExitStack() as st:
            pm = ps(st, "pm", [P, 4, 512])
            s = Stage(straight)
            for i in range(NT):
                s.do("tensor", ("agg", i), lambda e, i=i: e.transpose(
                    pm[:, i % 4, 0:P], acc[:, 0, i * P:(i + 1) * P], ident[:, :]), ring("x6", i, 4))
                s.do("vector", ("x6", i), lambda e, i=i: e.tensor_tensor(
                    x[:, i, :], x[:, i, :], pm[:, i % 4, 0:P], ALU.add), ("agg", i))
                store(s, ("out", i), lambda e, i=i: e.dma_start(
                    out[i * P:i * P + rows(i), :], x[0:rows(i), i, :]), ("x6", i))
            s.wait("sync", *[("out", i) for i in range(NT)])
            s.straight(nc)


def kernel(**inputs):
    import concourse.bacc as bacc
    from concourse.bass_utils import run_bass_kernel_spmd

    v = {k: np.asarray(q) for k, q in inputs.items()}
    N, E = v["x"].shape[0], v["src"].shape[0]
    turns = -(-E // TURN_EDGES)
    pad = turns * TURN_EDGES - E
    nt = -(-N // P)

    def edges(q, fill=0):
        return np.concatenate([q, np.full((pad,) + q.shape[1:], fill, q.dtype)])

    def cols(q):
        return np.ascontiguousarray(q.reshape((-1, P) + q.shape[1:]).swapaxes(0, 1).reshape(P, -1))

    arrays = {
        "x": v["x"],
        "src_cols": cols(edges(v["src"])),
        "dst_cols": cols(edges(v["dst"], -1)),
        "dst_rows": edges(v["dst"], -1).reshape(-1, BATCH_EDGES),
        "type_cols": cols(edges(v["edge_type_3"])),
        "weight_cols": cols(edges(v["edge_weight"])),
        "sh_cols": cols(edges(v["edge_attr_4"])),
        "radial_cols": np.ascontiguousarray(
            edges(v["edge_attr_8"]).reshape(-1, BATCH_GROUPS, GROUP, P, R)
            .transpose(1, 2, 4, 0, 3).reshape(P, -1)),
        "node_type": np.ascontiguousarray(np.concatenate(
            [v["node_type_5"], np.zeros(nt * P - N, v["node_type_5"].dtype)]).reshape(nt, P).T),
        "L0_rel_t": np.ascontiguousarray(v["L0_gnn_W_rel"].T),
        "L0_root_t": np.ascontiguousarray(v["L0_gnn_W_root"].T),
        "L3_b_cols": np.ascontiguousarray(np.stack([v["L3_gnn_b_conv"][0], v["L3_gnn_b_skip"][0]], 1)),
    }
    for n in ("L0_gnn_b_rel", "L2_gnn_msg_b", "L2_gnn_upd_b", "L2_gnn_gate_b"):
        arrays[n] = v[n].reshape(1, -1)
    for n in ("L1_gnn_W_up_s", "L1_gnn_W_up_v", "L1_gnn_W_r1", "L1_gnn_W_r2", "L1_gnn_W_down_s",
              "L1_gnn_W_down_v", "L1_gnn_W_skip_s", "L1_gnn_W_skip_v", "L2_gnn_msg_w", "L2_gnn_msg_g",
              "L2_gnn_msg_beta", "L2_gnn_upd_w", "L2_gnn_upd_g", "L2_gnn_upd_beta", "L2_gnn_gate_w",
              "L3_gnn_w_rel", "L3_gnn_w_root", "L3_gnn_w_skip", "L3_gnn_b_conv", "L3_gnn_b_skip"):
        arrays[n] = v[n]

    nc = bacc.Bacc("TRN2", target_bir_lowering=False, num_devices=1)
    aps, feed = {}, {}
    for n, q in arrays.items():
        feed["in_" + n] = q
        aps[n] = nc.dram_tensor("in_" + n, q.shape, mybir.dt.from_np(q.dtype), kind="ExternalInput").ap()
    result = nc.dram_tensor("out", (N, P), F32, kind="ExternalOutput").ap()
    build(nc, aps, result, (N, E))
    r = run_bass_kernel_spmd(nc, [feed], core_ids=[0])
    return r.results[0]["out"]
```
